# Optimizing a Trainium2 kernel written in Bass

```python
import numpy as np
import jax
import jax.numpy as jnp

def _softmax(x, axis=-1):
    return jax.nn.softmax(x, axis=axis)

def _gelu(x):
    return jax.nn.gelu(x, approximate=True)

def _silu(x):
    return jax.nn.silu(x)

def _sigmoid(x):
    return jax.nn.sigmoid(x)

def _layernorm(x, axis=-1, eps=1e-05):
    m = jnp.mean(x, axis=axis, keepdims=True)
    v = jnp.var(x, axis=axis, keepdims=True)
    return (x - m) / jnp.sqrt(v + eps)

def _scatter_add(tgt, idx, src, axis=0):
    return tgt.at[idx].add(src)

def _segment_sum(src, seg, n):
    return jax.ops.segment_sum(src, seg, n)
kernel_name = 'mk_adj_ffn_d2_adj_r2_7f5fae'

def setup_inputs(seed: int=0):
    np.random.seed(seed)
    _w = jnp.asarray

    def _rec_inputs():
        import jax
        import jax.numpy as jnp
        _gk = jax.random.key(seed)
        x = -0.0005207 + 1.001 * jax.random.normal(jax.random.fold_in(_gk, 1), (4096, 128), jnp.float32)
        _w = (1.0 + jnp.arange(4096, dtype=jnp.float32)) ** (-0.5)
        _w = _w / _w.mean()
        _pij = jnp.clip(0.00195312 * _w[:, None] * _w[None, :], 0.0, 1.0)
        _a = jax.random.uniform(jax.random.fold_in(_gk, 2), (4096, 4096)) < _pij
        _a = jnp.logical_or(_a, jnp.swapaxes(_a, -1, -2))
        _a = jnp.logical_or(_a, jnp.eye(4096, dtype=bool))
        _af = _a.astype(jnp.float32)
        _af = _af * jax.random.uniform(jax.random.fold_in(_gk, 3), (4096, 4096), jnp.float32, 0.05, 2.05)
        adj = _af
        return (x, adj)
    x, adj = _rec_inputs()

    def _L0_gnn_setup():
        import jax, jax.numpy as jnp
        import numpy as np
        N = 4096
        D = 128
        CUTOFF = 1.0
        MU = 1.0
        SIGMA = 0.5

        def sensitivity(r, mu, sigma):
            return jnp.exp(-(1.0 / r - 1.0 / mu) ** 2 / (2.0 * sigma * sigma))
        key = jax.random.key(seed)
        k_z, k_d, k_w = jax.random.split(key, 3)
        z = jax.random.normal(k_z, (N, D), dtype=jnp.float32)
        dist_matrix = jax.random.uniform(k_d, (N, N), dtype=jnp.float32) * 2.0 + 0.05
        W = jax.random.normal(k_w, (D, D), dtype=jnp.float32)
        B = jnp.zeros((D,), dtype=jnp.float32)
        return {'z': z, 'dist_matrix': dist_matrix, 'W': W, 'B': B}
    _L0_gnn_all = _L0_gnn_setup()
    _L0_gnn_in = {k: v for k, v in _L0_gnn_all.items() if k in ('W', 'B')}
    del _L0_gnn_all

    def _L0_ffn_setup():
        import jax, jax.numpy as jnp
        import numpy as np
        B, T, D, H, L = (16, 2048, 128, 128, 2)

        def _lstm(x, W_ih, W_hh, b_ih, b_hh):
            x_proj = jnp.einsum('btd,gd->btg', x, W_ih) + b_ih + b_hh
            h0 = jnp.zeros((x.shape[0], W_hh.shape[1]), x.dtype)
            c0 = jnp.zeros_like(h0)

            def step(carry, xp):
                h, c = carry
                gates = xp + h @ W_hh.T
                i, f, g, o = jnp.split(gates, 4, axis=-1)
                c = jax.nn.sigmoid(f) * c + jax.nn.sigmoid(i) * jnp.tanh(g)
                h = jax.nn.sigmoid(o) * jnp.tanh(c)
                return ((h, c), h)
            _, hs = jax.lax.scan(step, (h0, c0), jnp.swapaxes(x_proj, 0, 1))
            return jnp.swapaxes(hs, 0, 1)
        key = jax.random.key(seed)
        ks = jax.random.split(key, 9)
        s = 1.0 / np.sqrt(H)
        u = lambda k, shape: jax.random.uniform(k, shape, jnp.float32, -s, s)
        return {'x': jax.random.normal(ks[0], (B, T, D), jnp.float32), 'W_ih': u(ks[1], (4 * H, D)), 'W_hh': u(ks[2], (4 * H, H)), 'b_ih': u(ks[3], (4 * H,)), 'b_hh': u(ks[4], (4 * H,)), 'W_lin': u(ks[5], (L, H)), 'b_lin': u(ks[6], (L,)), 'fw_att': jnp.full((1, H), 0.001, jnp.float32), 'bw_att': jnp.full((1, H), 0.001, jnp.float32)}
    _L0_ffn_all = _L0_ffn_setup()
    _L0_ffn_in = {k: v for k, v in _L0_ffn_all.items() if k in ('W_ih', 'W_hh', 'b_ih', 'b_hh', 'W_lin', 'b_lin', 'fw_att', 'bw_att')}
    del _L0_ffn_all

    def _L1_gnn_setup():
        import jax, jax.numpy as jnp
        import numpy as np
        N, F, OUT = (4096, 128, 128)
        key = jax.random.key(seed)
        k1, k2, k3, k4 = jax.random.split(key, 4)
        features = jax.random.normal(k1, (N, F), dtype=jnp.float32)
        adj = jax.random.uniform(k2, (N, N), dtype=jnp.float32)
        gain = float(np.sqrt(2.0))
        b_n = gain * np.sqrt(6.0 / (F + F))
        neigh_W = jax.random.uniform(k3, (F, F), dtype=jnp.float32, minval=-b_n, maxval=b_n)
        b_l = gain * np.sqrt(6.0 / (2 * F + OUT))
        lin_W = jax.random.uniform(k4, (OUT, 2 * F), dtype=jnp.float32, minval=-b_l, maxval=b_l)
        return {'features': features, 'adj': adj, 'neigh_W': neigh_W, 'lin_W': lin_W}
    _L1_gnn_all = _L1_gnn_setup()
    _L1_gnn_in = {k: v for k, v in _L1_gnn_all.items() if k in ('neigh_W', 'lin_W')}
    del _L1_gnn_all

    def _L1_ffn_setup():
        import jax, jax.numpy as jnp
        import numpy as np
        B, T, C = (64, 192, 128)
        NH, NKV = (4, 2)
        HD = C // NH
        NREP = NH // NKV
        NE, TOPK = (8, 2)
        HID = int(8 / 3 * C)
        EPS_RMS = 1e-06

        def _rope_tables(t_len):
            inv_freq = 1.0 / 10000.0 ** (np.arange(0, HD, 2, dtype=np.float32) / HD)
            t = np.arange(t_len, dtype=np.float32)
            freqs = np.outer(t, inv_freq)
            emb = np.concatenate([freqs, freqs], axis=-1)
            return (jnp.asarray(np.cos(emb)), jnp.asarray(np.sin(emb)))

        def _rotate_half(x):
            h = x.shape[-1] // 2
            return jnp.concatenate([-x[..., h:], x[..., :h]], axis=-1)

        def _rmsnorm(v, w):
            return v * jax.lax.rsqrt(jnp.mean(v * v, axis=-1, keepdims=True) + EPS_RMS) * w
        key = jax.random.key(seed)
        ks = jax.random.split(key, 10)
        s = lambda k, shape: jax.random.normal(k, shape, jnp.float32) * 0.02
        return {'x': jax.random.normal(ks[0], (B, T, C), jnp.float32), 'ln1_w': jnp.ones((C,), jnp.float32), 'ln2_w': jnp.ones((C,), jnp.float32), 'wq': s(ks[1], (NH * HD, C)), 'wk': s(ks[2], (NKV * HD, C)), 'wv': s(ks[3], (NKV * HD, C)), 'wo': s(ks[4], (C, C)), 'router_w': s(ks[5], (NE, C)), 'w1': s(ks[6], (NE, HID, C)), 'w2': s(ks[7], (NE, C, HID)), 'w3': s(ks[8], (NE, HID, C))}
    _L1_ffn_all = _L1_ffn_setup()
    _L1_ffn_in = {k: v for k, v in _L1_ffn_all.items() if k in ('ln1_w', 'ln2_w', 'wq', 'wk', 'wv', 'wo', 'router_w', 'w1', 'w2', 'w3')}
    del _L1_ffn_all
    return {'x': x, 'adj': adj, 'L0_gnn_W': _L0_gnn_in['W'], 'L0_gnn_B': _L0_gnn_in['B'], 'L0_ffn_W_ih': _L0_ffn_in['W_ih'], 'L0_ffn_W_hh': _L0_ffn_in['W_hh'], 'L0_ffn_b_ih': _L0_ffn_in['b_ih'], 'L0_ffn_b_hh': _L0_ffn_in['b_hh'], 'L0_ffn_W_lin': _L0_ffn_in['W_lin'], 'L0_ffn_b_lin': _L0_ffn_in['b_lin'], 'L0_ffn_fw_att': _L0_ffn_in['fw_att'], 'L0_ffn_bw_att': _L0_ffn_in['bw_att'], 'L1_gnn_neigh_W': _L1_gnn_in['neigh_W'], 'L1_gnn_lin_W': _L1_gnn_in['lin_W'], 'L1_ffn_ln1_w': _L1_ffn_in['ln1_w'], 'L1_ffn_ln2_w': _L1_ffn_in['ln2_w'], 'L1_ffn_wq': _L1_ffn_in['wq'], 'L1_ffn_wk': _L1_ffn_in['wk'], 'L1_ffn_wv': _L1_ffn_in['wv'], 'L1_ffn_wo': _L1_ffn_in['wo'], 'L1_ffn_router_w': _L1_ffn_in['router_w'], 'L1_ffn_w1': _L1_ffn_in['w1'], 'L1_ffn_w2': _L1_ffn_in['w2'], 'L1_ffn_w3': _L1_ffn_in['w3']}

def reference(x, adj, L0_gnn_W, L0_gnn_B, L0_ffn_W_ih, L0_ffn_W_hh, L0_ffn_b_ih, L0_ffn_b_hh, L0_ffn_W_lin, L0_ffn_b_lin, L0_ffn_fw_att, L0_ffn_bw_att, L1_gnn_neigh_W, L1_gnn_lin_W, L1_ffn_ln1_w, L1_ffn_ln2_w, L1_ffn_wq, L1_ffn_wk, L1_ffn_wv, L1_ffn_wo, L1_ffn_router_w, L1_ffn_w1, L1_ffn_w2, L1_ffn_w3):
    import jax
    import jax.numpy as jnp

    def _L0_gnn_ref(z, dist_matrix, W, B):
        import jax, jax.numpy as jnp
        import numpy as np
        N = 4096
        D = 128
        CUTOFF = 1.0
        MU = 1.0
        SIGMA = 0.5

        def sensitivity(r, mu, sigma):
            return jnp.exp(-(1.0 / r - 1.0 / mu) ** 2 / (2.0 * sigma * sigma))
        msg = z @ W + B
        sens = sensitivity(dist_matrix, MU, SIGMA)
        weights = jnp.where(dist_matrix < CUTOFF, sens, 0.0)
        return weights @ msg

    def _L0_ffn_ref(x, W_ih, W_hh, b_ih, b_hh, W_lin, b_lin, fw_att, bw_att):
        import jax, jax.numpy as jnp
        import numpy as np
        B, T, D, H, L = (16, 2048, 128, 128, 2)

        def _lstm(x, W_ih, W_hh, b_ih, b_hh):
            x_proj = jnp.einsum('btd,gd->btg', x, W_ih) + b_ih + b_hh
            h0 = jnp.zeros((x.shape[0], W_hh.shape[1]), x.dtype)
            c0 = jnp.zeros_like(h0)

            def step(carry, xp):
                h, c = carry
                gates = xp + h @ W_hh.T
                i, f, g, o = jnp.split(gates, 4, axis=-1)
                c = jax.nn.sigmoid(f) * c + jax.nn.sigmoid(i) * jnp.tanh(g)
                h = jax.nn.sigmoid(o) * jnp.tanh(c)
                return ((h, c), h)
            _, hs = jax.lax.scan(step, (h0, c0), jnp.swapaxes(x_proj, 0, 1))
            return jnp.swapaxes(hs, 0, 1)
        lstm_out = _lstm(x, W_ih, W_hh, b_ih, b_hh)
        logits = jnp.einsum('bth,lh->btl', lstm_out, W_lin) + b_lin
        g = jax.lax.stop_gradient(jnp.argmax(logits, axis=-1).astype(lstm_out.dtype))[..., None]
        w = g * lstm_out
        inc = jnp.cumsum(w, axis=1)
        prefix = inc - w
        suffix = inc[:, -1:, :] - inc
        return 2.0 * lstm_out + prefix * fw_att + suffix * bw_att

    def _L1_gnn_ref(features, adj, neigh_W, lin_W):
        import jax, jax.numpy as jnp
        import numpy as np
        N, F, OUT = (4096, 128, 128)
        h = features @ neigh_W.T
        deg = adj.sum(axis=1, keepdims=True) + 1.0
        h = adj @ h / deg
        z = jnp.concatenate([features, h], axis=-1) @ lin_W.T
        return z

    def _L1_ffn_ref(x, ln1_w, ln2_w, wq, wk, wv, wo, router_w, w1, w2, w3):
        import jax, jax.numpy as jnp
        import numpy as np
        B, T, C = (64, 192, 128)
        NH, NKV = (4, 2)
        HD = C // NH
        NREP = NH // NKV
        NE, TOPK = (8, 2)
        HID = int(8 / 3 * C)
        EPS_RMS = 1e-06

        def _rope_tables(t_len):
            inv_freq = 1.0 / 10000.0 ** (np.arange(0, HD, 2, dtype=np.float32) / HD)
            t = np.arange(t_len, dtype=np.float32)
            freqs = np.outer(t, inv_freq)
            emb = np.concatenate([freqs, freqs], axis=-1)
            return (jnp.asarray(np.cos(emb)), jnp.asarray(np.sin(emb)))

        def _rotate_half(x):
            h = x.shape[-1] // 2
            return jnp.concatenate([-x[..., h:], x[..., :h]], axis=-1)

        def _rmsnorm(v, w):
            return v * jax.lax.rsqrt(jnp.mean(v * v, axis=-1, keepdims=True) + EPS_RMS) * w
        Bx, Tx, Cx = x.shape
        h = _rmsnorm(x, ln1_w)
        q = (h @ wq.T).reshape(Bx, Tx, NH, HD).transpose(0, 2, 1, 3)
        k = (h @ wk.T).reshape(Bx, Tx, NKV, HD).transpose(0, 2, 1, 3)
        v = (h @ wv.T).reshape(Bx, Tx, NKV, HD).transpose(0, 2, 1, 3)
        cos, sin = _rope_tables(Tx)
        cos, sin = (cos[None, None], sin[None, None])
        q = q * cos + _rotate_half(q) * sin
        k = k * cos + _rotate_half(k) * sin
        k = jnp.repeat(k, NREP, axis=1)
        v = jnp.repeat(v, NREP, axis=1)
        scores = jnp.einsum('bhtd,bhsd->bhts', q, k) / jnp.sqrt(jnp.float32(HD))
        causal = jnp.tril(jnp.ones((Tx, Tx), dtype=bool))
        scores = jnp.where(causal[None, None], scores, jnp.float32(-1e+30))
        att = jax.nn.softmax(scores, axis=-1)
        y = jnp.einsum('bhts,bhsd->bhtd', att, v).transpose(0, 2, 1, 3).reshape(Bx, Tx, Cx)
        x = x + y @ wo.T
        flat = _rmsnorm(x, ln2_w).reshape(-1, Cx)
        probs = jax.nn.softmax(flat @ router_w.T, axis=-1)
        tp, ti = jax.lax.top_k(probs, TOPK)
        tp = tp / (jnp.sum(tp, axis=-1, keepdims=True) + 1e-09)
        weights = jnp.sum(tp[..., None] * jax.nn.one_hot(ti, NE, dtype=flat.dtype), axis=1)
        out = jnp.zeros_like(flat)
        for e in range(NE):
            hh = jax.nn.silu(flat @ w1[e].T) * (flat @ w3[e].T)
            out = out + weights[:, e:e + 1] * (hh @ w2[e].T)
        return x + out.reshape(Bx, Tx, Cx)
    x = x + _L0_gnn_ref(_layernorm(x, axis=-1), adj, L0_gnn_W, L0_gnn_B)
    x = x + _L0_ffn_ref(_layernorm(x, axis=-1)[None], L0_ffn_W_ih, L0_ffn_W_hh, L0_ffn_b_ih, L0_ffn_b_hh, L0_ffn_W_lin, L0_ffn_b_lin, L0_ffn_fw_att, L0_ffn_bw_att)[0]
    x = x + _L1_gnn_ref(_layernorm(x, axis=-1), adj, L1_gnn_neigh_W, L1_gnn_lin_W)
    x = x + _L1_ffn_ref(_layernorm(x, axis=-1)[None], L1_ffn_ln1_w, L1_ffn_ln2_w, L1_ffn_wq, L1_ffn_wk, L1_ffn_wv, L1_ffn_wo, L1_ffn_router_w, L1_ffn_w1, L1_ffn_w2, L1_ffn_w3)[0]
    return x

_drawn_inputs = setup_inputs


def setup_inputs(seed=0):
    import zlib

    import numpy as np

    out = dict(_drawn_inputs(seed))
    spreads = {'L0_gnn_B': (0.0, 0.323),
     'L0_ffn_fw_att': (0.0010000000474974513, 0.6),
     'L0_ffn_bw_att': (0.0010000000474974513, 0.6),
     'L1_ffn_ln1_w': (1.0, 0.6),
     'L1_ffn_ln2_w': (1.0, 0.6)}
    factors = {'L0_ffn_W_ih': 3.372,
     'L0_ffn_W_hh': 8.0,
     'L0_ffn_b_ih': 8.0,
     'L0_ffn_b_hh': 8.0,
     'L0_ffn_W_lin': 8.0,
     'L0_ffn_b_lin': 8.0,
     'L1_ffn_wq': 8.0,
     'L1_ffn_wk': 8.0,
     'L1_ffn_wv': 8.0,
     'L1_ffn_wo': 8.0,
     'L1_ffn_router_w': 8.0,
     'L1_ffn_w1': 8.0,
     'L1_ffn_w2': 8.0,
     'L1_ffn_w3': 8.0}
    for name, (base, spread) in spreads.items():
        noise = np.random.default_rng([zlib.crc32(name.encode()), seed]).standard_normal(out[name].shape)
        drawn = base * np.exp(spread * noise) if base else spread * noise
        out[name] = jnp.asarray(drawn.astype(out[name].dtype))
    for name, factor in factors.items():
        out[name] = (out[name] * factor).astype(out[name].dtype)
    return out
```

```python
import concourse.bass as bass
from concourse import mybir
from contextlib import ExitStack
import numpy as np

F32 = mybir.dt.float32
BF16 = mybir.dt.bfloat16
F16 = mybir.dt.float16
I32 = mybir.dt.int32
ACT = mybir.ActivationFunctionType
ALU = mybir.AluOpType
AX = mybir.AxisListType
RMAX = bass.bass_isa.ReduceOp.max

P = 128
N = 4096
NT = N // P
G = 512
NG = N // G
TPG = G // P
NHEAD, NKV, HD = 4, 2, 32
NE, HID = 8, 341
TINY = 1e-12
HCH = [(0, 128), (128, 128), (256, HID - 256)]


class Steps:

    def __init__(self, eng, sem, start=0):
        self.eng, self.sem, self.start, self.n = eng, sem, start, 0

    def mark(self, ins):
        self.n += 1
        ins.then_inc(self.sem, 1)

    def sync(self):
        self.eng.wait_ge(self.sem, self.start + self.n)

    def done(self, ins):
        self.mark(ins)
        self.sync()


class Phase:

    used = []

    def __init__(self, nc, name):
        self.nc, self.name, self.stack = nc, name, ExitStack()

    def __enter__(self):
        self.stack.__enter__()
        return self

    def __exit__(self, *a):
        return self.stack.__exit__(*a)

    def sb(self, name, shape, dt=F32):
        return self.stack.enter_context(self.nc.sbuf_tensor(f"{self.name}_{name}", shape, dt))

    def ps(self, name, shape, dt=F32):
        return self.stack.enter_context(self.nc.psum_tensor(f"{self.name}_{name}", shape, dt))

    def sem(self, name):
        s = self.nc.alloc_semaphore(f"{self.name}_{name}")
        Phase.used.append(s)
        return s

    def block(self):
        return self.stack.enter_context(self.nc.Block())


def clear_semaphores(nc):
    nc.clear_and_free_semaphores(list(Phase.used))
    Phase.used.clear()
    nc.all_engine_barrier()


def load_constants(nc, T, D):
    with Phase(nc, "load") as ph:
        loaded = ph.sem("loaded")
        zeroed = ph.sem("zeroed")
        made = ph.sem("made")
        block = ph.block()

        @block.sync
        def _(sp):
            sp.dma_start(T.x[:, :, :], D["x"].rearrange("(t p) c -> p t c", p=P)).then_inc(loaded, 16)
            sp.dma_start(T.gnn_w[:, :], D["gnn_w"]).then_inc(loaded, 16)
            sp.dma_start(T.gnn_b[:, :], D["gnn_b"].broadcast_to([P, P])).then_inc(loaded, 16)
            sp.dma_start(T.wih[:, :], D["wih"]).then_inc(loaded, 16)
            sp.dma_start(T.whh[:, :], D["whh"]).then_inc(loaded, 16)
            sp.wait_ge(zeroed, 1)
            sp.dma_start(T.bias_rows[0:1, 0, :], D["b_ih"]).then_inc(loaded, 16)
            sp.dma_start(T.bias_rows[0:1, 1, :], D["b_hh"]).then_inc(loaded, 16)
            sp.wait_ge(loaded, 7 * 16)

        @block.vector
        def _(dve):
            nc.vector.memset(T.bias_rows[:, :, :], 0.0).then_inc(zeroed, 1)
            nc.vector.memset(T.ones[:, :], 1.0)
            nc.vector.memset(T.tiny[:, :], TINY)

        @block.gpsimd
        def _(pool):
            nc.gpsimd.memset(T.ident[:, :], 0.0).then_inc(made, 1)
            pool.wait_ge(made, 1)
            nc.gpsimd.affine_select(out=T.ident[:, :], in_=T.ident[:, :], compare_op=ALU.not_equal, fill=1.0,
                                    base=0, pattern=[[-1, P]], channel_multiplier=1).then_inc(made, 1)


def normalise(nc, name, T, src, dst, dst_t, rms_weight=None, eps=1e-5, tiles=NT):
    with Phase(nc, name) as ph:
        stats = ph.sb("stats", [P, tiles, 6])
        mv = ph.sb("mv", [P, tiles, 2])
        var = ph.sb("var", [P, tiles])
        root = ph.sb("root", [P, tiles])
        inv = ph.sb("inv", [P, tiles])
        tmp = ph.sb("tmp", [P, tiles])
        tp = [ph.ps(f"tp{i}", [P, G]) for i in range(2)]
        chain, var_ready, root_ready = ph.sem("chain"), ph.sem("var_ready"), ph.sem("root_ready")
        rows_ready, transposed, copied = ph.sem("rows_ready"), ph.sem("transposed"), ph.sem("copied")
        block = ph.block()

        @block.vector
        def _(dve):
            s = Steps(dve, chain)
            for t in range(tiles):
                s.mark(nc.vector.bn_stats(stats[:, t, :], src[:, t, :]))
            s.sync()
            for t in range(tiles):
                s.mark(nc.vector.bn_aggr(mv[:, t, :], stats[:, t, :]))
            s.sync()
            if rms_weight is None:
                nc.vector.tensor_scalar(var[:, :], mv[:, :, 1], eps, None, ALU.add).then_inc(var_ready, 1)
            else:
                s.done(nc.vector.tensor_tensor(tmp[:, :], mv[:, :, 0], mv[:, :, 0], ALU.mult))
                nc.vector.scalar_tensor_tensor(out=var[:, :], in0=mv[:, :, 1], scalar=eps, in1=tmp[:, :],
                                               op0=ALU.add, op1=ALU.add).then_inc(var_ready, 1)
            dve.wait_ge(var_ready, 1)
            dve.wait_ge(root_ready, 1)
            s.done(nc.vector.reciprocal(inv[:, :], root[:, :]))
            s.done(nc.vector.tensor_tensor(tmp[:, :], var[:, :], inv[:, :], ALU.mult))
            s.done(nc.vector.tensor_tensor(tmp[:, :], tmp[:, :], root[:, :], ALU.add))
            s.done(nc.vector.tensor_scalar(tmp[:, :], tmp[:, :], 0.5, None, ALU.mult))
            s.done(nc.vector.reciprocal(inv[:, :], tmp[:, :]))
            for t in range(tiles):
                if rms_weight is None:
                    nc.vector.tensor_scalar(dst[:, t, :], src[:, t, :], mv[:, t, 0:1], inv[:, t:t + 1],
                                            ALU.subtract, ALU.mult).then_inc(rows_ready, 1)
                else:
                    nc.vector.scalar_tensor_tensor(out=dst[:, t, :], in0=src[:, t, :], scalar=inv[:, t:t + 1],
                                                   in1=rms_weight[:, :], op0=ALU.mult,
                                                   op1=ALU.mult).then_inc(rows_ready, 1)

        @block.tensor
        def _(pe):
            for g in range(tiles // TPG if dst_t is not None else 0):
                pe.wait_ge(rows_ready, TPG * (g + 1))
                if g >= 2:
                    pe.wait_ge(copied, g - 1)
                for k in range(TPG):
                    last = nc.tensor.transpose(tp[g % 2][:, k * P:(k + 1) * P], dst[:, TPG * g + k, :], T.ident[:, :])
                last.then_inc(transposed, 1)

        @block.scalar
        def _(act):
            act.wait_ge(var_ready, 1)
            nc.scalar.activation(root[:, :], var[:, :], ACT.Sqrt).then_inc(root_ready, 1)
            for g in range(tiles // TPG if dst_t is not None else 0):
                act.wait_ge(transposed, g + 1)
                nc.scalar.copy(dst_t[:, g * G:(g + 1) * G], tp[g % 2][:, :]).then_inc(copied, 1)


def load(nc, name, *pairs):
    with Phase(nc, f"load_{name}") as ph:
        loaded = ph.sem("loaded")
        block = ph.block()

        @block.sync
        def _(sp):
            for dst, src in pairs:
                sp.dma_start(dst, src).then_inc(loaded, 16)
            sp.wait_ge(loaded, 16 * len(pairs))


def project_rows(nc, name, src_t, weight, dst, bias=None):
    with Phase(nc, name) as ph:
        pp = [ph.ps(f"pp{i}", [P, TPG, P]) for i in range(2)]
        multiplied, stored = ph.sem("multiplied"), ph.sem("stored")
        block = ph.block()

        @block.tensor
        def _(pe):
            for g in range(NG):
                if g >= 2:
                    pe.wait_ge(stored, g - 1)
                for k in range(TPG):
                    t = TPG * g + k
                    last = nc.tensor.matmul(pp[g % 2][:, k, :], src_t[:, t * P:(t + 1) * P], weight[:, :],
                                            start=True, stop=True)
                last.then_inc(multiplied, 1)

        @block.vector
        def _(dve):
            for g in range(NG):
                dve.wait_ge(multiplied, g + 1)
                o = dst[:, TPG * g:TPG * (g + 1), :]
                if bias is None:
                    nc.vector.tensor_copy(o, pp[g % 2][:, :, :]).then_inc(stored, 1)
                else:
                    for k in range(TPG):
                        last = nc.vector.tensor_tensor(dst[:, TPG * g + k, :], pp[g % 2][:, k, :], bias[:, :], ALU.add)
                    last.then_inc(stored, 1)


LEAD = 4


def lead(eng, *sems):
    for s in sems:
        eng.sem_inc(s, LEAD)


def graph_product(nc, name, T, adj, rows, dst, weigh, deg=None, groups=NG):
    CP = 512
    NP = N // CP
    BP = CP // P
    NB = N // P
    NR = 4
    LAG = 3
    NTP = 4
    NW = 4
    with Phase(nc, name) as ph:
        ring = ph.sb("ring", [P, NR, TPG, CP])
        wt = [ph.sb(f"wt{i}", [P, G]) for i in range(NW)]
        tp = [ph.ps(f"tp{i}", [P, G]) for i in range(NTP)]
        acc = ph.ps("acc", [P, G])
        if weigh:
            dist = [ph.sb(f"dist{i}", [P, G]) for i in range(2)]
            rec = [ph.sb(f"rec{i}", [P, G]) for i in range(2)]
            sens = [ph.sb(f"sens{i}", [P, G]) for i in range(2)]
            out_t = ph.sb("out_t", [P, G])
            back = ph.ps("back", [P, TPG, P])
        else:
            dsum = ph.sb("dsum", [P, NG, TPG, NP])
        loaded = [ph.sem(f"loaded{i}") for i in range(NR)]
        transposed = ph.sem("transposed")
        block_ready = ph.sem("block_ready")
        act_block, dve_block = ph.sem("act_block"), ph.sem("dve_block")
        multiplied = ph.sem("multiplied")
        rec_ready, sq_ready, sens_ready = ph.sem("rec_ready"), ph.sem("sq_ready"), ph.sem("sens_ready")
        dist_ready = ph.sem("dist_ready")
        summed = ph.sem("summed")
        acc_out, back_done, added = ph.sem("acc_out"), ph.sem("back_done"), ph.sem("added")
        chain = ph.sem("chain")
        block = ph.block()

        @block.sync
        def _(sp):
            def load(g, p):
                src = adj[bass.ds(g * G, G), p * CP:(p + 1) * CP]
                sp.dma_start(ring[:, p % NR, :, :],
                             src.rearrange("(t p) c -> p t c", p=P)).then_inc(loaded[p % NR], 16)

            def reload(g, p, next_g):
                if weigh:
                    sp.wait_ge(transposed, LEAD + g * NB + BP * (p + 1))
                else:
                    sp.wait_ge(summed, LEAD + g * NP + p + 1)
                if p + NR < NP:
                    load(g, p + NR)
                else:
                    load(next_g, p + NR - NP)

            for p in range(NR):
                load(0, p)
            if groups > 1:
                with sp.Fori(0, groups - 1) as g:
                    for p in range(NP):
                        reload(g, p, g + 1)
            for p in range(NP - NR):
                reload(groups - 1, p, None)

        @block.tensor
        def _(pe):
            lead(pe, transposed, multiplied)

            def product(g, j):
                if weigh:
                    pe.wait_ge(block_ready, LEAD + g * NB + j + 1)
                elif j % 2:
                    pe.wait_ge(act_block, LEAD + g * (NB // 2) + j // 2 + 1)
                else:
                    pe.wait_ge(dve_block, LEAD + g * (NB // 2) + j // 2 + 1)
                if j == 0:
                    pe.wait_ge(acc_out, LEAD + g)
                nc.tensor.matmul(acc[:, :], rows[:, j, :], wt[j % NW][:, :], start=(j == 0),
                                 stop=(j == NB - 1)).then_inc(multiplied, 1)

            with pe.Fori(0, groups) as g:
                for j in range(NB):
                    p, b = divmod(j, BP)
                    if b == 0:
                        pe.wait_ge(loaded[p % NR], (g * (NP // NR) + p // NR + 1) * 16)
                    if weigh:
                        pe.wait_ge(block_ready, LEAD + g * NB + j - NTP + 1)
                    elif j % 2:
                        pe.wait_ge(act_block, LEAD + g * (NB // 2) + j // 2 - NTP // 2 + 1)
                    else:
                        pe.wait_ge(dve_block, LEAD + g * (NB // 2) + j // 2 - NTP // 2 + 1)
                    for k in range(TPG):
                        last = nc.tensor.transpose(tp[j % NTP][:, k * P:(k + 1) * P],
                                                   ring[:, p % NR, k, b * P:(b + 1) * P], T.ident[:, :])
                    last.then_inc(transposed, 1)
                    if j >= LAG:
                        product(g, j - LAG)
                for j in range(NB - LAG, NB):
                    product(g, j)
                if weigh:
                    pe.wait_ge(acc_out, LEAD + g + 1)
                    pe.wait_ge(added, LEAD + g)
                    for k in range(TPG):
                        last = nc.tensor.transpose(back[:, k, :], out_t[:, k * P:(k + 1) * P], T.ident[:, :])
                    last.then_inc(back_done, 1)

        @block.scalar
        def _(act):
            lead(act, acc_out)
            if weigh:
                lead(act, sens_ready, dist_ready)

                def shift(g, j):
                    act.wait_ge(transposed, LEAD + g * NB + j + 1)
                    nc.scalar.activation(dist[j % 2][:, :], tp[j % NTP][:, :], ACT.Identity,
                                         bias=T.tiny[:, :]).then_inc(dist_ready, 1)
            else:
                lead(act, act_block)
            with act.Fori(0, groups) as g:
                if weigh:
                    act.wait_ge(rec_ready, LEAD + g * NB)
                    shift(g, 0)
                for j in range(NB):
                    if weigh:
                        if j + 1 < NB:
                            act.wait_ge(rec_ready, LEAD + g * NB + j)
                            shift(g, j + 1)
                        act.wait_ge(rec_ready, LEAD + g * NB + j + 1)
                        act.wait_ge(block_ready, LEAD + g * NB + j - 1)
                        nc.scalar.activation(sens[j % 2][:, :], rec[j % 2][:, :], ACT.Square,
                                             bias=-1.0).then_inc(sq_ready, 1)
                        act.wait_ge(sq_ready, g * NB + j + 1)
                        nc.scalar.activation(sens[j % 2][:, :], sens[j % 2][:, :], ACT.Exp,
                                             scale=-2.0).then_inc(sens_ready, 1)
                    elif j % 2:
                        act.wait_ge(transposed, LEAD + g * NB + j + 1)
                        act.wait_ge(multiplied, LEAD + g * NB + j - NW + 1)
                        nc.scalar.copy(wt[j % NW][:, :], tp[j % NTP][:, :]).then_inc(act_block, 1)
                act.wait_ge(multiplied, LEAD + (g + 1) * NB)
                if weigh:
                    act.wait_ge(added, LEAD + g)
                    nc.scalar.copy(out_t[:, :], acc[:, :]).then_inc(acc_out, 1)
                else:
                    nc.scalar.copy(dst[:, bass.ts(g, G)], acc[:, :]).then_inc(acc_out, 1)

        @block.vector
        def _(dve):
            if weigh:
                lead(dve, rec_ready, block_ready, added)

                def mask(g, j):
                    dve.wait_ge(sens_ready, LEAD + g * NB + j + 1)
                    dve.wait_ge(multiplied, LEAD + g * NB + j - NW + 1)
                    nc.vector.scalar_tensor_tensor(out=wt[j % NW][:, :], in0=tp[j % NTP][:, :], scalar=1.0,
                                                   in1=sens[j % 2][:, :], op0=ALU.is_lt,
                                                   op1=ALU.mult).then_inc(block_ready, 1)

                with dve.Fori(0, groups) as g:
                    for j in range(NB):
                        dve.wait_ge(dist_ready, LEAD + g * NB + j + 1)
                        dve.wait_ge(sens_ready, LEAD + g * NB + j - 1)
                        nc.vector.reciprocal(rec[j % 2][:, :], dist[j % 2][:, :]).then_inc(rec_ready, 1)
                        if j >= 1:
                            mask(g, j - 1)
                    mask(g, NB - 1)
                    dve.wait_ge(back_done, g + 1)
                    o = dst[:, bass.ds(g * TPG, TPG), :].rearrange("p t c -> p (t c)")
                    nc.vector.tensor_tensor(o, o, back[:, :, :].rearrange("p t c -> p (t c)"),
                                            ALU.add).then_inc(added, 1)
            else:
                lead(dve, dve_block, summed)
                with dve.Fori(0, groups) as g:
                    for j in range(NB):
                        p, b = divmod(j, BP)
                        if j % 2 == 0:
                            dve.wait_ge(transposed, LEAD + g * NB + j + 1)
                            dve.wait_ge(multiplied, LEAD + g * NB + j - NW + 1)
                            nc.vector.tensor_copy(wt[j % NW][:, :], tp[j % NTP][:, :]).then_inc(dve_block, 1)
                        if b == BP - 1:
                            dve.wait_ge(loaded[p % NR], (g * (NP // NR) + p // NR + 1) * 16)
                            dve.wait_ge(transposed, LEAD + g * NB + j + 1)
                            nc.vector.tensor_reduce(dsum[:, bass.ds(g, 1), :, p].rearrange("p a t -> p (a t)"),
                                                    ring[:, p % NR, :, :], AX.X, ALU.add).then_inc(summed, 1)
                s = Steps(dve, chain)
                dve.wait_ge(summed, LEAD + NG * NP)
                s.done(nc.vector.tensor_reduce(deg[:, :], dsum[:, :, :, :].rearrange("p g t n -> p (g t) n"),
                                               AX.X, ALU.add))
                s.done(nc.vector.tensor_scalar(deg[:, :], deg[:, :], 1.0, None, ALU.add))
                s.done(nc.vector.reciprocal(deg[:, :], deg[:, :]))


CHUNK = 32
GATES = [0, 1, 3, 2]


def lstm(nc, T):
    SPL = 2 * CHUNK
    IPG = G // SPL
    UPI = NT // IPG
    SPU = SPL // UPI
    TAIL = 2 * TPG + 8
    with Phase(nc, "lstm") as ph:
        wrec = ph.sb("wrec", [P, 2, 4, P], F16)
        win = ph.sb("win", [P, 4, P])
        bias = ph.sb("bias", [P, 4, P])
        wtmp = ph.sb("wtmp", [P, 4, P])
        tanhs = ph.sb("tanhs", [P, 5])
        terms = ph.sb("terms", [P, 2])
        c_twice = ph.ps("c_twice", [P, 1])
        tanh_c = ph.sb("tanh_c", [P, 1])
        half_term = ph.sb("half_term", [P, 1])
        o_plus = ph.sb("o_plus", [P, 1])
        warm = ph.sb("warm", [P, 1])
        h_parts = ph.sb("h_parts", [P, SPL, 2], F16)
        h_full = ph.sb("h_full", [P, SPL])
        gates = [ph.ps(f"gates{b}", [P, CHUNK, 4]) for b in range(2)]
        largest = ph.sb("largest", [P, 2])
        scale = ph.sb("scale", [P, 2])
        chain, weights_ready = ph.sem("chain"), ph.sem("weights_ready")
        largest_ready, largest_of_all, scale_ready = (ph.sem(n) for n in ("largest_ready", "largest_of_all", "scale_ready"))
        gates_ready, tanhs_ready = ph.sem("gates_ready"), ph.sem("tanhs_ready")
        c_ready, c_kept = ph.sem("c_ready"), ph.sem("c_kept")
        half_ready, o_ready = ph.sem("half_ready"), ph.sem("o_ready")
        tanh_c_ready = ph.sem("tanh_c_ready")
        high_ready, low_ready, full_ready = ph.sem("high_ready"), ph.sem("low_ready"), ph.sem("full_ready")
        collected = ph.sem("collected")
        ring = ph.sb("ring", [P, UPI, TPG, P])
        dist = ph.sb("dist", [P, G])
        rec = ph.sb("rec", [P, G])
        sens = ph.sb("sens", [P, G])
        wt = ph.sb("wt", [P, 2, G])
        msg_now = ph.sb("msg_now", [P, UPI, P])
        part_sum = ph.sb("part_sum", [P, G])
        total = ph.sb("total", [P, G])
        row = ph.sb("row", [P, TPG, P])
        square = ph.sb("square", [P, TPG, P])
        mean, var, root, inv, tmp = (ph.sb(n, [P, TPG]) for n in ("mean", "var", "root", "inv", "tmp"))
        tp = ph.ps("tp", [P, G])
        acc = ph.ps("acc", [P, G])
        back = ph.ps("back", [P, TPG, P])
        loaded = [ph.sem(f"loaded{j}") for j in range(UPI)]
        transposed, dist_ready, rec_ready = ph.sem("transposed"), ph.sem("dist_ready"), ph.sem("rec_ready")
        sq_ready, sens_ready, block_ready = ph.sem("sq_ready"), ph.sem("sens_ready"), ph.sem("block_ready")
        multiplied, acc_out, summed = ph.sem("multiplied"), ph.sem("acc_out"), ph.sem("summed")
        msg_copied, total_zeroed = ph.sem("msg_copied"), ph.sem("total_zeroed")
        back_done, tail_chain = ph.sem("back_done"), ph.sem("tail_chain")
        var_ready, root_ready, rows_ready = ph.sem("var_ready"), ph.sem("root_ready"), ph.sem("rows_ready")
        row_t_done, row_t_out = ph.sem("row_t_done"), ph.sem("row_t_out")
        block = ph.block()

        @block.sync
        def _(sp):
            def load_block(group, i, j):
                src = T.D["adj"][bass.ds(group * G, G), bass.ds((i * UPI + j) * P, P)]
                sp.dma_start(ring[:, j, :, :], src.rearrange("(t p) c -> p t c", p=P)).then_inc(loaded[j], 16)

            def reload(q, group, i):
                for j in range(UPI):
                    sp.wait_ge(transposed, LEAD + q * UPI + j + 1)
                    load_block(group, i, j)

            for j in range(UPI):
                load_block(1, 0, j)
            with sp.Fori(0, NG - 2) as g:
                with sp.Fori(0, IPG - 1) as i:
                    reload(g * IPG + i, g + 1, i + 1)
                reload(g * IPG + IPG - 1, g + 2, 0)
            with sp.Fori(0, IPG - 1) as i:
                reload((NG - 2) * IPG + i, NG - 1, i + 1)

        @block.tensor
        def _(pe):
            lead(pe, transposed, multiplied)

            def input_gates(b, first_step, m):
                g, k = m // 2, m % 2
                w = (win if k else bias)[:, g, :]
                x = T.xn_t[:, bass.ds(first_step, CHUNK)] if k else T.ones[:, 0:CHUNK]
                nc.tensor.matmul(gates[b][:, :, g], w, x, start=(m == 0), stop=False, skip_group_check=True)

            def steps(base, q=None):
                for n in range(SPL):
                    b, t = divmod(n, CHUNK)
                    last_n = (n - 1) % SPL
                    for part, sem in ((0, high_ready), (1, low_ready)):
                        pe.wait_ge(sem, base + n + 1)
                        for w in range(2 - part):
                            for g in range(4):
                                last = nc.tensor.matmul(gates[b][:, t, g:g + 1], wrec[:, w, g, :],
                                                        h_parts[:, last_n, part:part + 1], start=False, stop=True,
                                                        skip_group_check=True)
                    last.then_inc(gates_ready, 1)
                    if 2 <= t < 10:
                        input_gates(1 - b, base + (b + 1) * CHUNK, t - 2)
                    j, s = divmod(n, SPU)
                    if q is not None and s == 0:
                        pe.wait_ge(loaded[j], (q + 1) * 16)
                        pe.wait_ge(dist_ready, LEAD + q * UPI + j)
                        for k in range(TPG):
                            last = nc.tensor.transpose(tp[:, k * P:(k + 1) * P], ring[:, j, k, :], T.ident[:, :])
                        last.then_inc(transposed, 1)
                    if q is not None and s in (13, 14):
                        half = s - 13
                        c = slice(half * (G // 2), (half + 1) * (G // 2))
                        pe.wait_ge(block_ready, LEAD + (q * UPI + j) * 2 + half + 1)
                        if j == 0 and half == 0:
                            pe.wait_ge(acc_out, LEAD + q)
                            pe.wait_ge(msg_copied, q + 1)
                        nc.tensor.matmul(acc[:, c], msg_now[:, j, :], wt[:, j % 2, c], start=(j == 0 and half == 0),
                                         stop=True, skip_group_check=True).then_inc(multiplied, 1)

            pe.wait_ge(weights_ready, 1)
            for m in range(8):
                input_gates(0, 0, m)
            with pe.Fori(0, NG - 1) as g:
                with pe.Fori(0, IPG) as i:
                    steps(g * G + i * SPL, g * IPG + i)
                pe.wait_ge(summed, LEAD + (g + 1) * IPG)
                for k in range(TPG):
                    last = nc.tensor.transpose(back[:, k, :], total[:, k * P:(k + 1) * P], T.ident[:, :])
                last.then_inc(back_done, 1)
                pe.wait_ge(rows_ready, g + 1)
                for k in range(TPG):
                    last = nc.tensor.transpose(tp[:, k * P:(k + 1) * P], row[:, k, :], T.ident[:, :])
                last.then_inc(row_t_done, 1)
                pe.wait_ge(row_t_out, g + 1)
                for m in range(8):
                    input_gates(0, g * G + G, m)
            with pe.Fori(0, IPG) as i:
                steps((NG - 1) * G + i * SPL)

        @block.scalar
        def _(act):
            lead(act, dist_ready, acc_out, sq_ready)
            nc.scalar.activation(warm[:, :], T.tiny[:, :], ACT.Tanh)
            unscale = act.alloc_register("unscale")
            act.wait_ge(scale_ready, 1)
            act.reg_load(unscale, scale[0:1, 1:2].bitcast(I32))

            def steps(base, q=None):
                for n in range(SPL):
                    b, t = divmod(n, CHUNK)
                    act.wait_ge(gates_ready, base + n + 1)
                    act.wait_ge(full_ready, base + n + 1)
                    nc.scalar.activation(tanhs[:, 0:4], gates[b][:, t, :], ACT.Tanh,
                                         scale=unscale).then_inc(tanhs_ready, 1)
                    act.wait_ge(c_ready, base + n + 1)
                    nc.scalar.activation(tanh_c[:, :], c_twice[:, :], ACT.Tanh, scale=0.5).then_inc(tanh_c_ready, 1)
                    if q is None:
                        continue
                    j, s = divmod(n, SPU)
                    if s == 0:
                        act.wait_ge(transposed, LEAD + q * UPI + j + 1)
                        act.wait_ge(block_ready, LEAD + (q * UPI + j) * 2)
                        nc.scalar.activation(dist[:, :], tp[:, :], ACT.Identity,
                                             bias=T.tiny[:, :]).then_inc(dist_ready, 1)
                    if s == 9:
                        act.wait_ge(rec_ready, (q * UPI + j + 1) * 8)
                        nc.scalar.activation(sens[:, :], rec[:, :], ACT.Square, bias=-1.0).then_inc(sq_ready, 1)
                    if s == 10:
                        act.wait_ge(sq_ready, LEAD + q * UPI + j + 1)
                        nc.scalar.activation(sens[:, :], sens[:, :], ACT.Exp, scale=-2.0).then_inc(sens_ready, 1)
                    if n == SPL - 1:
                        act.wait_ge(multiplied, LEAD + (q + 1) * UPI * 2)
                        act.wait_ge(summed, LEAD + q)
                        nc.scalar.copy(part_sum[:, :], acc[:, :]).then_inc(acc_out, 1)

            with act.Fori(0, NG - 1) as g:
                with act.Fori(0, IPG) as i:
                    steps(g * G + i * SPL, g * IPG + i)
                act.wait_ge(var_ready, g + 1)
                nc.scalar.activation(root[:, :], var[:, :], ACT.Sqrt).then_inc(root_ready, 1)
                act.wait_ge(row_t_done, g + 1)
                nc.scalar.copy(T.xn_t[:, bass.ds(g * G + G, G)], tp[:, :]).then_inc(row_t_out, 1)
                nc.scalar.activation(warm[:, :], T.tiny[:, :], ACT.Tanh)
            with act.Fori(0, IPG) as i:
                steps((NG - 1) * G + i * SPL)

        @block.vector
        def _(dve):
            s = Steps(dve, chain)
            s.mark(nc.vector.memset(T.xn_t[:, N:N + CHUNK], 0.0))
            s.mark(nc.vector.tensor_tensor(T.bias_rows[:, 0, :], T.bias_rows[:, 0, :], T.bias_rows[:, 1, :], ALU.add))
            s.sync()
            for g, src in enumerate(GATES):
                cols = slice(src * P, (src + 1) * P)
                k = 1.0 if g == 3 else 0.5
                s.mark(nc.vector.tensor_scalar(win[:, g, :], T.wih[:, cols], k, None, ALU.mult))
                s.mark(nc.vector.tensor_scalar(bias[:, g, :], T.bias_rows[:, 0, cols], k, None, ALU.mult))
                s.mark(nc.vector.tensor_scalar(wtmp[:, g, :], T.whh[:, cols], k / 2, None, ALU.mult))
            s.sync()
            nc.vector.tensor_reduce(largest[:, 0:1], wtmp[:, :, :], AX.XY, ALU.max,
                                    apply_absolute_value=True).then_inc(largest_ready, 1)
            dve.wait_ge(largest_of_all, 1)
            s.done(nc.vector.tensor_scalar(scale[:, 0:1].bitcast(I32), largest[:, 1:2].bitcast(I32), 0x7F800000, None,
                                           ALU.bitwise_and))
            s.done(nc.vector.tensor_scalar(scale[:, 0:1], scale[:, 0:1], 2.0 ** -20, None, ALU.max))
            nc.vector.tensor_scalar(scale[:, 1:2], scale[:, 0:1], 2.0 ** -13, None, ALU.mult).then_inc(scale_ready, 1)
            dve.wait_ge(scale_ready, 1)
            s.done(nc.vector.reciprocal(scale[:, 0:1], scale[:, 1:2]))
            for w in (win, bias, wtmp):
                s.mark(nc.vector.tensor_scalar(w[:, :, :], w[:, :, :], scale[:, 0:1], None, ALU.mult))
            s.sync()
            s.done(nc.vector.tensor_copy(wrec[:, 0, :, :], wtmp[:, :, :]))
            s.done(nc.vector.tensor_tensor(wrec[:, 1, :, :], wtmp[:, :, :], wrec[:, 0, :, :], ALU.subtract))
            nc.vector.memset(c_twice[:, :], 0.0).then_inc(weights_ready, 1)
            nc.vector.memset(tanhs[:, 4:5], 0.0).then_inc(c_kept, 1)
            nc.vector.memset(h_parts[:, SPL - 1, 0:1], 0.0).then_inc(high_ready, 1)
            nc.vector.memset(h_parts[:, SPL - 1, 1:2], 0.0).then_inc(low_ready, 1)
            nc.vector.memset(h_full[:, :], 0.0).then_inc(full_ready, 1)

            def steps(base, chunk, q=None):
                for n in range(SPL):
                    at = base + n + 1
                    dve.wait_ge(tanhs_ready, at)
                    dve.wait_ge(c_kept, at)
                    nc.vector.scalar_tensor_tensor(out=terms[:, :], in0=tanhs[:, 0:2], scalar=1.0,
                                                   in1=tanhs[:, 3:5], op0=ALU.add, op1=ALU.mult,
                                                   accum_out=c_twice[:, :]).then_inc(c_ready, 1)
                    dve.wait_ge(c_ready, at)
                    nc.vector.tensor_scalar(half_term[:, :], terms[:, 1:2], 0.5, None, ALU.mult).then_inc(half_ready, 1)
                    nc.vector.tensor_scalar(o_plus[:, :], tanhs[:, 2:3], 1.0, None, ALU.add).then_inc(o_ready, 1)
                    dve.wait_ge(tanh_c_ready, at)
                    nc.vector.scalar_tensor_tensor(out=h_parts[:, n, 0:1], in0=tanhs[:, 2:3], scalar=1.0,
                                                   in1=tanh_c[:, :], op0=ALU.add,
                                                   op1=ALU.mult).then_inc(high_ready, 1)
                    dve.wait_ge(high_ready, at + 1)
                    dve.wait_ge(o_ready, at)
                    nc.vector.scalar_tensor_tensor(out=h_parts[:, n, 1:2], in0=tanh_c[:, :], scalar=o_plus[:, :],
                                                   in1=h_parts[:, n, 0:1], op0=ALU.mult,
                                                   op1=ALU.subtract).then_inc(low_ready, 1)
                    dve.wait_ge(half_ready, at)
                    nc.vector.scalar_tensor_tensor(out=tanhs[:, 4:5], in0=terms[:, 0:1], scalar=0.5,
                                                   in1=half_term[:, :], op0=ALU.mult, op1=ALU.add).then_inc(c_kept, 1)
                    if n % CHUNK == 0:
                        dve.wait_ge(collected, chunk + n // CHUNK)
                    nc.vector.scalar_tensor_tensor(out=h_full[:, n:n + 1], in0=tanhs[:, 2:3], scalar=1.0,
                                                   in1=tanh_c[:, :], op0=ALU.add, op1=ALU.mult).then_inc(full_ready, 1)
                    if q is None:
                        continue
                    j, s = divmod(n, SPU)
                    if 1 <= s <= 8:
                        c = slice((s - 1) * (G // 8), s * (G // 8))
                        dve.wait_ge(dist_ready, LEAD + q * UPI + j + 1)
                        dve.wait_ge(sq_ready, LEAD + q * UPI + j)
                        nc.vector.reciprocal(rec[:, c], dist[:, c]).then_inc(rec_ready, 1)
                    if s in (11, 12):
                        half = s - 11
                        c = slice(half * (G // 2), (half + 1) * (G // 2))
                        dve.wait_ge(sens_ready, q * UPI + j + 1)
                        dve.wait_ge(multiplied, LEAD + (q * UPI + j - 1) * 2)
                        nc.vector.scalar_tensor_tensor(out=wt[:, j % 2, c], in0=dist[:, c], scalar=1.0,
                                                       in1=sens[:, c], op0=ALU.is_lt,
                                                       op1=ALU.mult).then_inc(block_ready, 1)

            def wide(column):
                return column[:, :].unsqueeze(2).broadcast_to([P, TPG, P])

            lead(dve, block_ready)
            with dve.Fori(0, NG - 1) as g:
                with dve.Fori(0, IPG) as i:
                    steps(g * G + i * SPL, LEAD - 1 + (g * IPG + i) * 2, g * IPG + i)
                s = Steps(dve, tail_chain, g * TAIL)
                dve.wait_ge(back_done, g + 1)
                x = T.x[:, bass.ds(g * TPG + TPG, TPG), :]
                for k in range(TPG):
                    s.mark(nc.vector.scalar_tensor_tensor(out=row[:, k, :], in0=back[:, k, :], scalar=0.0,
                                                          in1=T.x[:, bass.ds(g * TPG + TPG + k, 1), :]
                                                          .rearrange("p a c -> p (a c)"), op0=ALU.add, op1=ALU.add,
                                                          accum_out=mean[:, k:k + 1]))
                s.sync()
                s.mark(nc.vector.tensor_scalar(x, row[:, :, :], 0.0, None, ALU.add))
                s.done(nc.vector.tensor_scalar(mean[:, :], mean[:, :], 1 / P, None, ALU.mult))
                s.done(nc.vector.tensor_tensor(row[:, :, :], row[:, :, :], wide(mean), ALU.subtract))
                for k in range(TPG):
                    s.mark(nc.vector.scalar_tensor_tensor(out=square[:, k, :], in0=row[:, k, :], scalar=1.0,
                                                          in1=row[:, k, :], op0=ALU.mult, op1=ALU.mult,
                                                          accum_out=var[:, k:k + 1]))
                s.sync()
                nc.vector.tensor_scalar(var[:, :], var[:, :], 1 / P, 1e-5, ALU.mult, ALU.add).then_inc(var_ready, 1)
                dve.wait_ge(root_ready, g + 1)
                dve.wait_ge(var_ready, g + 1)
                s.done(nc.vector.reciprocal(inv[:, :], root[:, :]))
                s.done(nc.vector.tensor_tensor(tmp[:, :], var[:, :], inv[:, :], ALU.mult))
                s.done(nc.vector.tensor_tensor(tmp[:, :], tmp[:, :], root[:, :], ALU.add))
                s.done(nc.vector.tensor_scalar(tmp[:, :], tmp[:, :], 0.5, None, ALU.mult))
                s.done(nc.vector.reciprocal(inv[:, :], tmp[:, :]))
                assert s.n == TAIL
                last = nc.vector.tensor_tensor(row[:, :, :], row[:, :, :], wide(inv), ALU.mult)
                last.then_inc(rows_ready, 1)
            with dve.Fori(0, IPG) as i:
                steps((NG - 1) * G + i * SPL, LEAD - 1 + (NG - 1) * IPG * 2 + i * 2)

        @block.gpsimd
        def _(pool):
            lead(pool, collected, summed)
            pool.wait_ge(largest_ready, 1)
            nc.gpsimd.partition_all_reduce(largest[:, 1:2], largest[:, 0:1], P, RMAX).then_inc(largest_of_all, 1)

            def collect(base):
                for b in range(2):
                    pool.wait_ge(full_ready, base + (b + 1) * CHUNK + 1)
                    nc.gpsimd.tensor_copy(T.hid_t[:, bass.ds(base + b * CHUNK, CHUNK)],
                                          h_full[:, b * CHUNK:(b + 1) * CHUNK]).then_inc(collected, 1)

            with pool.Fori(0, NG - 1) as g:
                nc.gpsimd.memset(total[:, :], 0.0).then_inc(total_zeroed, 1)
                with pool.Fori(0, IPG) as i:
                    q = g * IPG + i
                    pool.wait_ge(multiplied, LEAD + q * UPI * 2)
                    nc.gpsimd.tensor_copy(msg_now[:, :, :], T.msg[:, bass.ds(i * UPI, UPI), :]).then_inc(msg_copied, 1)
                    collect(g * G + i * SPL)
                    pool.wait_ge(acc_out, LEAD + q + 1)
                    pool.wait_ge(total_zeroed, g + 1)
                    nc.gpsimd.tensor_tensor(total[:, :], total[:, :], part_sum[:, :], ALU.add).then_inc(summed, 1)
                pool.wait_ge(back_done, g + 1)
            with pool.Fori(0, IPG) as i:
                collect((NG - 1) * G + i * SPL)


def add_sequence_sums(nc, T):
    with Phase(nc, "sums") as ph:
        logit = [ph.ps(f"logit{i}", [P, 2, G]) for i in range(2)]
        back = [ph.ps(f"back{i}", [P, TPG, P]) for i in range(2)]
        wsel = ph.sb("wsel", [P, 2, P])
        one = [ph.sb(f"one{i}", [P, G]) for i in range(2)]
        cls = ph.sb("cls", [P, G])
        w = ph.sb("w", [P, N])
        inc = ph.sb("inc", [P, N])
        zero = ph.sb("zero", [P, G])
        cols = ph.sb("cols", [P, 6])
        wlin, blin, att = ph.sb("wlin", [P, 2]), ph.sb("blin", [P, 2]), ph.sb("att", [P, 2])
        loaded, ready, chain = ph.sem("loaded"), ph.sem("ready"), ph.sem("chain")
        logits_ready, logit_used, one_ready = ph.sem("logits_ready"), ph.sem("logit_used"), ph.sem("one_ready")
        update_ready, transposed, added = ph.sem("update_ready"), ph.sem("transposed"), ph.sem("added")
        block = ph.block()

        @block.sync
        def _(sp):
            sp.dma_start(wlin[:, :], T.D["w_lin"]).then_inc(loaded, 16)
            sp.dma_start(blin[:, :], T.D["b_lin"].broadcast_to([P, 2])).then_inc(loaded, 16)
            sp.dma_start(att[:, 0:1], T.D["fw_att"]).then_inc(loaded, 16)
            sp.dma_start(att[:, 1:2], T.D["bw_att"]).then_inc(loaded, 16)

        @block.tensor
        def _(pe):
            pe.wait_ge(ready, 1)
            for g in range(NG):
                if g >= 2:
                    pe.wait_ge(logit_used, g - 1)
                for l in range(2):
                    last = nc.tensor.matmul(logit[g % 2][:, l, :], wsel[:, l, :], T.hid_t[:, g * G:(g + 1) * G],
                                            start=True, stop=True)
                last.then_inc(logits_ready, 1)
            for g in range(NG):
                pe.wait_ge(update_ready, g + 1)
                if g >= 2:
                    pe.wait_ge(added, g - 1)
                for k in range(TPG):
                    t = TPG * g + k
                    last = nc.tensor.transpose(back[g % 2][:, k, :], T.hid_t[:, t * P:(t + 1) * P], T.ident[:, :])
                last.then_inc(transposed, 1)

        @block.scalar
        def _(act):
            act.wait_ge(ready, 1)
            for g in range(NG):
                act.wait_ge(logits_ready, g + 1)
                if g >= 2:
                    act.wait_ge(logit_used, g - 1)
                nc.scalar.activation(one[g % 2][:, :], logit[g % 2][:, 1, :], ACT.Identity,
                                     bias=blin[:, 1:2]).then_inc(one_ready, 1)

        @block.vector
        def _(dve):
            s = Steps(dve, chain)
            dve.wait_ge(loaded, 64)
            s.mark(nc.vector.memset(zero[:, :], 0.0))
            for l in range(2):
                s.mark(nc.vector.tensor_scalar(wsel[:, l, :], T.ones[:, :], wlin[:, l:l + 1], 0.5, ALU.mult, ALU.mult))
            s.mark(nc.vector.tensor_scalar(cols[:, 0:2], att[:, :], 0.5, None, ALU.mult))
            s.sync()
            s.mark(nc.vector.tensor_tensor(cols[:, 2:3], cols[:, 0:1], cols[:, 1:2], ALU.subtract))
            nc.vector.tensor_scalar(cols[:, 3:4], cols[:, 0:1], -1.0, None, ALU.mult).then_inc(ready, 1)
            for g in range(NG):
                c = slice(g * G, (g + 1) * G)
                dve.wait_ge(one_ready, g + 1)
                s.done(nc.vector.scalar_tensor_tensor(out=cls[:, :], in0=logit[g % 2][:, 0, :], scalar=blin[:, 0:1],
                                                      in1=one[g % 2][:, :], op0=ALU.add, op1=ALU.is_lt))
                nc.vector.tensor_tensor(w[:, c], cls[:, :], T.hid_t[:, c], ALU.mult).then_inc(logit_used, 1)
                dve.wait_ge(logit_used, g + 1)
                start = 0.0 if g == 0 else inc[:, g * G - 1:g * G]
                s.done(nc.vector.tensor_tensor_scan(out=inc[:, c], data0=w[:, c], data1=zero[:, :],
                                                    initial=start, op0=ALU.add, op1=ALU.add))
            s.done(nc.vector.tensor_tensor(cols[:, 4:5], inc[:, N - 1:N], cols[:, 1:2], ALU.mult))
            for g in range(NG):
                c = slice(g * G, (g + 1) * G)
                s.done(nc.vector.scalar_tensor_tensor(out=T.hid_t[:, c], in0=inc[:, c], scalar=cols[:, 2:3],
                                                      in1=T.hid_t[:, c], op0=ALU.mult, op1=ALU.add))
                s.done(nc.vector.scalar_tensor_tensor(out=T.hid_t[:, c], in0=w[:, c], scalar=cols[:, 3:4],
                                                      in1=T.hid_t[:, c], op0=ALU.mult, op1=ALU.add))
                nc.vector.tensor_scalar(T.hid_t[:, c], T.hid_t[:, c], cols[:, 4:5], None,
                                        ALU.add).then_inc(update_ready, 1)
                dve.wait_ge(transposed, g + 1)
                o = T.x[:, TPG * g:TPG * (g + 1), :]
                nc.vector.tensor_tensor(o, o, back[g % 2][:, :, :], ALU.add).then_inc(added, 1)


def combine_neighbours(nc, T):
    with Phase(nc, "combine") as ph:
        own = [ph.ps(f"own{i}", [P, TPG, P]) for i in range(2)]
        nb = [ph.ps(f"nb{i}", [P, TPG, P]) for i in range(2)]
        lin = ph.sb("lin", [P, 2, P])
        loaded, multiplied, scaled, added = (ph.sem(n) for n in ("loaded", "multiplied", "scaled", "added"))
        block = ph.block()

        @block.sync
        def _(sp):
            sp.dma_start(lin[:, :, :], T.D["lin_w"].rearrange("(a p) o -> p a o", p=P)).then_inc(loaded, 16)

        @block.tensor
        def _(pe):
            pe.wait_ge(loaded, 16)
            for g in range(NG):
                if g >= 2:
                    pe.wait_ge(added, g - 1)
                for k in range(TPG):
                    c = slice((TPG * g + k) * P, (TPG * g + k + 1) * P)
                    nc.tensor.matmul(own[g % 2][:, k, :], T.xn_t[:, c], lin[:, 0, :], start=True, stop=True)
                    last = nc.tensor.matmul(nb[g % 2][:, k, :], T.agg_t[:, c], lin[:, 1, :], start=True, stop=True)
                last.then_inc(multiplied, 1)

        @block.vector
        def _(dve):
            for g in range(NG):
                dve.wait_ge(multiplied, g + 1)
                for k in range(TPG):
                    t = TPG * g + k
                    last = nc.vector.scalar_tensor_tensor(out=T.x[:, t, :], in0=nb[g % 2][:, k, :],
                                                          scalar=T.deg[:, t:t + 1], in1=T.x[:, t, :],
                                                          op0=ALU.mult, op1=ALU.add)
                last.then_inc(scaled, 1)
                dve.wait_ge(scaled, g + 1)
                o = T.x[:, TPG * g:TPG * (g + 1), :]
                nc.vector.tensor_tensor(o, o, own[g % 2][:, :, :], ALU.add).then_inc(added, 1)


def split_heads(nc, T):
    NQK = NHEAD + NKV
    with Phase(nc, "heads") as ph:
        wqk = ph.sb("wqk", [P, NQK, 2, P])
        wv = ph.sb("wv", [P, NKV * HD])
        cos = [ph.sb(f"cos{i}", [P, G]) for i in range(2)]
        sin = [ph.sb(f"sin{i}", [P, G]) for i in range(2)]
        rc = [ph.sb(f"rc{i}", [P, G]) for i in range(2)]
        rs = [ph.sb(f"rs{i}", [P, G]) for i in range(2)]
        q = [ph.sb(f"q{i}", [P, G]) for i in range(2)]
        p1 = [ph.sb(f"p1{i}", [P, G], BF16) for i in range(2)]
        r1 = [ph.sb(f"r1{i}", [P, G]) for i in range(2)]
        p2 = [ph.sb(f"p2{i}", [P, G], BF16) for i in range(2)]
        plain = [ph.ps(f"plain{i}", [P, G]) for i in range(2)]
        turned = [ph.ps(f"turned{i}", [P, G]) for i in range(2)]
        vp = [ph.ps(f"vp{i}", [P, TPG, NKV * HD]) for i in range(2)]
        loaded, tables = ph.sem("loaded"), [ph.sem("tables0"), ph.sem("tables1")]
        projected, turned_by, q_ready = ph.sem("projected"), ph.sem("turned_by"), ph.sem("q_ready")
        p1_ready, r1_ready, p2_ready = (ph.sem(n) for n in ("p1_ready", "r1_ready", "p2_ready"))
        stacked_a, stacked_b, first_placed = ph.sem("stacked_a"), ph.sem("stacked_b"), ph.sem("first_placed")
        v_ready, v_stored, ones_ready = ph.sem("v_ready"), ph.sem("v_stored"), ph.sem("ones_ready")
        block = ph.block()
        units = [(g, h) for g in range(NG) for h in range(NQK)]

        def stacks(h):
            return (T.qa[h], T.qb[h]) if h < NHEAD else (T.ka[h - NHEAD], T.kb[h - NHEAD])

        @block.sync
        def _(sp):
            sp.dma_start(wqk[:, :, :, :], T.D["wqk"].rearrange("c (h r m) -> c h r m", h=NQK, r=2)).then_inc(loaded, 16)
            sp.dma_start(wv[:, :], T.D["wv"]).then_inc(loaded, 16)
            for g in range(NG):
                if g >= 2:
                    sp.wait_ge(turned_by, NQK * (g - 1))
                for quad in range(4):
                    rows = slice(quad * HD, (quad + 1) * HD)
                    sp.dma_start(cos[g % 2][rows, :], T.D["cos"][:, g * G:(g + 1) * G]).then_inc(tables[g % 2], 16)
                    sp.dma_start(sin[g % 2][rows, :], T.D["sin"][:, g * G:(g + 1) * G]).then_inc(tables[g % 2], 16)

        @block.tensor
        def _(pe):
            pe.wait_ge(loaded, 32)
            for n, (g, h) in enumerate(units):
                if n >= 2:
                    pe.wait_ge(turned_by, n - 1)
                x = T.xn_t[:, g * G:(g + 1) * G]
                nc.tensor.matmul(plain[n % 2][:, :], wqk[:, h, 0, :], x, start=True, stop=True)
                nc.tensor.matmul(turned[n % 2][:, :], wqk[:, h, 1, :], x, start=True, stop=True).then_inc(projected, 1)
            for g in range(NG):
                if g >= 2:
                    pe.wait_ge(v_stored, g - 1)
                for k in range(TPG):
                    t = TPG * g + k
                    last = nc.tensor.matmul(vp[g % 2][:, k, :], T.xn_t[:, t * P:(t + 1) * P], wv[:, :],
                                            start=True, stop=True)
                last.then_inc(v_ready, 1)

        @block.vector
        def _(dve):
            for kv in range(NKV):
                nc.vector.memset(T.kb[kv][2 * HD:2 * HD + 2, :], 1.0)
            for n, (g, h) in enumerate(units):
                b = n % 2
                if h == 0:
                    dve.wait_ge(tables[g % 2], (g // 2 + 1) * 8 * 16)
                dve.wait_ge(projected, n + 1)
                if n >= 2:
                    dve.wait_ge(q_ready, n - 1)
                nc.vector.tensor_tensor(rc[b][:, :], plain[b][:, :], cos[g % 2][:, :], ALU.mult)
                nc.vector.tensor_tensor(rs[b][:, :], turned[b][:, :], sin[g % 2][:, :], ALU.mult).then_inc(turned_by, 1)
                if n >= 1:
                    m = n - 1
                    dve.wait_ge(p1_ready, m + 1)
                    if m >= 2:
                        dve.wait_ge(stacked_b, m - 1)
                    nc.vector.tensor_tensor(r1[m % 2][:, :], q[m % 2][:, :], p1[m % 2][:, :],
                                            ALU.subtract).then_inc(r1_ready, 1)
            m = len(units) - 1
            dve.wait_ge(p1_ready, m + 1)
            dve.wait_ge(stacked_b, m - 1)
            nc.vector.tensor_tensor(r1[m % 2][:, :], q[m % 2][:, :], p1[m % 2][:, :],
                                    ALU.subtract).then_inc(r1_ready, 1)
            for g in range(NG):
                dve.wait_ge(v_ready, g + 1)
                nc.vector.tensor_copy(T.v[:, TPG * g:TPG * (g + 1), :, 0:HD],
                                      vp[g % 2][:, :, :].rearrange("p t (k d) -> p t k d", k=NKV)).then_inc(v_stored, 1)

        @block.scalar
        def _(act):
            for n, (g, h) in enumerate(units):
                b, c = n % 2, slice(g * G, (g + 1) * G)
                act.wait_ge(q_ready, n + 1)
                if n >= 2:
                    act.wait_ge(stacked_b, n - 1)
                nc.scalar.copy(p1[b][:, :], q[b][:, :]).then_inc(p1_ready, 1)
                act.wait_ge(r1_ready, n + 1)
                nc.scalar.copy(p2[b][:, :], r1[b][:, :]).then_inc(p2_ready, 1)
                act.wait_ge(p1_ready, n + 1)
                act.wait_ge(p2_ready, n + 1)
                sa, _ = stacks(h)
                for quad in range(4):
                    part = p2 if (quad >= 2 if h < NHEAD else quad % 2) else p1
                    rows = slice(quad * HD, (quad + 1) * HD)
                    last = nc.scalar.copy(sa[rows, c], part[b][rows, :])
                last.then_inc(stacked_a, 1)

        @block.gpsimd
        def _(pool):
            nc.gpsimd.memset(T.v[:, :, :, HD:HD + 1], 1.0).then_inc(ones_ready, 1)
            pool.wait_ge(ones_ready, 1)
            for n, (g, h) in enumerate(units):
                b, c = n % 2, slice(g * G, (g + 1) * G)
                pool.wait_ge(turned_by, n + 1)
                if n >= 2:
                    pool.wait_ge(r1_ready, n - 1)
                nc.gpsimd.tensor_tensor(q[b][:, :], rc[b][:, :], rs[b][:, :], ALU.add).then_inc(q_ready, 1)
                pool.wait_ge(p2_ready, n + 1)
                _, sb_ = stacks(h)
                lo, hi = slice(0, HD), slice(HD, 2 * HD)
                first, third = (lo, hi) if h < NHEAD else (hi, lo)
                pool.wait_ge(q_ready, n + 1)
                nc.gpsimd.tensor_copy(sb_[first, c], p1[b][first, :]).then_inc(first_placed, 1)
                pool.wait_ge(first_placed, n + 1)
                nc.gpsimd.tensor_tensor(sb_[third, c], r1[b][third, :], p2[b][third, :],
                                        ALU.subtract).then_inc(stacked_b, 1)
                pool.wait_ge(stacked_b, n + 1)


def row_maxima(nc, T):
    with Phase(nc, "maxima") as ph:
        sc = [ph.ps(f"sc{i}", [P, 2, G]) for i in range(3)]
        flat = ph.ps("flat", [2, NHEAD, G], BF16)
        part = ph.sb("part", [P, 2, NHEAD, NG // 2])
        neg = ph.sb("neg", [P, 2, NHEAD])
        halves = ph.sb("halves", [P, TPG, NHEAD, 2], BF16)
        scored, reduced, neg_ready = ph.sem("scored"), ph.sem("reduced"), ph.sem("neg_ready")
        high_ready, halves_ready = ph.sem("high_ready"), ph.sem("halves_ready")
        flat_ready, placed = ph.sem("flat_ready"), ph.sem("placed")
        block = ph.block()

        def pairs(g):
            return g // 2 + 1

        def before(g):
            return sum(TPG * NHEAD * pairs(k) for k in range(g))

        @block.tensor
        def _(pe):
            lead(pe, scored)
            for g in range(NG):
                with pe.Fori(0, 2) as two:
                    for half in range(2):
                        for h in range(NHEAD):
                            for c in range(pairs(g)):
                                u = (half * NHEAD + h) * pairs(g) + c
                                at = before(g) + two * (2 * NHEAD * pairs(g)) + u
                                q = (g * TPG + two * 2 + half) * P
                                pe.wait_ge(reduced, LEAD + at - 2)
                                if u < 3:
                                    pe.wait_ge(reduced, LEAD + at - u)
                                for k in range(min(2, g + 1 - 2 * c)):
                                    s = 2 * c + k
                                    o = sc[u % 3][:, k, :]
                                    keys = slice(s * G, (s + 1) * G)
                                    nc.tensor.matmul(o, T.qa[h][:, bass.ds(q, P)], T.ka[h // 2][:, keys],
                                                     start=True, stop=False)
                                    last = nc.tensor.matmul(o, T.qb[h][0:2 * HD, bass.ds(q, P)],
                                                            T.kb[h // 2][0:2 * HD, keys], start=False, stop=(s != g))
                                    if s == g:
                                        last = nc.tensor.matmul(o, T.ident16[:, :],
                                                                T.future_keys[:, bass.ds(two * 2 + half, 1), :]
                                                                .rearrange("p a s -> p (a s)"),
                                                                start=False, stop=True)
                                last.then_inc(scored, 1)
                pe.wait_ge(halves_ready, TPG * (g + 1))
                if g >= 1:
                    pe.wait_ge(placed, g)
                for h in range(NHEAD):
                    for k in range(TPG):
                        last = nc.tensor.transpose(flat[:, h, k * P:(k + 1) * P], halves[:, k, h, :], T.ident16[:, :])
                last.then_inc(flat_ready, 1)

        @block.vector
        def _(dve):
            lead(dve, reduced)
            for g in range(NG):
                with dve.Fori(0, 2) as two:
                    for half in range(2):
                        for h in range(NHEAD):
                            for c in range(pairs(g)):
                                u = (half * NHEAD + h) * pairs(g) + c
                                at = before(g) + two * (2 * NHEAD * pairs(g)) + u
                                w = min(2, g + 1 - 2 * c)
                                dve.wait_ge(scored, LEAD + at + 1)
                                nc.vector.reduce_max(part[:, half, h, c:c + 1],
                                                     sc[u % 3][:, 0:w, :].rearrange("p a s -> p (a s)"),
                                                     AX.X).then_inc(reduced, 1)
                        done = before(g) + (two * 2 + half + 1) * (NHEAD * pairs(g))
                        tile = two * 2 + half
                        dve.wait_ge(reduced, LEAD + done)
                        nc.vector.tensor_reduce(neg[:, half, :], part[:, half, :, 0:pairs(g)], AX.X, ALU.max,
                                                negate=True).then_inc(neg_ready, 1)
                        dve.wait_ge(neg_ready, g * TPG + tile + 1)
                        dve.wait_ge(flat_ready, g) if g else None
                        nc.vector.tensor_copy(halves[:, bass.ds(tile, 1), :, 0].rearrange("p a h -> p (a h)"),
                                              neg[:, half, :]).then_inc(high_ready, 1)
                        dve.wait_ge(high_ready, g * TPG + tile + 1)
                        nc.vector.tensor_tensor(halves[:, bass.ds(tile, 1), :, 1].rearrange("p a h -> p (a h)"),
                                                neg[:, half, :],
                                                halves[:, bass.ds(tile, 1), :, 0].rearrange("p a h -> p (a h)"),
                                                ALU.subtract).then_inc(halves_ready, 1)

        @block.scalar
        def _(act):
            for g in range(NG):
                act.wait_ge(flat_ready, g + 1)
                for h in range(NHEAD):
                    last = nc.scalar.copy(T.qb[h][2 * HD:2 * HD + 2, g * G:(g + 1) * G], flat[:, h, :])
                last.then_inc(placed, 1)


def attend(nc, T):
    with Phase(nc, "attend") as ph:
        sc = [ph.ps(f"sc{i}", [P, 2, G]) for i in range(2)]
        heads = [ph.ps(f"heads{h}", [HD + 1, G]) for h in range(NHEAD)]
        probs = [ph.sb(f"probs{i}", [P, 2, G]) for i in range(2)]
        vt = [ph.sb(f"vt{i}", [P, 2, NKV, HD + 1]) for i in range(2)]
        ot = ph.sb("ot", [HD + 1, NHEAD, G])
        wo = ph.sb("wo", [HD + 1, NHEAD, P + 1])
        inv = ph.sb("inv", [P, 2, NHEAD])
        loaded, wo_zeroed, wo_one = ph.sem("loaded"), ph.sem("wo_zeroed"), ph.sem("wo_one")
        scored, exps_ready, multiplied = ph.sem("scored"), ph.sem("exps_ready"), ph.sem("multiplied")
        v_copied, heads_out, projected = ph.sem("v_copied"), ph.sem("heads_out"), ph.sem("projected")
        inv_ready, head_added, added = ph.sem("inv_ready"), ph.sem("head_added"), ph.sem("added")
        block = ph.block()
        UP = 2 * NHEAD

        def before(g):
            return sum(UP * (k + 1) for k in range(g))

        @block.sync
        def _(sp):
            sp.wait_ge(wo_zeroed, 1)
            sp.dma_start(wo[0:HD, :, 0:P], T.D["wo"].rearrange("(h d) o -> d h o", d=HD)).then_inc(loaded, 16)

        @block.tensor
        def _(pe):
            lead(pe, multiplied, scored)
            pe.wait_ge(loaded, 16)
            pe.wait_ge(wo_one, 1)

            def score(g, at, u, tile, diag):
                pr, h = divmod(u, NHEAD)
                pe.wait_ge(exps_ready, LEAD + at - 1)
                for k in range(2):
                    o = sc[u % 2][:, k, :]
                    st = (tile + 2 * pr + k) * P
                    keys = bass.ds(st, P)
                    qs = slice(g * G, (g + 1) * G)
                    nc.tensor.matmul(o, T.ka[h // 2][:, keys], T.qa[h][:, qs], start=True, stop=False)
                    last = nc.tensor.matmul(o, T.kb[h // 2][0:2 * HD + 2, keys], T.qb[h][0:2 * HD + 2, qs],
                                            start=False, stop=not diag)
                    if diag:
                        last = nc.tensor.matmul(o, T.ident16[:, :], T.past_queries[:, 2 * pr + k, :],
                                                start=False, stop=True)
                last.then_inc(scored, 1)

            def two_pairs(g, at0, tile, diag, pairs0):
                for u in range(UP + 1):
                    if u < UP:
                        score(g, at0 + u, u, tile, diag)
                    if u >= 1:
                        v = u - 1
                        pr, h = divmod(v, NHEAD)
                        pe.wait_ge(exps_ready, LEAD + at0 + v + 1)
                        if h == 0:
                            pe.wait_ge(v_copied, LEAD + pairs0 + pr + 1)
                        for k in range(2):
                            last = nc.tensor.matmul(heads[h][:, :], vt[pr][:, k, h // 2, :], probs[v % 2][:, k, :],
                                                    start=(diag and pr == 0 and k == 0), stop=True,
                                                    skip_group_check=True)
                        last.then_inc(multiplied, 1)

            for g in range(NG):
                if g >= 1:
                    pe.wait_ge(heads_out, g)
                    pe.wait_ge(added, TPG * g)
                two_pairs(g, before(g), g * TPG, True, before(g) // NHEAD)
                if g >= 1:
                    with pe.Fori(0, g) as it:
                        two_pairs(g, before(g) + UP + it * UP, it * TPG, False, before(g) // NHEAD + 2 + it * 2)
                pe.wait_ge(heads_out, g + 1)
                for k in range(TPG):
                    if k >= 2:
                        pe.wait_ge(added, TPG * g + k - 1)
                    for h in range(NHEAD):
                        o = sc[k % 2][:, h // 2, (h % 2) * (P + 1):(h % 2 + 1) * (P + 1)]
                        last = nc.tensor.matmul(o, ot[:, h, k * P:(k + 1) * P], wo[:, h, :], start=True, stop=True)
                    last.then_inc(projected, 1)

        @block.scalar
        def _(act):
            lead(act, exps_ready)

            def exps(at0):
                for u in range(UP):
                    act.wait_ge(scored, LEAD + at0 + u + 1)
                    act.wait_ge(multiplied, LEAD + at0 + u - 1)
                    nc.scalar.activation(probs[u % 2][:, :, :], sc[u % 2][:, :, :], ACT.Exp,
                                         scale=float(1.0 / np.sqrt(np.float32(HD)))).then_inc(exps_ready, 1)

            for g in range(NG):
                exps(before(g))
                if g >= 1:
                    with act.Fori(0, g) as it:
                        exps(before(g) + UP + it * UP)

        @block.gpsimd
        def _(pool):
            lead(pool, v_copied)
            nc.gpsimd.memset(wo[:, :, :], 0.0).then_inc(wo_zeroed, 1)
            pool.wait_ge(wo_zeroed, 1)
            nc.gpsimd.memset(wo[HD:HD + 1, :, P:P + 1], 1.0).then_inc(wo_one, 1)
            pool.wait_ge(wo_one, 1)

            def copies(at0, tile, first=False):
                for pr in range(2):
                    if not (first and pr == 0):
                        pool.wait_ge(multiplied, LEAD + at0 + NHEAD * (pr - 1))
                    nc.gpsimd.tensor_copy(vt[pr][:, :, :, :], T.v[:, bass.ds(tile + 2 * pr, 2), :, :]
                                          ).then_inc(v_copied, 1)

            for g in range(NG):
                copies(before(g), g * TPG, g == 0)
                if g >= 1:
                    with pool.Fori(0, g) as it:
                        copies(before(g) + UP + it * UP, it * TPG)

        @block.vector
        def _(dve):
            for g in range(NG):
                dve.wait_ge(multiplied, LEAD + before(g + 1))
                if g >= 1:
                    dve.wait_ge(projected, TPG * g)
                for h in range(NHEAD):
                    last = nc.vector.tensor_copy(ot[:, h, :], heads[h][:, :])
                last.then_inc(heads_out, 1)
                for k in range(TPG):
                    t = TPG * g + k
                    dve.wait_ge(projected, t + 1)
                    s2 = sc[k % 2][:, :, 0:2 * (P + 1)].rearrange("p a (b c) -> p a b c", b=2)
                    if t >= 2:
                        dve.wait_ge(added, t - 1)
                    nc.vector.reciprocal(inv[:, k % 2, :].rearrange("p (a b) -> p a b", a=2),
                                         s2[:, :, :, P]).then_inc(inv_ready, 1)
                    dve.wait_ge(inv_ready, t + 1)
                    for h in range(NHEAD):
                        ins = nc.vector.scalar_tensor_tensor(out=T.xn[:, t, :], in0=s2[:, h // 2, h % 2, 0:P],
                                                             scalar=inv[:, k % 2, h:h + 1], in1=T.xn[:, t, :],
                                                             op0=ALU.mult, op1=ALU.add)
                        if h < NHEAD - 1:
                            ins.then_inc(head_added, 1)
                            dve.wait_ge(head_added, (NHEAD - 1) * t + h + 1)
                    ins.then_inc(added, 1)


def route(nc, T):
    with Phase(nc, "route") as ph:
        rw = ph.sb("rw", [P, NE])
        e = ph.sb("e", [P, NT, NE])
        neg = ph.sb("neg", [P, NT])
        logits = ph.sb("logits", [P, NT, NE])
        top = ph.sb("top", [P, NT, 8])
        idx = ph.sb("idx", [P, NT, 8], mybir.dt.uint32)
        best = ph.sb("best", [P, 2, NT])
        number = ph.sb("number", [P, NE])
        s1 = ph.sb("s1", [P, NT])
        hot = ph.sb("hot", [P, 2, NT, NE])
        lp = ph.ps("lp", [P, NT, NE])
        back = [ph.ps(f"back{i}", [NE, G]) for i in range(2)]
        loaded, multiplied, neg_ready, exps_ready = (ph.sem(n) for n in ("loaded", "multiplied", "neg_ready", "exps_ready"))
        route_zeroed = ph.sem("route_zeroed")
        weights_ready, transposed, copied, chain = (ph.sem(n) for n in ("weights_ready", "transposed", "copied", "chain"))
        block = ph.block()

        @block.sync
        def _(sp):
            sp.dma_start(rw[:, :], T.D["router_w"]).then_inc(loaded, 16)

        @block.tensor
        def _(pe):
            pe.wait_ge(loaded, 16)
            for t in range(NT):
                last = nc.tensor.matmul(lp[:, t, :], T.xn_t[:, t * P:(t + 1) * P], rw[:, :], start=True, stop=True)
            last.then_inc(multiplied, 1)
            pe.wait_ge(weights_ready, 1)
            for g in range(NG):
                if g >= 2:
                    pe.wait_ge(copied, g - 1)
                for k in range(TPG):
                    last = nc.tensor.transpose(back[g % 2][:, k * P:(k + 1) * P], hot[:, 0, TPG * g + k, :],
                                               T.ident[:, :])
                last.then_inc(transposed, 1)

        @block.scalar
        def _(act):
            act.wait_ge(neg_ready, 1)
            for t in range(NT):
                last = nc.scalar.activation(e[:, t, :], logits[:, t, :], ACT.Exp, bias=neg[:, t:t + 1])
            last.then_inc(exps_ready, 1)
            for g in range(NG):
                act.wait_ge(transposed, g + 1)
                act.wait_ge(route_zeroed, 1)
                nc.scalar.copy(T.route_t[0:NE, g * G:(g + 1) * G], back[g % 2][:, :]).then_inc(copied, 1)

        @block.vector
        def _(dve):
            s = Steps(dve, chain)
            nc.vector.memset(T.route_t[:, :], 0.0).then_inc(route_zeroed, 1)
            wide = lambda ap: ap.rearrange("p (t o) -> p t o", o=1).broadcast_to([P, NT, NE])
            for n in range(NE):
                s.mark(nc.vector.memset(number[:, n:n + 1], float(n)))
            dve.wait_ge(multiplied, 1)
            s.done(nc.vector.tensor_copy(logits[:, :, :], lp[:, :, :]))
            nc.vector.tensor_reduce(neg[:, :], logits[:, :, :], AX.X, ALU.max, negate=True).then_inc(neg_ready, 1)
            dve.wait_ge(exps_ready, 1)
            s.done(nc.vector.tensor_reduce(s1[:, :], e[:, :, :], AX.X, ALU.add))
            s.done(nc.vector.reciprocal(s1[:, :], s1[:, :]))
            s.done(nc.vector.tensor_tensor(e[:, :, :], e[:, :, :], wide(s1[:, :]), ALU.mult))
            for t in range(NT):
                s.mark(nc.vector.max(top[:, t, :], e[:, t, :]))
            s.sync()
            for t in range(NT):
                s.mark(nc.vector.max_index(idx[:, t, :], top[:, t, :], e[:, t, :]))
            s.mark(nc.vector.tensor_tensor(s1[:, :], top[:, :, 0], top[:, :, 1], ALU.add))
            s.sync()
            s.done(nc.vector.tensor_scalar(s1[:, :], s1[:, :], 1e-9, None, ALU.add))
            s.done(nc.vector.reciprocal(s1[:, :], s1[:, :]))
            for j in range(2):
                s.mark(nc.vector.tensor_copy(best[:, j, :], idx[:, :, j]))
            s.mark(nc.vector.tensor_tensor(top[:, :, 0:2], top[:, :, 0:2],
                                           s1[:, :].rearrange("p (t o) -> p t o", o=1).broadcast_to([P, NT, 2]),
                                           ALU.mult))
            s.sync()
            for j in range(2):
                s.done(nc.vector.tensor_tensor(hot[:, j, :, :],
                                               number[:, :].rearrange("p (o n) -> p o n", o=1).broadcast_to([P, NT, NE]),
                                               wide(best[:, j, :]), ALU.is_equal))
                s.done(nc.vector.tensor_tensor(hot[:, j, :, :], hot[:, j, :, :],
                                               top[:, :, j:j + 1].broadcast_to([P, NT, NE]), ALU.mult))
            nc.vector.tensor_tensor(hot[:, 0, :, :], hot[:, 0, :, :], hot[:, 1, :, :],
                                    ALU.add).then_inc(weights_ready, 1)


def experts(nc, T, out):
    NC = len(HCH)
    with Phase(nc, "experts") as ph:
        w1, w3 = (ph.sb(n, [P, NE, HID]) for n in ("w1", "w3"))
        w2 = ph.sb("w2", [P, NE, NC, P])
        sel = ph.sb("sel", [P, NE, P])
        zero = ph.sb("zero", [P, G])
        up = [[ph.ps(f"up{i}{j}", [P, G]) for j in range(2)] for i in range(2)]
        down = [ph.ps(f"down{i}", [P, G]) for i in range(2)]
        spread = ph.ps("spread", [P, G])
        back = ph.ps("back", [P, TPG, P])
        act_out = [ph.sb(f"silu{i}", [P, G]) for i in range(2)]
        hidden = [ph.sb(f"hidden{i}", [P, G]) for i in range(2 * NC)]
        weight = [ph.sb(f"weight{i}", [P, G]) for i in range(2)]
        scaled = [ph.sb(f"scaled{i}", [P, G]) for i in range(2)]
        total = [ph.sb(f"total{i}", [P, G]) for i in range(2)]
        loaded, sel_ready = ph.sem("loaded"), ph.sem("sel_ready")
        upped, silu_ready, hidden_ready = ph.sem("upped"), ph.sem("silu_ready"), ph.sem("hidden_ready")
        downed, spread_ready, weight_ready = ph.sem("downed"), ph.sem("spread_ready"), ph.sem("weight_ready")
        scaled_ready, total_ready, back_ready, added = (ph.sem(n) for n in ("scaled_ready", "total_ready", "back_ready", "added"))
        stored, summed, zeroed = ph.sem("stored"), ph.sem("summed"), ph.sem("zeroed")
        block = ph.block()

        @block.sync
        def _(sp):
            sp.dma_start(w1[:, :, :], T.D["w1"].rearrange("e c h -> c e h")).then_inc(loaded, 16)
            sp.dma_start(w3[:, :, :], T.D["w3"].rearrange("e c h -> c e h")).then_inc(loaded, 16)
            for c, (h0, hn) in enumerate(HCH):
                sp.dma_start(w2[0:hn, :, c, :], T.D["w2"][:, h0:h0 + hn, :].rearrange("e h c -> h e c")).then_inc(loaded, 16)
            with sp.Fori(0, NG) as g:
                sp.wait_ge(added, LEAD + g + 1)
                sp.dma_start(out[bass.ds(g * G, G), :].rearrange("(t p) c -> p t c", p=P),
                             T.x[:, bass.ds(g * TPG, TPG), :]).then_inc(stored, 16)
            sp.wait_ge(stored, 16 * NG)

        @block.tensor
        def _(pe):
            lead(pe, upped, downed, back_ready)
            pe.wait_ge(loaded, 16 * (2 + NC))
            pe.wait_ge(sel_ready, 2)

            def ups(g, e):
                x = T.xn_t[:, bass.ds(g * G, G)]
                pe.wait_ge(weight_ready, LEAD + g * NE + e)
                nc.tensor.matmul(spread[:, :], sel[:, e, :], T.route_t[:, bass.ds(g * G, G)],
                                 start=True, stop=True).then_inc(spread_ready, 1)
                for c, (h0, hn) in enumerate(HCH):
                    u = NC * e + c
                    pe.wait_ge(hidden_ready, LEAD + g * (NE * NC) + u - 1)
                    for j, w in enumerate((w1, w3)):
                        last = nc.tensor.matmul(up[u % 2][j][0:hn, :], w[:, e, h0:h0 + hn], x, start=True, stop=True)
                    last.then_inc(upped, 1)

            def downs(g, e):
                pe.wait_ge(scaled_ready, LEAD + g * NE + e - 1)
                for c, (h0, hn) in enumerate(HCH):
                    pe.wait_ge(hidden_ready, LEAD + g * (NE * NC) + NC * e + c + 1)
                    last = nc.tensor.matmul(down[e % 2][:, :], w2[0:hn, e, c, :], hidden[(e % 2) * NC + c][0:hn, :],
                                            start=(c == 0), stop=(c == NC - 1))
                last.then_inc(downed, 1)

            with pe.Fori(0, NG) as g:
                for e in range(NE):
                    ups(g, e)
                    if e >= 1:
                        downs(g, e - 1)
                downs(g, NE - 1)
                pe.wait_ge(total_ready, LEAD + (g + 1) * NE)
                pe.wait_ge(added, LEAD + g)
                for k in range(TPG):
                    last = nc.tensor.transpose(back[:, k, :], total[(NE - 1) % 2][:, k * P:(k + 1) * P], T.ident[:, :])
                last.then_inc(back_ready, 1)

        @block.scalar
        def _(act):
            lead(act, weight_ready, silu_ready)
            with act.Fori(0, NG) as g:
                for e in range(NE):
                    act.wait_ge(spread_ready, g * NE + e + 1)
                    act.wait_ge(scaled_ready, LEAD + g * NE + e - 1)
                    nc.scalar.copy(weight[e % 2][:, :], spread[:, :]).then_inc(weight_ready, 1)
                    for c, (h0, hn) in enumerate(HCH):
                        u = NC * e + c
                        act.wait_ge(upped, LEAD + g * (NE * NC) + u + 1)
                        act.wait_ge(hidden_ready, LEAD + g * (NE * NC) + u - 1)
                        nc.scalar.activation(act_out[u % 2][0:hn, :], up[u % 2][0][0:hn, :],
                                             ACT.Silu).then_inc(silu_ready, 1)

        @block.vector
        def _(dve):
            lead(dve, hidden_ready, scaled_ready, added)
            nc.vector.memset(zero[:, :], 0.0).then_inc(zeroed, 1)
            with dve.Fori(0, NG) as g:
                def scale(e):
                    dve.wait_ge(downed, LEAD + g * NE + e + 1)
                    dve.wait_ge(weight_ready, LEAD + g * NE + e + 1)
                    dve.wait_ge(total_ready, LEAD + g * NE + e - 1)
                    nc.vector.tensor_tensor(scaled[e % 2][:, :], down[e % 2][:, :], weight[e % 2][:, :],
                                            ALU.mult).then_inc(scaled_ready, 1)

                for e in range(NE):
                    for c, (h0, hn) in enumerate(HCH):
                        u = NC * e + c
                        dve.wait_ge(silu_ready, LEAD + g * (NE * NC) + u + 1)
                        dve.wait_ge(downed, LEAD + g * NE + e - 1)
                        nc.vector.tensor_tensor(hidden[(e % 2) * NC + c][0:hn, :], act_out[u % 2][0:hn, :],
                                                up[u % 2][1][0:hn, :], ALU.mult).then_inc(hidden_ready, 1)
                    if e >= 1:
                        scale(e - 1)
                scale(NE - 1)
                o = T.x[:, bass.ds(g * TPG, TPG), :].rearrange("p t c -> p (t c)")
                n = T.xn[:, bass.ds(g * TPG, TPG), :].rearrange("p t c -> p (t c)")
                nc.vector.tensor_tensor(o, o, n, ALU.add).then_inc(summed, 1)
                dve.wait_ge(summed, g + 1)
                dve.wait_ge(back_ready, LEAD + g + 1)
                nc.vector.tensor_tensor(o, o, back[:, :, :].rearrange("p t c -> p (t c)"), ALU.add).then_inc(added, 1)

        @block.gpsimd
        def _(pool):
            lead(pool, total_ready)
            pool.wait_ge(zeroed, 1)
            nc.gpsimd.memset(sel[:, :, :], 0.0).then_inc(sel_ready, 1)
            pool.wait_ge(sel_ready, 1)
            nc.gpsimd.affine_select(out=sel[:, :, :], in_=sel[:, :, :], compare_op=ALU.not_equal, fill=1.0, base=0,
                                    pattern=[[-1, NE], [0, P]], channel_multiplier=1).then_inc(sel_ready, 1)
            with pool.Fori(0, NG) as g:
                pool.wait_ge(back_ready, LEAD + g)
                for e in range(NE):
                    pool.wait_ge(scaled_ready, LEAD + g * NE + e + 1)
                    if e == 0:
                        nc.gpsimd.tensor_tensor(total[0][:, :], zero[:, :], scaled[0][:, :],
                                                ALU.add).then_inc(total_ready, 1)
                    else:
                        pool.wait_ge(total_ready, LEAD + g * NE + e)
                        nc.gpsimd.tensor_tensor(total[e % 2][:, :], total[(e - 1) % 2][:, :], scaled[e % 2][:, :],
                                                ALU.add).then_inc(total_ready, 1)


def make_masks(nc, T):
    with Phase(nc, "masks") as ph:
        made = ph.sem("made")
        block = ph.block()

        @block.gpsimd
        def _(pool):
            nc.gpsimd.memset(T.ident16[:, :], 0.0).then_inc(made, 1)
            nc.gpsimd.memset(T.future_keys[:, :, :], 0.0).then_inc(made, 1)
            nc.gpsimd.memset(T.past_queries[:, :, :], 0.0).then_inc(made, 1)
            pool.wait_ge(made, 3)
            nc.gpsimd.affine_select(out=T.ident16[:, :], in_=T.ident16[:, :], compare_op=ALU.not_equal, fill=1.0,
                                    base=0, pattern=[[-1, P]], channel_multiplier=1)
            nc.gpsimd.affine_select(out=T.future_keys[:, :, :], in_=T.future_keys[:, :, :], compare_op=ALU.is_ge,
                                    fill=-1e30, base=0, pattern=[[P, TPG], [-1, G]], channel_multiplier=1)
            nc.gpsimd.affine_select(out=T.past_queries[:, :, :], in_=T.past_queries[:, :, :], compare_op=ALU.is_ge,
                                    fill=-1e30, base=0, pattern=[[-P, TPG], [1, G]], channel_multiplier=-1)


class Tensors:
    pass


def program(nc, D, out):
    T = Tensors()
    Phase.used.clear()
    with ExitStack() as ctx:
        def sb(name, shape, dt=F32):
            return ctx.enter_context(nc.sbuf_tensor(name, shape, dt))

        T.x = sb("x", [P, NT, P])
        T.xn = sb("xn", [P, NT, P])
        T.xn_t = sb("xn_t", [P, N + CHUNK])
        T.ident = sb("ident", [P, P])
        T.ones = sb("ones", [P, P])
        T.tiny = sb("tiny", [P, 1])
        T.D = D
        with ExitStack() as first:
            ctx_first = first.enter_context
            T.gnn_w = ctx_first(nc.sbuf_tensor("gnn_w", [P, P], F32))
            T.gnn_b = ctx_first(nc.sbuf_tensor("gnn_b", [P, P], F32))
            T.wih = ctx_first(nc.sbuf_tensor("wih", [P, 4 * P], F32))
            T.whh = ctx_first(nc.sbuf_tensor("whh", [P, 4 * P], F32))
            T.bias_rows = ctx_first(nc.sbuf_tensor("bias_rows", [P, 2, 4 * P], F32))
            T.msg = ctx_first(nc.sbuf_tensor("msg", [P, NT, P], F32))
            load_constants(nc, T, D)
            normalise(nc, "norm0", T, T.x, T.xn, T.xn_t)
            project_rows(nc, "message", T.xn_t, T.gnn_w, T.msg, T.gnn_b)
            graph_product(nc, "gnn0", T, D["adj"], T.msg, T.x, True, groups=1)
            normalise(nc, "norm1", T, T.x, T.xn, T.xn_t, tiles=TPG)
            T.hid_t = ctx_first(nc.sbuf_tensor("hid_t", [P, N], F32))
            lstm(nc, T)
            add_sequence_sums(nc, T)
        
        with ExitStack() as second:
            def sb2(name, shape, dt=F32):
                return second.enter_context(nc.sbuf_tensor(name, shape, dt))

            T.h = sb2("h", [P, NT, P])
            T.agg_t = sb2("agg_t", [P, N])
            T.deg = sb2("deg", [P, NT])
            T.neigh_w = sb2("neigh_w", [P, P])
            load(nc, "neigh", (T.neigh_w[:, :], D["neigh_w"]))
            normalise(nc, "norm2", T, T.x, T.xn, T.xn_t)
            project_rows(nc, "neigh", T.xn_t, T.neigh_w, T.h)
            graph_product(nc, "gnn1", T, D["adj"], T.h, T.agg_t, False, T.deg)
            combine_neighbours(nc, T)
        
        clear_semaphores(nc)
        normalise(nc, "norm3", T, T.x, T.xn, None)
        with ExitStack() as third:
            def sb3(name, shape, dt=F32):
                return third.enter_context(nc.sbuf_tensor(name, shape, dt))

            with ExitStack() as fourth:
                T.h1 = fourth.enter_context(nc.sbuf_tensor("h1", [P, NT, P], F32))
                T.ln_w = fourth.enter_context(nc.sbuf_tensor("ln_w", [P, P], F32))
                load(nc, "ln1", (T.ln_w[:, :], D["ln1"].broadcast_to([P, P])))
                normalise(nc, "rms1", T, T.xn, T.h1, T.xn_t, rms_weight=T.ln_w, eps=1e-6)
            T.qa = [sb3(f"qa{h}", [P, N], BF16) for h in range(NHEAD)]
            T.qb = [sb3(f"qb{h}", [P, N], BF16) for h in range(NHEAD)]
            T.ka = [sb3(f"ka{h}", [P, N], BF16) for h in range(NKV)]
            T.kb = [sb3(f"kb{h}", [P, N], BF16) for h in range(NKV)]
            T.v = sb3("v", [P, NT, NKV, HD + 1])
            split_heads(nc, T)
            T.ident16 = sb3("ident16", [P, P], BF16)
            T.future_keys = sb3("future_keys", [P, TPG, G], BF16)
            T.past_queries = sb3("past_queries", [P, TPG, G], BF16)
            make_masks(nc, T)
            row_maxima(nc, T)
            attend(nc, T)
        with ExitStack() as fifth:
            T.route_t = fifth.enter_context(nc.sbuf_tensor("route_t", [P, N], F32))
            with ExitStack() as sixth:
                T.h2 = sixth.enter_context(nc.sbuf_tensor("h2", [P, NT, P], F32))
                T.ln_w = sixth.enter_context(nc.sbuf_tensor("ln_w2", [P, P], F32))
                load(nc, "ln2", (T.ln_w[:, :], D["ln2"].broadcast_to([P, P])))
                normalise(nc, "rms2", T, T.xn, T.h2, T.xn_t, rms_weight=T.ln_w, eps=1e-6)
            route(nc, T)
            experts(nc, T, out)


def rope_tables():
    inv = 1.0 / 10000.0 ** (np.arange(0, HD, 2, dtype=np.float32) / HD)
    freqs = np.outer(np.arange(N, dtype=np.float32), inv)
    emb = np.concatenate([freqs, freqs], axis=-1)
    cos, sin = np.cos(emb).T, np.sin(emb).T
    sign = np.where(np.arange(HD) < HD // 2, -1.0, 1.0).astype(np.float32)[:, None]
    return np.ascontiguousarray(cos), np.ascontiguousarray(sin * sign)


def layouts(inputs):
    a = {k: np.asarray(v) for k, v in inputs.items()}
    t = lambda w: np.ascontiguousarray(np.swapaxes(w, -1, -2))
    row = lambda w: np.ascontiguousarray(w.reshape(1, -1))
    cos, sin = rope_tables()
    heads = np.concatenate([a["L1_ffn_wq"], a["L1_ffn_wk"]]).reshape(NHEAD + NKV, HD, P)
    swapped = np.concatenate([heads[:, HD // 2:], heads[:, :HD // 2]], axis=1)
    wqk = np.stack([np.tile(heads, (1, 4, 1)), np.tile(swapped, (1, 4, 1))], axis=1)
    return {
        "x": a["x"], "adj": a["adj"], "gnn_w": a["L0_gnn_W"], "gnn_b": row(a["L0_gnn_B"]),
        "wih": t(a["L0_ffn_W_ih"]), "whh": t(a["L0_ffn_W_hh"]),
        "b_ih": row(a["L0_ffn_b_ih"]), "b_hh": row(a["L0_ffn_b_hh"]),
        "neigh_w": t(a["L1_gnn_neigh_W"]), "lin_w": t(a["L1_gnn_lin_W"]),
        "w_lin": t(a["L0_ffn_W_lin"]), "b_lin": row(a["L0_ffn_b_lin"]),
        "fw_att": t(a["L0_ffn_fw_att"]), "bw_att": t(a["L0_ffn_bw_att"]),
        "ln1": row(a["L1_ffn_ln1_w"]), "ln2": row(a["L1_ffn_ln2_w"]),
        "wqk": t(wqk.reshape(-1, P)), "wv": t(a["L1_ffn_wv"]), "wo": t(a["L1_ffn_wo"]),
        "cos": cos, "sin": sin, "router_w": t(a["L1_ffn_router_w"]),
        "w1": t(a["L1_ffn_w1"]), "w2": t(a["L1_ffn_w2"]), "w3": t(a["L1_ffn_w3"]),
    }


def kernel(**inputs):
    import concourse.bacc as bacc
    from concourse.bass_utils import run_bass_kernel_spmd as run

    nc = bacc.Bacc("TRN2", target_bir_lowering=False, num_devices=1)
    arrays = layouts(inputs)
    D = {k: nc.dram_tensor(f"in_{k}", v.shape, mybir.dt.from_np(v.dtype), kind="ExternalInput").ap()
         for k, v in arrays.items()}
    out = nc.dram_tensor("out", [N, P], F32, kind="ExternalOutput").ap()
    program(nc, D, out)
    r = run(nc, [{f"in_{k}": v for k, v in arrays.items()}], core_ids=[0])
    return r.results[0]["out"]
```

```python
import concourse.bass as bass
from concourse import mybir
from contextlib import ExitStack
import numpy as np

F32 = mybir.dt.float32
BF16 = mybir.dt.bfloat16
F16 = mybir.dt.float16
I32 = mybir.dt.int32
ACT = mybir.ActivationFunctionType
ALU = mybir.AluOpType
AX = mybir.AxisListType
RMAX = bass.bass_isa.ReduceOp.max

P = 128
N = 4096
NT = N // P
G = 512
NG = N // G
TPG = G // P
NHEAD, NKV, HD = 4, 2, 32
NE, HID = 8, 341
TINY = 1e-12
ROUTE_SCALE = 2.0 ** 12
VW = 3 * HD + 1
SKEW = 2
HCH = [(0, 128), (128, 128), (256, HID - 256)]


class Steps:

    def __init__(self, eng, sem, start=0):
        self.eng, self.sem, self.start, self.n = eng, sem, start, 0

    def mark(self, ins):
        self.n += 1
        ins.then_inc(self.sem, 1)

    def sync(self):
        self.eng.wait_ge(self.sem, self.start + self.n)

    def done(self, ins):
        self.mark(ins)
        self.sync()


class Phase:

    used = []

    def __init__(self, nc, name):
        self.nc, self.name, self.stack = nc, name, ExitStack()

    def __enter__(self):
        self.stack.__enter__()
        return self

    def __exit__(self, *a):
        return self.stack.__exit__(*a)

    def sb(self, name, shape, dt=F32):
        return self.stack.enter_context(self.nc.sbuf_tensor(f"{self.name}_{name}", shape, dt))

    def ps(self, name, shape, dt=F32):
        return self.stack.enter_context(self.nc.psum_tensor(f"{self.name}_{name}", shape, dt))

    def sem(self, name):
        s = self.nc.alloc_semaphore(f"{self.name}_{name}")
        Phase.used.append(s)
        return s

    def block(self):
        return self.stack.enter_context(self.nc.Block())


def clear_semaphores(nc):
    nc.clear_and_free_semaphores(list(Phase.used))
    Phase.used.clear()
    nc.all_engine_barrier()


def load_constants(nc, T, D):
    with Phase(nc, "load") as ph:
        loaded = ph.sem("loaded")
        zeroed = ph.sem("zeroed")
        made = ph.sem("made")
        block = ph.block()

        @block.sync
        def _(sp):
            sp.dma_start(T.x[:, :, :], D["x"].rearrange("(t p) c -> p t c", p=P)).then_inc(loaded, 16)
            sp.dma_start(T.gnn_w[:, :], D["gnn_w"]).then_inc(loaded, 16)
            sp.dma_start(T.gnn_b[:, :], D["gnn_b"].broadcast_to([P, P])).then_inc(loaded, 16)
            sp.dma_start(T.wih[:, :], D["wih"]).then_inc(loaded, 16)
            sp.dma_start(T.whh[:, :], D["whh"]).then_inc(loaded, 16)
            sp.wait_ge(zeroed, 1)
            sp.dma_start(T.bias_rows[0:1, 0, :], D["b_ih"]).then_inc(loaded, 16)
            sp.dma_start(T.bias_rows[0:1, 1, :], D["b_hh"]).then_inc(loaded, 16)
            sp.wait_ge(loaded, 7 * 16)

        @block.vector
        def _(dve):
            nc.vector.memset(T.bias_rows[:, :, :], 0.0).then_inc(zeroed, 1)
            nc.vector.memset(T.ones[:, :], 1.0)
            nc.vector.memset(T.tiny[:, :], TINY)

        @block.gpsimd
        def _(pool):
            nc.gpsimd.memset(T.ident[:, :], 0.0).then_inc(made, 1)
            pool.wait_ge(made, 1)
            nc.gpsimd.affine_select(out=T.ident[:, :], in_=T.ident[:, :], compare_op=ALU.not_equal, fill=1.0,
                                    base=0, pattern=[[-1, P]], channel_multiplier=1).then_inc(made, 1)


def normalise(nc, name, T, src, dst, dst_t, rms_weight=None, eps=1e-5, tiles=NT):
    with Phase(nc, name) as ph:
        stats = ph.sb("stats", [P, tiles, 6])
        mv = ph.sb("mv", [P, tiles, 2])
        var = ph.sb("var", [P, tiles])
        root = ph.sb("root", [P, tiles])
        inv = ph.sb("inv", [P, tiles])
        tmp = ph.sb("tmp", [P, tiles])
        tp = [ph.ps(f"tp{i}", [P, G]) for i in range(2)]
        chain, var_ready, root_ready = ph.sem("chain"), ph.sem("var_ready"), ph.sem("root_ready")
        rows_ready, transposed, copied = ph.sem("rows_ready"), ph.sem("transposed"), ph.sem("copied")
        block = ph.block()

        @block.vector
        def _(dve):
            s = Steps(dve, chain)
            for t in range(tiles):
                s.mark(nc.vector.bn_stats(stats[:, t, :], src[:, t, :]))
            s.sync()
            for t in range(tiles):
                s.mark(nc.vector.bn_aggr(mv[:, t, :], stats[:, t, :]))
            s.sync()
            if rms_weight is None:
                nc.vector.tensor_scalar(var[:, :], mv[:, :, 1], eps, None, ALU.add).then_inc(var_ready, 1)
            else:
                s.done(nc.vector.tensor_tensor(tmp[:, :], mv[:, :, 0], mv[:, :, 0], ALU.mult))
                nc.vector.scalar_tensor_tensor(out=var[:, :], in0=mv[:, :, 1], scalar=eps, in1=tmp[:, :],
                                               op0=ALU.add, op1=ALU.add).then_inc(var_ready, 1)
            dve.wait_ge(var_ready, 1)
            dve.wait_ge(root_ready, 1)
            s.done(nc.vector.reciprocal(inv[:, :], root[:, :]))
            s.done(nc.vector.tensor_tensor(tmp[:, :], var[:, :], inv[:, :], ALU.mult))
            s.done(nc.vector.tensor_tensor(tmp[:, :], tmp[:, :], root[:, :], ALU.add))
            s.done(nc.vector.tensor_scalar(tmp[:, :], tmp[:, :], 0.5, None, ALU.mult))
            s.done(nc.vector.reciprocal(inv[:, :], tmp[:, :]))
            for t in range(tiles):
                if rms_weight is None:
                    nc.vector.tensor_scalar(dst[:, t, :], src[:, t, :], mv[:, t, 0:1], inv[:, t:t + 1],
                                            ALU.subtract, ALU.mult).then_inc(rows_ready, 1)
                else:
                    nc.vector.scalar_tensor_tensor(out=dst[:, t, :], in0=src[:, t, :], scalar=inv[:, t:t + 1],
                                                   in1=rms_weight[:, :], op0=ALU.mult,
                                                   op1=ALU.mult).then_inc(rows_ready, 1)

        @block.tensor
        def _(pe):
            for g in range(tiles // TPG if dst_t is not None else 0):
                pe.wait_ge(rows_ready, TPG * (g + 1))
                if g >= 2:
                    pe.wait_ge(copied, g - 1)
                for k in range(TPG):
                    last = nc.tensor.transpose(tp[g % 2][:, k * P:(k + 1) * P], dst[:, TPG * g + k, :], T.ident[:, :])
                last.then_inc(transposed, 1)

        @block.scalar
        def _(act):
            act.wait_ge(var_ready, 1)
            nc.scalar.activation(root[:, :], var[:, :], ACT.Sqrt).then_inc(root_ready, 1)
            for g in range(tiles // TPG if dst_t is not None else 0):
                act.wait_ge(transposed, g + 1)
                nc.scalar.copy(dst_t[:, g * G:(g + 1) * G], tp[g % 2][:, :]).then_inc(copied, 1)


def load(nc, name, *pairs):
    with Phase(nc, f"load_{name}") as ph:
        loaded = ph.sem("loaded")
        block = ph.block()

        @block.sync
        def _(sp):
            for dst, src in pairs:
                sp.dma_start(dst, src).then_inc(loaded, 16)
            sp.wait_ge(loaded, 16 * len(pairs))


def project_rows(nc, name, src_t, weight, dst, bias=None):
    with Phase(nc, name) as ph:
        pp = [ph.ps(f"pp{i}", [P, TPG, P]) for i in range(2)]
        multiplied, stored = ph.sem("multiplied"), ph.sem("stored")
        block = ph.block()

        @block.tensor
        def _(pe):
            for g in range(NG):
                if g >= 2:
                    pe.wait_ge(stored, g - 1)
                for k in range(TPG):
                    t = TPG * g + k
                    last = nc.tensor.matmul(pp[g % 2][:, k, :], src_t[:, t * P:(t + 1) * P], weight[:, :],
                                            start=True, stop=True)
                last.then_inc(multiplied, 1)

        @block.vector
        def _(dve):
            for g in range(NG):
                dve.wait_ge(multiplied, g + 1)
                o = dst[:, TPG * g:TPG * (g + 1), :]
                if bias is None:
                    nc.vector.tensor_copy(o, pp[g % 2][:, :, :]).then_inc(stored, 1)
                else:
                    for k in range(TPG):
                        last = nc.vector.tensor_tensor(dst[:, TPG * g + k, :], pp[g % 2][:, k, :], bias[:, :], ALU.add)
                    last.then_inc(stored, 1)


LEAD = 4


def lead(eng, *sems):
    for s in sems:
        eng.sem_inc(s, LEAD)


def graph_product(nc, name, T, adj, rows, dst, weigh, deg=None, groups=NG):
    CP = 512
    NP = N // CP
    BP = CP // P
    NB = N // P
    NR = 4
    LAG = 3
    NTP = 4
    NW = 4
    with Phase(nc, name) as ph:
        ring = ph.sb("ring", [P, NR, TPG, CP])
        wt = [ph.sb(f"wt{i}", [P, G]) for i in range(NW)]
        tp = [ph.ps(f"tp{i}", [P, G]) for i in range(NTP)]
        acc = ph.ps("acc", [P, G])
        if weigh:
            dist = [ph.sb(f"dist{i}", [P, G]) for i in range(2)]
            rec = [ph.sb(f"rec{i}", [P, G]) for i in range(2)]
            sens = [ph.sb(f"sens{i}", [P, G]) for i in range(2)]
            out_t = ph.sb("out_t", [P, G])
            back = ph.ps("back", [P, TPG, P])
        else:
            dsum = ph.sb("dsum", [P, NG, TPG, NP])
        loaded = [ph.sem(f"loaded{i}") for i in range(NR)]
        transposed = ph.sem("transposed")
        block_ready = ph.sem("block_ready")
        act_block, dve_block = ph.sem("act_block"), ph.sem("dve_block")
        multiplied = ph.sem("multiplied")
        rec_ready, sq_ready, sens_ready = ph.sem("rec_ready"), ph.sem("sq_ready"), ph.sem("sens_ready")
        dist_ready = ph.sem("dist_ready")
        summed = ph.sem("summed")
        acc_out, back_done, added = ph.sem("acc_out"), ph.sem("back_done"), ph.sem("added")
        chain = ph.sem("chain")
        block = ph.block()

        @block.sync
        def _(sp):
            def load(g, p):
                src = adj[bass.ds(g * G, G), p * CP:(p + 1) * CP]
                sp.dma_start(ring[:, p % NR, :, :],
                             src.rearrange("(t p) c -> p t c", p=P)).then_inc(loaded[p % NR], 16)

            def reload(g, p, next_g):
                if weigh:
                    sp.wait_ge(transposed, LEAD + g * NB + BP * (p + 1))
                else:
                    sp.wait_ge(summed, LEAD + g * NP + p + 1)
                if p + NR < NP:
                    load(g, p + NR)
                else:
                    load(next_g, p + NR - NP)

            for p in range(NR):
                load(0, p)
            if groups > 1:
                with sp.Fori(0, groups - 1) as g:
                    for p in range(NP):
                        reload(g, p, g + 1)
            for p in range(NP - NR):
                reload(groups - 1, p, None)

        @block.tensor
        def _(pe):
            lead(pe, transposed, multiplied)

            def product(g, j):
                if weigh:
                    pe.wait_ge(block_ready, LEAD + g * NB + j + 1)
                elif j % 2:
                    pe.wait_ge(act_block, LEAD + g * (NB // 2) + j // 2 + 1)
                else:
                    pe.wait_ge(dve_block, LEAD + g * (NB // 2) + j // 2 + 1)
                if j == 0:
                    pe.wait_ge(acc_out, LEAD + g)
                nc.tensor.matmul(acc[:, :], rows[:, j, :], wt[j % NW][:, :], start=(j == 0),
                                 stop=(j == NB - 1)).then_inc(multiplied, 1)

            with pe.Fori(0, groups) as g:
                for j in range(NB):
                    p, b = divmod(j, BP)
                    if b == 0:
                        pe.wait_ge(loaded[p % NR], (g * (NP // NR) + p // NR + 1) * 16)
                    if weigh:
                        pe.wait_ge(block_ready, LEAD + g * NB + j - NTP + 1)
                    elif j % 2:
                        pe.wait_ge(act_block, LEAD + g * (NB // 2) + j // 2 - NTP // 2 + 1)
                    else:
                        pe.wait_ge(dve_block, LEAD + g * (NB // 2) + j // 2 - NTP // 2 + 1)
                    for k in range(TPG):
                        last = nc.tensor.transpose(tp[j % NTP][:, k * P:(k + 1) * P],
                                                   ring[:, p % NR, k, b * P:(b + 1) * P], T.ident[:, :])
                    last.then_inc(transposed, 1)
                    if j >= LAG:
                        product(g, j - LAG)
                for j in range(NB - LAG, NB):
                    product(g, j)
                if weigh:
                    pe.wait_ge(acc_out, LEAD + g + 1)
                    pe.wait_ge(added, LEAD + g)
                    for k in range(TPG):
                        last = nc.tensor.transpose(back[:, k, :], out_t[:, k * P:(k + 1) * P], T.ident[:, :])
                    last.then_inc(back_done, 1)

        @block.scalar
        def _(act):
            lead(act, acc_out)
            if weigh:
                lead(act, sens_ready, dist_ready)

                def shift(g, j):
                    act.wait_ge(transposed, LEAD + g * NB + j + 1)
                    nc.scalar.activation(dist[j % 2][:, :], tp[j % NTP][:, :], ACT.Identity,
                                         bias=T.tiny[:, :]).then_inc(dist_ready, 1)
            else:
                lead(act, act_block)
            with act.Fori(0, groups) as g:
                if weigh:
                    act.wait_ge(rec_ready, LEAD + g * NB)
                    shift(g, 0)
                for j in range(NB):
                    if weigh:
                        if j + 1 < NB:
                            act.wait_ge(rec_ready, LEAD + g * NB + j)
                            shift(g, j + 1)
                        act.wait_ge(rec_ready, LEAD + g * NB + j + 1)
                        act.wait_ge(block_ready, LEAD + g * NB + j - 1)
                        nc.scalar.activation(sens[j % 2][:, :], rec[j % 2][:, :], ACT.Square,
                                             bias=-1.0).then_inc(sq_ready, 1)
                        act.wait_ge(sq_ready, g * NB + j + 1)
                        nc.scalar.activation(sens[j % 2][:, :], sens[j % 2][:, :], ACT.Exp,
                                             scale=-2.0).then_inc(sens_ready, 1)
                    elif j % 2:
                        act.wait_ge(transposed, LEAD + g * NB + j + 1)
                        act.wait_ge(multiplied, LEAD + g * NB + j - NW + 1)
                        nc.scalar.copy(wt[j % NW][:, :], tp[j % NTP][:, :]).then_inc(act_block, 1)
                act.wait_ge(multiplied, LEAD + (g + 1) * NB)
                if weigh:
                    act.wait_ge(added, LEAD + g)
                    nc.scalar.copy(out_t[:, :], acc[:, :]).then_inc(acc_out, 1)
                else:
                    nc.scalar.copy(dst[:, bass.ts(g, G)], acc[:, :]).then_inc(acc_out, 1)

        @block.vector
        def _(dve):
            if weigh:
                lead(dve, rec_ready, block_ready, added)

                def mask(g, j):
                    dve.wait_ge(sens_ready, LEAD + g * NB + j + 1)
                    dve.wait_ge(multiplied, LEAD + g * NB + j - NW + 1)
                    nc.vector.scalar_tensor_tensor(out=wt[j % NW][:, :], in0=tp[j % NTP][:, :], scalar=1.0,
                                                   in1=sens[j % 2][:, :], op0=ALU.is_lt,
                                                   op1=ALU.mult).then_inc(block_ready, 1)

                with dve.Fori(0, groups) as g:
                    for j in range(NB):
                        dve.wait_ge(dist_ready, LEAD + g * NB + j + 1)
                        dve.wait_ge(sens_ready, LEAD + g * NB + j - 1)
                        nc.vector.reciprocal(rec[j % 2][:, :], dist[j % 2][:, :]).then_inc(rec_ready, 1)
                        if j >= 1:
                            mask(g, j - 1)
                    mask(g, NB - 1)
                    dve.wait_ge(back_done, g + 1)
                    o = dst[:, bass.ds(g * TPG, TPG), :].rearrange("p t c -> p (t c)")
                    nc.vector.tensor_tensor(o, o, back[:, :, :].rearrange("p t c -> p (t c)"),
                                            ALU.add).then_inc(added, 1)
            else:
                lead(dve, dve_block, summed)
                with dve.Fori(0, groups) as g:
                    for j in range(NB):
                        p, b = divmod(j, BP)
                        if j % 2 == 0:
                            dve.wait_ge(transposed, LEAD + g * NB + j + 1)
                            dve.wait_ge(multiplied, LEAD + g * NB + j - NW + 1)
                            nc.vector.tensor_copy(wt[j % NW][:, :], tp[j % NTP][:, :]).then_inc(dve_block, 1)
                        if b == BP - 1:
                            dve.wait_ge(loaded[p % NR], (g * (NP // NR) + p // NR + 1) * 16)
                            dve.wait_ge(transposed, LEAD + g * NB + j + 1)
                            nc.vector.tensor_reduce(dsum[:, bass.ds(g, 1), :, p].rearrange("p a t -> p (a t)"),
                                                    ring[:, p % NR, :, :], AX.X, ALU.add).then_inc(summed, 1)
                s = Steps(dve, chain)
                dve.wait_ge(summed, LEAD + NG * NP)
                s.done(nc.vector.tensor_reduce(deg[:, :], dsum[:, :, :, :].rearrange("p g t n -> p (g t) n"),
                                               AX.X, ALU.add))
                s.done(nc.vector.tensor_scalar(deg[:, :], deg[:, :], 1.0, None, ALU.add))
                s.done(nc.vector.reciprocal(deg[:, :], deg[:, :]))


CHUNK = 32
GATES = [0, 1, 3, 2]


def lstm(nc, T):
    SPL = 2 * CHUNK
    IPG = G // SPL
    UPI = NT // IPG
    SPU = SPL // UPI
    TAIL = 2 * TPG + 8
    with Phase(nc, "lstm") as ph:
        wrec = ph.sb("wrec", [P, 2, 4, P], F16)
        win = ph.sb("win", [P, 4, P])
        bias = ph.sb("bias", [P, 4, P])
        wtmp = ph.sb("wtmp", [P, 4, P])
        tanhs = ph.sb("tanhs", [P, 5])
        terms = ph.sb("terms", [P, 2])
        c_twice = ph.ps("c_twice", [P, 1])
        tanh_c = ph.sb("tanh_c", [P, 1])
        half_term = ph.sb("half_term", [P, 1])
        o_plus = ph.sb("o_plus", [P, 1])
        warm = ph.sb("warm", [P, 1])
        h_parts = ph.sb("h_parts", [P, SPL, 2], F16)
        h_full = ph.sb("h_full", [P, SPL])
        gates = [ph.ps(f"gates{b}", [P, CHUNK, 4]) for b in range(2)]
        largest = ph.sb("largest", [P, 2])
        scale = ph.sb("scale", [P, 2])
        chain, weights_ready = ph.sem("chain"), ph.sem("weights_ready")
        largest_ready, largest_of_all, scale_ready = (ph.sem(n) for n in ("largest_ready", "largest_of_all", "scale_ready"))
        gates_ready, tanhs_ready = ph.sem("gates_ready"), ph.sem("tanhs_ready")
        c_ready, c_kept = ph.sem("c_ready"), ph.sem("c_kept")
        half_ready, o_ready = ph.sem("half_ready"), ph.sem("o_ready")
        tanh_c_ready = ph.sem("tanh_c_ready")
        high_ready, low_ready, full_ready = ph.sem("high_ready"), ph.sem("low_ready"), ph.sem("full_ready")
        collected = ph.sem("collected")
        ring = ph.sb("ring", [P, UPI, TPG, P])
        dist = ph.sb("dist", [P, G])
        rec = ph.sb("rec", [P, G])
        sens = ph.sb("sens", [P, G])
        wt = ph.sb("wt", [P, 2, G])
        msg_now = ph.sb("msg_now", [P, UPI, P])
        total = ph.sb("total", [P, G])
        row = ph.sb("row", [P, TPG, P])
        square = ph.sb("square", [P, TPG, P])
        mean, var, root, inv, tmp = (ph.sb(n, [P, TPG]) for n in ("mean", "var", "root", "inv", "tmp"))
        tp = ph.ps("tp", [P, G])
        acc = ph.ps("acc", [P, G])
        back = ph.ps("back", [P, TPG, P])
        loaded = [ph.sem(f"loaded{j}") for j in range(UPI)]
        transposed, dist_ready, rec_ready = ph.sem("transposed"), ph.sem("dist_ready"), ph.sem("rec_ready")
        sq_ready, sens_ready, block_ready = ph.sem("sq_ready"), ph.sem("sens_ready"), ph.sem("block_ready")
        multiplied, acc_out, acc_zeroed = ph.sem("multiplied"), ph.sem("acc_out"), ph.sem("acc_zeroed")
        msg_copied = ph.sem("msg_copied")
        back_done, tail_chain = ph.sem("back_done"), ph.sem("tail_chain")
        var_ready, root_ready, rows_ready = ph.sem("var_ready"), ph.sem("root_ready"), ph.sem("rows_ready")
        row_t_done, row_t_out = ph.sem("row_t_done"), ph.sem("row_t_out")
        block = ph.block()

        @block.sync
        def _(sp):
            def load_block(group, i, j):
                src = T.D["adj"][bass.ds(group * G, G), bass.ds((i * UPI + j) * P, P)]
                sp.dma_start(ring[:, j, :, :], src.rearrange("(t p) c -> p t c", p=P)).then_inc(loaded[j], 16)

            def reload(q, group, i):
                for j in range(UPI):
                    sp.wait_ge(transposed, LEAD + q * UPI + j + 1)
                    load_block(group, i, j)

            for j in range(UPI):
                load_block(1, 0, j)
            with sp.Fori(0, NG - 2) as g:
                with sp.Fori(0, IPG - 1) as i:
                    reload(g * IPG + i, g + 1, i + 1)
                reload(g * IPG + IPG - 1, g + 2, 0)
            with sp.Fori(0, IPG - 1) as i:
                reload((NG - 2) * IPG + i, NG - 1, i + 1)

        @block.tensor
        def _(pe):
            lead(pe, transposed, multiplied)

            def input_gates(b, first_step, m):
                k, g = m // 4, m % 4
                w = (win if k else bias)[:, g, :]
                x = T.xn_t[:, bass.ds(first_step, CHUNK)] if k else T.ones[:, 0:CHUNK]
                nc.tensor.matmul(gates[b][:, :, g], w, x, start=(m == 0), stop=False, skip_group_check=True)

            def steps(base, q=None, group=None):
                for n in range(SPL):
                    b, t = divmod(n, CHUNK)
                    last_n = (n - 1) % SPL
                    for part, sem in ((0, high_ready), (1, low_ready)):
                        pe.wait_ge(sem, base + n + 1)
                        for w in range(2 - part):
                            for g in range(4):
                                last = nc.tensor.matmul(gates[b][:, t, g:g + 1], wrec[:, w, g, :],
                                                        h_parts[:, last_n, part:part + 1], start=False, stop=True,
                                                        skip_group_check=True)
                    last.then_inc(gates_ready, 1)
                    if 2 <= t < 10:
                        input_gates(1 - b, base + (b + 1) * CHUNK, t - 2)
                    j, s = divmod(n, SPU)
                    if q is not None and s == 0:
                        pe.wait_ge(loaded[j], (q + 1) * 16)
                        pe.wait_ge(dist_ready, LEAD + q * UPI + j)
                        for k in range(TPG):
                            last = nc.tensor.transpose(tp[:, k * P:(k + 1) * P], ring[:, j, k, :], T.ident[:, :])
                        last.then_inc(transposed, 1)
                    if q is not None and s in (14, 15):
                        half = s - 14
                        c = slice(half * (G // 2), (half + 1) * (G // 2))
                        pe.wait_ge(block_ready, LEAD + (q * UPI + j) * 2 + half + 1)
                        if j == 0 and half == 0:
                            pe.wait_ge(acc_zeroed, group + 1)
                            pe.wait_ge(msg_copied, q + 1)
                        nc.tensor.matmul(acc[:, c], msg_now[:, j, :], wt[:, j % 2, c], start=False,
                                         stop=True, skip_group_check=True).then_inc(multiplied, 1)

            pe.wait_ge(weights_ready, 1)
            for m in range(8):
                input_gates(0, 0, m)
            with pe.Fori(0, NG - 1) as g:
                with pe.Fori(0, IPG) as i:
                    steps(g * G + i * SPL, g * IPG + i, g)
                pe.wait_ge(acc_out, g + 1)
                for k in range(TPG):
                    last = nc.tensor.transpose(back[:, k, :], total[:, k * P:(k + 1) * P], T.ident[:, :])
                last.then_inc(back_done, 1)
                for m in range(4):
                    input_gates(0, g * G + G, m)
                pe.wait_ge(rows_ready, g + 1)
                for k in range(TPG):
                    last = nc.tensor.transpose(tp[:, k * P:(k + 1) * P], row[:, k, :], T.ident[:, :])
                last.then_inc(row_t_done, 1)
                pe.wait_ge(row_t_out, g + 1)
                for m in range(4, 8):
                    input_gates(0, g * G + G, m)
            with pe.Fori(0, IPG) as i:
                steps((NG - 1) * G + i * SPL)

        @block.scalar
        def _(act):
            lead(act, dist_ready, sq_ready)
            nc.scalar.activation(warm[:, :], T.tiny[:, :], ACT.Tanh)
            unscale = act.alloc_register("unscale")
            act.wait_ge(scale_ready, 1)
            act.reg_load(unscale, scale[0:1, 1:2].bitcast(I32))

            def steps(base, q=None):
                for n in range(SPL):
                    b, t = divmod(n, CHUNK)
                    act.wait_ge(gates_ready, base + n + 1)
                    act.wait_ge(full_ready, base + n + 1)
                    nc.scalar.activation(tanhs[:, 0:4], gates[b][:, t, :], ACT.Tanh,
                                         scale=unscale).then_inc(tanhs_ready, 1)
                    act.wait_ge(c_ready, base + n + 1)
                    nc.scalar.activation(tanh_c[:, :], c_twice[:, :], ACT.Tanh, scale=0.5).then_inc(tanh_c_ready, 1)
                    if q is None:
                        continue
                    j, s = divmod(n, SPU)
                    if s == 1:
                        act.wait_ge(transposed, LEAD + q * UPI + j + 1)
                        act.wait_ge(block_ready, LEAD + (q * UPI + j) * 2)
                        nc.scalar.activation(dist[:, :], tp[:, :], ACT.Identity,
                                             bias=T.tiny[:, :]).then_inc(dist_ready, 1)
                    if s == 10:
                        act.wait_ge(rec_ready, (q * UPI + j + 1) * 8)
                        nc.scalar.activation(sens[:, :], rec[:, :], ACT.Square, bias=-1.0).then_inc(sq_ready, 1)
                    if s == 11:
                        act.wait_ge(sq_ready, LEAD + q * UPI + j + 1)
                        nc.scalar.activation(sens[:, :], sens[:, :], ACT.Exp, scale=-2.0).then_inc(sens_ready, 1)

            with act.Fori(0, NG - 1) as g:
                with act.Fori(0, IPG) as i:
                    steps(g * G + i * SPL, g * IPG + i)
                act.wait_ge(multiplied, LEAD + (g + 1) * (NT * 2))
                nc.scalar.copy(total[:, :], acc[:, :]).then_inc(acc_out, 1)
                act.wait_ge(var_ready, g + 1)
                nc.scalar.activation(root[:, :], var[:, :], ACT.Sqrt).then_inc(root_ready, 1)
                act.wait_ge(row_t_done, g + 1)
                nc.scalar.copy(T.xn_t[:, bass.ds(g * G + G, G)], tp[:, :]).then_inc(row_t_out, 1)
                nc.scalar.activation(warm[:, :], T.tiny[:, :], ACT.Tanh)
            with act.Fori(0, IPG) as i:
                steps((NG - 1) * G + i * SPL)

        @block.vector
        def _(dve):
            s = Steps(dve, chain)
            s.mark(nc.vector.memset(T.xn_t[:, N:N + CHUNK], 0.0))
            s.mark(nc.vector.tensor_tensor(T.bias_rows[:, 0, :], T.bias_rows[:, 0, :], T.bias_rows[:, 1, :], ALU.add))
            s.sync()
            for g, src in enumerate(GATES):
                cols = slice(src * P, (src + 1) * P)
                k = 1.0 if g == 3 else 0.5
                s.mark(nc.vector.tensor_scalar(win[:, g, :], T.wih[:, cols], k, None, ALU.mult))
                s.mark(nc.vector.tensor_scalar(bias[:, g, :], T.bias_rows[:, 0, cols], k, None, ALU.mult))
                s.mark(nc.vector.tensor_scalar(wtmp[:, g, :], T.whh[:, cols], k / 2, None, ALU.mult))
            s.sync()
            nc.vector.tensor_reduce(largest[:, 0:1], wtmp[:, :, :], AX.XY, ALU.max,
                                    apply_absolute_value=True).then_inc(largest_ready, 1)
            dve.wait_ge(largest_of_all, 1)
            s.done(nc.vector.tensor_scalar(scale[:, 0:1].bitcast(I32), largest[:, 1:2].bitcast(I32), 0x7F800000, None,
                                           ALU.bitwise_and))
            s.done(nc.vector.tensor_scalar(scale[:, 0:1], scale[:, 0:1], 2.0 ** -20, None, ALU.max))
            nc.vector.tensor_scalar(scale[:, 1:2], scale[:, 0:1], 2.0 ** -13, None, ALU.mult).then_inc(scale_ready, 1)
            dve.wait_ge(scale_ready, 1)
            s.done(nc.vector.reciprocal(scale[:, 0:1], scale[:, 1:2]))
            for w in (win, bias, wtmp):
                s.mark(nc.vector.tensor_scalar(w[:, :, :], w[:, :, :], scale[:, 0:1], None, ALU.mult))
            s.sync()
            s.done(nc.vector.tensor_copy(wrec[:, 0, :, :], wtmp[:, :, :]))
            s.done(nc.vector.tensor_tensor(wrec[:, 1, :, :], wtmp[:, :, :], wrec[:, 0, :, :], ALU.subtract))
            nc.vector.memset(c_twice[:, :], 0.0).then_inc(weights_ready, 1)
            nc.vector.memset(tanhs[:, 4:5], 0.0).then_inc(c_kept, 1)
            nc.vector.memset(h_parts[:, SPL - 1, 0:1], 0.0).then_inc(high_ready, 1)
            nc.vector.memset(h_parts[:, SPL - 1, 1:2], 0.0).then_inc(low_ready, 1)
            nc.vector.memset(h_full[:, :], 0.0).then_inc(full_ready, 1)
            nc.vector.memset(acc[:, :], 0.0).then_inc(acc_zeroed, 1)

            def steps(base, chunk, q=None):
                for n in range(SPL):
                    at = base + n + 1
                    dve.wait_ge(tanhs_ready, at)
                    dve.wait_ge(c_kept, at)
                    nc.vector.scalar_tensor_tensor(out=terms[:, :], in0=tanhs[:, 0:2], scalar=1.0,
                                                   in1=tanhs[:, 3:5], op0=ALU.add, op1=ALU.mult,
                                                   accum_out=c_twice[:, :]).then_inc(c_ready, 1)
                    dve.wait_ge(c_ready, at)
                    nc.vector.tensor_scalar(half_term[:, :], terms[:, 1:2], 0.5, None, ALU.mult).then_inc(half_ready, 1)
                    nc.vector.tensor_scalar(o_plus[:, :], tanhs[:, 2:3], 1.0, None, ALU.add).then_inc(o_ready, 1)
                    dve.wait_ge(tanh_c_ready, at)
                    nc.vector.scalar_tensor_tensor(out=h_parts[:, n, 0:1], in0=tanhs[:, 2:3], scalar=1.0,
                                                   in1=tanh_c[:, :], op0=ALU.add,
                                                   op1=ALU.mult).then_inc(high_ready, 1)
                    dve.wait_ge(high_ready, at + 1)
                    dve.wait_ge(o_ready, at)
                    nc.vector.scalar_tensor_tensor(out=h_parts[:, n, 1:2], in0=tanh_c[:, :], scalar=o_plus[:, :],
                                                   in1=h_parts[:, n, 0:1], op0=ALU.mult,
                                                   op1=ALU.subtract).then_inc(low_ready, 1)
                    dve.wait_ge(half_ready, at)
                    nc.vector.scalar_tensor_tensor(out=tanhs[:, 4:5], in0=terms[:, 0:1], scalar=0.5,
                                                   in1=half_term[:, :], op0=ALU.mult, op1=ALU.add).then_inc(c_kept, 1)
                    if n % CHUNK == 0:
                        dve.wait_ge(collected, chunk + n // CHUNK)
                    nc.vector.scalar_tensor_tensor(out=h_full[:, n:n + 1], in0=tanhs[:, 2:3], scalar=1.0,
                                                   in1=tanh_c[:, :], op0=ALU.add, op1=ALU.mult).then_inc(full_ready, 1)
                    if q is None:
                        continue
                    j, s = divmod(n, SPU)
                    if 2 <= s <= 9:
                        c = slice((s - 2) * (G // 8), (s - 1) * (G // 8))
                        dve.wait_ge(dist_ready, LEAD + q * UPI + j + 1)
                        dve.wait_ge(sq_ready, LEAD + q * UPI + j)
                        nc.vector.reciprocal(rec[:, c], dist[:, c]).then_inc(rec_ready, 1)
                    if s in (12, 13):
                        half = s - 12
                        c = slice(half * (G // 2), (half + 1) * (G // 2))
                        dve.wait_ge(sens_ready, q * UPI + j + 1)
                        dve.wait_ge(multiplied, LEAD + (q * UPI + j - 1) * 2)
                        nc.vector.scalar_tensor_tensor(out=wt[:, j % 2, c], in0=dist[:, c], scalar=1.0,
                                                       in1=sens[:, c], op0=ALU.is_lt,
                                                       op1=ALU.mult).then_inc(block_ready, 1)

            def wide(column):
                return column[:, :].unsqueeze(2).broadcast_to([P, TPG, P])

            lead(dve, block_ready)
            with dve.Fori(0, NG - 1) as g:
                with dve.Fori(0, IPG) as i:
                    steps(g * G + i * SPL, LEAD - 1 + (g * IPG + i) * 2, g * IPG + i)
                s = Steps(dve, tail_chain, g * TAIL)
                dve.wait_ge(acc_out, g + 1)
                nc.vector.memset(acc[:, :], 0.0).then_inc(acc_zeroed, 1)
                dve.wait_ge(back_done, g + 1)
                x = T.x[:, bass.ds(g * TPG + TPG, TPG), :]
                for k in range(TPG):
                    s.mark(nc.vector.scalar_tensor_tensor(out=row[:, k, :], in0=back[:, k, :], scalar=0.0,
                                                          in1=T.x[:, bass.ds(g * TPG + TPG + k, 1), :]
                                                          .rearrange("p a c -> p (a c)"), op0=ALU.add, op1=ALU.add,
                                                          accum_out=mean[:, k:k + 1]))
                s.sync()
                s.mark(nc.vector.tensor_scalar(x, row[:, :, :], 0.0, None, ALU.add))
                s.done(nc.vector.tensor_scalar(mean[:, :], mean[:, :], 1 / P, None, ALU.mult))
                s.done(nc.vector.tensor_tensor(row[:, :, :], row[:, :, :], wide(mean), ALU.subtract))
                for k in range(TPG):
                    s.mark(nc.vector.scalar_tensor_tensor(out=square[:, k, :], in0=row[:, k, :], scalar=1.0,
                                                          in1=row[:, k, :], op0=ALU.mult, op1=ALU.mult,
                                                          accum_out=var[:, k:k + 1]))
                s.sync()
                nc.vector.tensor_scalar(var[:, :], var[:, :], 1 / P, 1e-5, ALU.mult, ALU.add).then_inc(var_ready, 1)
                dve.wait_ge(root_ready, g + 1)
                dve.wait_ge(var_ready, g + 1)
                s.done(nc.vector.reciprocal(inv[:, :], root[:, :]))
                s.done(nc.vector.tensor_tensor(tmp[:, :], var[:, :], inv[:, :], ALU.mult))
                s.done(nc.vector.tensor_tensor(tmp[:, :], tmp[:, :], root[:, :], ALU.add))
                s.done(nc.vector.tensor_scalar(tmp[:, :], tmp[:, :], 0.5, None, ALU.mult))
                s.done(nc.vector.reciprocal(inv[:, :], tmp[:, :]))
                assert s.n == TAIL
                last = nc.vector.tensor_tensor(row[:, :, :], row[:, :, :], wide(inv), ALU.mult)
                last.then_inc(rows_ready, 1)
            with dve.Fori(0, IPG) as i:
                steps((NG - 1) * G + i * SPL, LEAD - 1 + (NG - 1) * IPG * 2 + i * 2)

        @block.gpsimd
        def _(pool):
            lead(pool, collected)
            pool.wait_ge(largest_ready, 1)
            nc.gpsimd.partition_all_reduce(largest[:, 1:2], largest[:, 0:1], P, RMAX).then_inc(largest_of_all, 1)

            def collect(base):
                for b in range(2):
                    pool.wait_ge(full_ready, base + (b + 1) * CHUNK + 1)
                    nc.gpsimd.tensor_copy(T.hid_t[:, bass.ds(base + b * CHUNK, CHUNK)],
                                          h_full[:, b * CHUNK:(b + 1) * CHUNK]).then_inc(collected, 1)

            with pool.Fori(0, NG - 1) as g:
                with pool.Fori(0, IPG) as i:
                    q = g * IPG + i
                    pool.wait_ge(multiplied, LEAD + q * UPI * 2)
                    nc.gpsimd.tensor_copy(msg_now[:, :, :], T.msg[:, bass.ds(i * UPI, UPI), :]).then_inc(msg_copied, 1)
                    collect(g * G + i * SPL)
            with pool.Fori(0, IPG) as i:
                collect((NG - 1) * G + i * SPL)


def add_sequence_sums(nc, T):
    with Phase(nc, "sums") as ph:
        logit = [ph.ps(f"logit{i}", [P, 2, G]) for i in range(2)]
        back = [ph.ps(f"back{i}", [P, TPG, P]) for i in range(2)]
        wsel = ph.sb("wsel", [P, 2, P])
        one = [ph.sb(f"one{i}", [P, G]) for i in range(2)]
        cls = ph.sb("cls", [P, G])
        w = ph.sb("w", [P, N])
        inc = ph.sb("inc", [P, N])
        zero = ph.sb("zero", [P, G])
        cols = ph.sb("cols", [P, 6])
        wlin, blin, att = ph.sb("wlin", [P, 2]), ph.sb("blin", [P, 2]), ph.sb("att", [P, 2])
        loaded, ready, chain = ph.sem("loaded"), ph.sem("ready"), ph.sem("chain")
        logits_ready, logit_used, one_ready = ph.sem("logits_ready"), ph.sem("logit_used"), ph.sem("one_ready")
        update_ready, transposed, added = ph.sem("update_ready"), ph.sem("transposed"), ph.sem("added")
        block = ph.block()

        @block.sync
        def _(sp):
            sp.dma_start(wlin[:, :], T.D["w_lin"]).then_inc(loaded, 16)
            sp.dma_start(blin[:, :], T.D["b_lin"].broadcast_to([P, 2])).then_inc(loaded, 16)
            sp.dma_start(att[:, 0:1], T.D["fw_att"]).then_inc(loaded, 16)
            sp.dma_start(att[:, 1:2], T.D["bw_att"]).then_inc(loaded, 16)

        @block.tensor
        def _(pe):
            pe.wait_ge(ready, 1)
            for g in range(NG):
                if g >= 2:
                    pe.wait_ge(logit_used, g - 1)
                for l in range(2):
                    last = nc.tensor.matmul(logit[g % 2][:, l, :], wsel[:, l, :], T.hid_t[:, g * G:(g + 1) * G],
                                            start=True, stop=True)
                last.then_inc(logits_ready, 1)
            for g in range(NG):
                pe.wait_ge(update_ready, g + 1)
                if g >= 2:
                    pe.wait_ge(added, g - 1)
                for k in range(TPG):
                    t = TPG * g + k
                    last = nc.tensor.transpose(back[g % 2][:, k, :], T.hid_t[:, t * P:(t + 1) * P], T.ident[:, :])
                last.then_inc(transposed, 1)

        @block.scalar
        def _(act):
            act.wait_ge(ready, 1)
            for g in range(NG):
                act.wait_ge(logits_ready, g + 1)
                if g >= 2:
                    act.wait_ge(logit_used, g - 1)
                nc.scalar.activation(one[g % 2][:, :], logit[g % 2][:, 1, :], ACT.Identity,
                                     bias=blin[:, 1:2]).then_inc(one_ready, 1)

        @block.vector
        def _(dve):
            s = Steps(dve, chain)
            dve.wait_ge(loaded, 64)
            s.mark(nc.vector.memset(zero[:, :], 0.0))
            for l in range(2):
                s.mark(nc.vector.tensor_scalar(wsel[:, l, :], T.ones[:, :], wlin[:, l:l + 1], 0.5, ALU.mult, ALU.mult))
            s.mark(nc.vector.tensor_scalar(cols[:, 0:2], att[:, :], 0.5, None, ALU.mult))
            s.sync()
            s.mark(nc.vector.tensor_tensor(cols[:, 2:3], cols[:, 0:1], cols[:, 1:2], ALU.subtract))
            nc.vector.tensor_scalar(cols[:, 3:4], cols[:, 0:1], -1.0, None, ALU.mult).then_inc(ready, 1)
            for g in range(NG):
                c = slice(g * G, (g + 1) * G)
                dve.wait_ge(one_ready, g + 1)
                s.done(nc.vector.scalar_tensor_tensor(out=cls[:, :], in0=logit[g % 2][:, 0, :], scalar=blin[:, 0:1],
                                                      in1=one[g % 2][:, :], op0=ALU.add, op1=ALU.is_lt))
                nc.vector.tensor_tensor(w[:, c], cls[:, :], T.hid_t[:, c], ALU.mult).then_inc(logit_used, 1)
                dve.wait_ge(logit_used, g + 1)
                start = 0.0 if g == 0 else inc[:, g * G - 1:g * G]
                s.done(nc.vector.tensor_tensor_scan(out=inc[:, c], data0=w[:, c], data1=zero[:, :],
                                                    initial=start, op0=ALU.add, op1=ALU.add))
            s.done(nc.vector.tensor_tensor(cols[:, 4:5], inc[:, N - 1:N], cols[:, 1:2], ALU.mult))

            def add_back(g):
                dve.wait_ge(transposed, g + 1)
                o = T.x[:, TPG * g:TPG * (g + 1), :]
                nc.vector.tensor_tensor(o, o, back[g % 2][:, :, :], ALU.add).then_inc(added, 1)

            for g in range(NG):
                c = slice(g * G, (g + 1) * G)
                s.done(nc.vector.scalar_tensor_tensor(out=T.hid_t[:, c], in0=inc[:, c], scalar=cols[:, 2:3],
                                                      in1=T.hid_t[:, c], op0=ALU.mult, op1=ALU.add))
                s.done(nc.vector.scalar_tensor_tensor(out=T.hid_t[:, c], in0=w[:, c], scalar=cols[:, 3:4],
                                                      in1=T.hid_t[:, c], op0=ALU.mult, op1=ALU.add))
                nc.vector.tensor_scalar(T.hid_t[:, c], T.hid_t[:, c], cols[:, 4:5], None,
                                        ALU.add).then_inc(update_ready, 1)
                if g >= 1:
                    add_back(g - 1)
            add_back(NG - 1)


def combine_neighbours(nc, T):
    with Phase(nc, "combine") as ph:
        own = [ph.ps(f"own{i}", [P, TPG, P]) for i in range(2)]
        nb = [ph.ps(f"nb{i}", [P, TPG, P]) for i in range(2)]
        lin = ph.sb("lin", [P, 2, P])
        loaded, multiplied, scaled, added = (ph.sem(n) for n in ("loaded", "multiplied", "scaled", "added"))
        block = ph.block()

        @block.sync
        def _(sp):
            sp.dma_start(lin[:, :, :], T.D["lin_w"].rearrange("(a p) o -> p a o", p=P)).then_inc(loaded, 16)

        @block.tensor
        def _(pe):
            pe.wait_ge(loaded, 16)
            for g in range(NG):
                if g >= 2:
                    pe.wait_ge(added, g - 1)
                for k in range(TPG):
                    c = slice((TPG * g + k) * P, (TPG * g + k + 1) * P)
                    nc.tensor.matmul(own[g % 2][:, k, :], T.xn_t[:, c], lin[:, 0, :], start=True, stop=True)
                    last = nc.tensor.matmul(nb[g % 2][:, k, :], T.agg_t[:, c], lin[:, 1, :], start=True, stop=True)
                last.then_inc(multiplied, 1)

        @block.vector
        def _(dve):
            for g in range(NG):
                dve.wait_ge(multiplied, g + 1)
                for k in range(TPG):
                    t = TPG * g + k
                    last = nc.vector.scalar_tensor_tensor(out=T.x[:, t, :], in0=nb[g % 2][:, k, :],
                                                          scalar=T.deg[:, t:t + 1], in1=T.x[:, t, :],
                                                          op0=ALU.mult, op1=ALU.add)
                last.then_inc(scaled, 1)
                dve.wait_ge(scaled, g + 1)
                o = T.x[:, TPG * g:TPG * (g + 1), :]
                nc.vector.tensor_tensor(o, o, own[g % 2][:, :, :], ALU.add).then_inc(added, 1)


def split_heads(nc, T):
    NQK = NHEAD + NKV
    NB = 3
    with Phase(nc, "heads") as ph:
        wqk = ph.sb("wqk", [P, NQK, 2, P])
        wv = ph.sb("wv", [P, NKV * HD])
        cos = [ph.sb(f"cos{i}", [P, G]) for i in range(2)]
        sin = [ph.sb(f"sin{i}", [P, G]) for i in range(2)]
        rs = [ph.sb(f"rs{i}", [P, G]) for i in range(2)]
        q = [ph.sb(f"q{i}", [P, G]) for i in range(NB)]
        r1 = [ph.sb(f"r1{i}", [P, G]) for i in range(NB)]
        p2 = [ph.sb(f"p2{i}", [P, G], BF16) for i in range(NB)]
        plain = [ph.ps(f"plain{i}", [P, G]) for i in range(2)]
        turned = [ph.ps(f"turned{i}", [P, G]) for i in range(2)]
        vp = [ph.ps(f"vp{i}", [P, TPG, NKV * HD]) for i in range(2)]
        loaded, tables = ph.sem("loaded"), [ph.sem("tables0"), ph.sem("tables1")]
        projected, turned_by, q_ready = ph.sem("projected"), ph.sem("turned_by"), ph.sem("q_ready")
        p1_ready, r1_ready, p2_ready = (ph.sem(n) for n in ("p1_ready", "r1_ready", "p2_ready"))
        first_placed, second_placed, third_placed = (ph.sem(n) for n in ("first_placed", "second_placed", "third_placed"))
        v_ready, v_stored, ones_ready = ph.sem("v_ready"), ph.sem("v_stored"), ph.sem("ones_ready")
        block = ph.block()
        units = [(g, h) for g in range(NG) for h in range(NQK)]
        lo, hi = slice(0, HD), slice(HD, 2 * HD)

        def stacks(n):
            h = units[n][1]
            return (T.qa[h], T.qb[h]) if h < NHEAD else (T.ka[h - NHEAD], T.kb[h - NHEAD])

        def cols(n):
            g = units[n][0]
            return slice(g * G, (g + 1) * G)

        def is_query(n):
            return units[n][1] < NHEAD

        @block.sync
        def _(sp):
            sp.dma_start(wqk[:, :, :, :], T.D["wqk"].rearrange("c (h r m) -> c h r m", h=NQK, r=2)).then_inc(loaded, 16)
            sp.dma_start(wv[:, :], T.D["wv"]).then_inc(loaded, 16)
            for g in range(NG):
                if g >= 2:
                    sp.wait_ge(turned_by, NQK * (g - 1))
                for quad in range(4):
                    rows = slice(quad * HD, (quad + 1) * HD)
                    sp.dma_start(cos[g % 2][rows, :], T.D["cos"][:, g * G:(g + 1) * G]).then_inc(tables[g % 2], 16)
                    sp.dma_start(sin[g % 2][rows, :], T.D["sin"][:, g * G:(g + 1) * G]).then_inc(tables[g % 2], 16)

        @block.tensor
        def _(pe):
            pe.wait_ge(loaded, 32)
            for n, (g, h) in enumerate(units):
                if n >= 2:
                    pe.wait_ge(turned_by, n - 1)
                x = T.xn_t[:, g * G:(g + 1) * G]
                nc.tensor.matmul(plain[n % 2][:, :], wqk[:, h, 0, :], x, start=True, stop=True)
                nc.tensor.matmul(turned[n % 2][:, :], wqk[:, h, 1, :], x, start=True, stop=True).then_inc(projected, 1)
                if h == NQK - 1:
                    if g >= 2:
                        pe.wait_ge(v_stored, g - 1)
                    for k in range(TPG):
                        t = TPG * g + k
                        last = nc.tensor.matmul(vp[g % 2][:, k, :], T.xn_t[:, t * P:(t + 1) * P], wv[:, :],
                                                start=True, stop=True)
                    last.then_inc(v_ready, 1)

        @block.vector
        def _(dve):
            for kv in range(NKV):
                nc.vector.memset(T.kb[kv][2 * HD:2 * HD + 2, :], 1.0)

            def remainder(m):
                dve.wait_ge(p1_ready, m + 1)
                if m >= NB:
                    dve.wait_ge(third_placed, m - NB + 1)
                nc.vector.tensor_tensor(r1[m % NB][:, :], q[m % NB][:, :], stacks(m)[0][:, cols(m)],
                                        ALU.subtract).then_inc(r1_ready, 1)

            def store_values(g):
                dve.wait_ge(v_ready, g + 1)
                nc.vector.tensor_copy(T.v[:, TPG * g:TPG * (g + 1), :, :],
                                      vp[g % 2][:, :, :].rearrange("p t (k d) -> p t k d", k=NKV)).then_inc(v_stored, 1)

            for n, (g, h) in enumerate(units):
                b = n % 2
                if h == 0:
                    dve.wait_ge(tables[g % 2], (g // 2 + 1) * 8 * 16)
                dve.wait_ge(projected, n + 1)
                if n >= 2:
                    dve.wait_ge(q_ready, n - 1)
                if n >= NB:
                    dve.wait_ge(r1_ready, n - NB + 1)
                    dve.wait_ge(first_placed, n - NB + 1)
                nc.vector.tensor_tensor(q[n % NB][:, :], plain[b][:, :], cos[g % 2][:, :], ALU.mult)
                nc.vector.tensor_tensor(rs[b][:, :], turned[b][:, :], sin[g % 2][:, :], ALU.mult).then_inc(turned_by, 1)
                if n >= 1:
                    remainder(n - 1)
                if h == 2 and g >= 1:
                    store_values(g - 1)
            remainder(len(units) - 1)
            store_values(NG - 1)

        @block.scalar
        def _(act):
            for n in range(len(units) + 1):
                m = n - 1
                if n < len(units):
                    act.wait_ge(q_ready, n + 1)
                    nc.scalar.copy(stacks(n)[0][:, cols(n)], q[n % NB][:, :]).then_inc(p1_ready, 1)
                if m >= 0:
                    act.wait_ge(r1_ready, m + 1)
                    if m >= NB:
                        act.wait_ge(third_placed, m - NB + 1)
                    nc.scalar.copy(p2[m % NB][:, :], r1[m % NB][:, :]).then_inc(p2_ready, 1)
                if n < len(units):
                    rows = lo if is_query(n) else hi
                    nc.scalar.copy(stacks(n)[1][rows, cols(n)], q[n % NB][rows, :]).then_inc(first_placed, 1)
                if m >= 0:
                    act.wait_ge(p2_ready, m + 1)
                    for rows in [slice(2 * HD, 4 * HD)] if is_query(m) else [hi, slice(3 * HD, 4 * HD)]:
                        last = nc.scalar.copy(stacks(m)[0][rows, cols(m)], p2[m % NB][rows, :])
                    last.then_inc(second_placed, 1)

        @block.gpsimd
        def _(pool):
            nc.gpsimd.memset(T.v_parts[:, :, :, VW - 1:VW], 1.0).then_inc(ones_ready, 1)
            pool.wait_ge(ones_ready, 1)
            for n in range(len(units) + 2):
                m = n - 2
                if n < len(units):
                    pool.wait_ge(turned_by, n + 1)
                    nc.gpsimd.tensor_tensor(q[n % NB][:, :], q[n % NB][:, :], rs[n % 2][:, :], ALU.add).then_inc(q_ready, 1)
                    pool.wait_ge(q_ready, n + 1)
                if m >= 0:
                    rows = hi if is_query(m) else lo
                    pool.wait_ge(p2_ready, m + 1)
                    pool.wait_ge(second_placed, m + 1)
                    nc.gpsimd.tensor_tensor(stacks(m)[1][rows, cols(m)], r1[m % NB][rows, :], p2[m % NB][rows, :],
                                            ALU.subtract).then_inc(third_placed, 1)
                    pool.wait_ge(third_placed, m + 1)


def row_maxima(nc, T):
    with Phase(nc, "maxima") as ph:
        sc = [ph.ps(f"sc{i}", [P, 2, G]) for i in range(3)]
        flat = ph.ps("flat", [2, NHEAD, G], BF16)
        part = ph.sb("part", [P, 2, NHEAD, NG // 2])
        neg = ph.sb("neg", [P, 2, NHEAD])
        halves = [ph.sb(f"halves{i}", [P, TPG, NHEAD, 2], BF16) for i in range(2)]
        scored, reduced, neg_ready = ph.sem("scored"), ph.sem("reduced"), ph.sem("neg_ready")
        high_ready, halves_ready = ph.sem("high_ready"), ph.sem("halves_ready")
        flat_ready, placed, split = ph.sem("flat_ready"), ph.sem("placed"), ph.sem("split")
        block = ph.block()

        def pairs(g):
            return g // 2 + 1

        def before(g):
            return sum(TPG * NHEAD * pairs(k) for k in range(g))

        def unread(g, u):
            return min((2 * NHEAD * pairs(k) - 1 - u) % 3 for k in (max(g - 1, 0), g))

        @block.tensor
        def _(pe):
            lead(pe, scored)

            def flatten(g):
                pe.wait_ge(halves_ready, TPG * (g + 1))
                if g >= 1:
                    pe.wait_ge(placed, g)
                for h in range(NHEAD):
                    for k in range(TPG):
                        last = nc.tensor.transpose(flat[:, h, k * P:(k + 1) * P], halves[g % 2][:, k, h, :],
                                                   T.ident16[:, :])
                last.then_inc(flat_ready, 1)

            for g in range(NG):
                with pe.Fori(0, 2) as two:
                    for half in range(2):
                        for h in range(NHEAD):
                            for c in range(pairs(g)):
                                u = (half * NHEAD + h) * pairs(g) + c
                                at = before(g) + two * (2 * NHEAD * pairs(g)) + u
                                q = (g * TPG + two * 2 + half) * P
                                pe.wait_ge(reduced, LEAD + at - (u + unread(g, u) if u < 3 else 2))
                                for k in range(min(2, g + 1 - 2 * c)):
                                    s = 2 * c + k
                                    o = sc[u % 3][:, k, :]
                                    keys = slice(s * G, (s + 1) * G)
                                    nc.tensor.matmul(o, T.qa[h][:, bass.ds(q, P)], T.ka[h // 2][:, keys],
                                                     start=True, stop=False)
                                    last = nc.tensor.matmul(o, T.qb[h][0:2 * HD, bass.ds(q, P)],
                                                            T.kb[h // 2][0:2 * HD, keys], start=False, stop=(s != g))
                                    if s == g:
                                        last = nc.tensor.matmul(o, T.ident16[:, :],
                                                                T.future_keys[:, bass.ds(two * 2 + half, 1), :]
                                                                .rearrange("p a s -> p (a s)"),
                                                                start=False, stop=True)
                                last.then_inc(scored, 1)
                if g >= 1:
                    flatten(g - 1)
            flatten(NG - 1)

        @block.vector
        def _(dve):
            lead(dve, reduced)
            for g in range(NG):
                with dve.Fori(0, 2) as two:
                    for half in range(2):
                        for h in range(NHEAD):
                            for c in range(pairs(g)):
                                u = (half * NHEAD + h) * pairs(g) + c
                                at = before(g) + two * (2 * NHEAD * pairs(g)) + u
                                w = min(2, g + 1 - 2 * c)
                                dve.wait_ge(scored, LEAD + at + 1)
                                nc.vector.reduce_max(part[:, half, h, c:c + 1],
                                                     sc[u % 3][:, 0:w, :].rearrange("p a s -> p (a s)"),
                                                     AX.X).then_inc(reduced, 1)
                        done = before(g) + (two * 2 + half + 1) * (NHEAD * pairs(g))
                        tile = two * 2 + half
                        dve.wait_ge(reduced, LEAD + done)
                        nc.vector.tensor_reduce(neg[:, half, :], part[:, half, :, 0:pairs(g)], AX.X, ALU.max,
                                                negate=True).then_inc(neg_ready, 1)
                        dve.wait_ge(neg_ready, g * TPG + tile + 1)
                        if g >= 2:
                            dve.wait_ge(flat_ready, g - 1)
                        nc.vector.tensor_copy(halves[g % 2][:, bass.ds(tile, 1), :, 0].rearrange("p a h -> p (a h)"),
                                              neg[:, half, :]).then_inc(high_ready, 1)
                        dve.wait_ge(high_ready, g * TPG + tile + 1)
                        nc.vector.tensor_tensor(halves[g % 2][:, bass.ds(tile, 1), :, 1].rearrange("p a h -> p (a h)"),
                                                neg[:, half, :],
                                                halves[g % 2][:, bass.ds(tile, 1), :, 0].rearrange("p a h -> p (a h)"),
                                                ALU.subtract).then_inc(halves_ready, 1)

        @block.gpsimd
        def _(pool):
            def part(i):
                return T.v_parts[:, :, :, i * HD:(i + 1) * HD]

            s = Steps(pool, split)
            s.done(nc.gpsimd.tensor_copy(part(0), T.v[:, :, :, :]))
            s.done(nc.gpsimd.tensor_tensor(T.v[:, :, :, :], T.v[:, :, :, :], part(0), ALU.subtract))
            s.done(nc.gpsimd.tensor_copy(part(1), T.v[:, :, :, :]))
            s.done(nc.gpsimd.tensor_tensor(part(2), T.v[:, :, :, :], part(1), ALU.subtract))

        @block.scalar
        def _(act):
            for g in range(NG):
                act.wait_ge(flat_ready, g + 1)
                for h in range(NHEAD):
                    last = nc.scalar.copy(T.qb[h][2 * HD:2 * HD + 2, g * G:(g + 1) * G], flat[:, h, :])
                last.then_inc(placed, 1)


def attend(nc, T):
    PROB_SHIFT = 8.0
    with Phase(nc, "attend") as ph:
        sc = [ph.ps(f"sc{i}", [P, 2, G]) for i in range(2)]
        heads = [ph.ps(f"heads{h}", [VW, G]) for h in range(NHEAD)]
        exp32 = [T.xn_t[:, i * 2 * G:(i + 1) * 2 * G].rearrange("p (k q) -> p k q", k=2) for i in range(4)]
        high = [ph.sb(f"high{i}", [P, 2, G], F16) for i in range(2)]
        low = [ph.sb(f"low{i}", [P, 2, G], F16) for i in range(2)]
        ot = ph.sb("ot", [VW, NHEAD, G])
        wo = ph.sb("wo", [VW, NHEAD, P + 1])
        inv = ph.sb("inv", [P, 2, NHEAD])
        shift = ph.sb("shift", [P, 1])
        loaded, wo_zeroed, wo_one = ph.sem("loaded"), ph.sem("wo_zeroed"), ph.sem("wo_one")
        scored, exps_ready, multiplied = ph.sem("scored"), ph.sem("exps_ready"), ph.sem("multiplied")
        high_ready, low_ready, shift_ready = ph.sem("high_ready"), ph.sem("low_ready"), ph.sem("shift_ready")
        heads_out, projected = ph.sem("heads_out"), ph.sem("projected")
        inv_ready, head_added, added = ph.sem("inv_ready"), ph.sem("head_added"), ph.sem("added")
        block = ph.block()
        UP = 2 * NHEAD

        def before(g):
            return sum(UP * (k + 1) for k in range(g))

        def queries(u, diag):
            return slice(2 * P if diag and u >= NHEAD else 0, G)

        @block.sync
        def _(sp):
            sp.wait_ge(wo_zeroed, 1)
            for part in range(3):
                sp.dma_start(wo[part * HD:(part + 1) * HD, :, 0:P],
                             T.D["wo"].rearrange("(h d) o -> d h o", d=HD)).then_inc(loaded, 16)

        @block.tensor
        def _(pe):
            lead(pe, multiplied, scored)
            pe.wait_ge(loaded, 3 * 16)
            pe.wait_ge(wo_one, 1)

            def score(g, at, u, tile, diag):
                pr, h = divmod(u, NHEAD)
                c = queries(u, diag)
                pe.wait_ge(exps_ready, LEAD + at - 1)
                for k in range(2):
                    o = sc[u % 2][:, k, c]
                    st = (tile + 2 * pr + k) * P
                    keys = bass.ds(st, P)
                    qs = slice(g * G + c.start, (g + 1) * G)
                    nc.tensor.matmul(o, T.ka[h // 2][:, keys], T.qa[h][:, qs], start=True, stop=False)
                    last = nc.tensor.matmul(o, T.kb[h // 2][0:2 * HD + 2, keys], T.qb[h][0:2 * HD + 2, qs],
                                            start=False, stop=not diag)
                    if diag:
                        last = nc.tensor.matmul(o, T.ident16[:, :], T.past_queries[:, 2 * pr + k, c],
                                                start=False, stop=True)
                last.then_inc(scored, 1)

            def multiply(g, at, u, tile, diag, first=False):
                pr, h = divmod(u, NHEAD)
                c = queries(u, diag)
                pe.wait_ge(low_ready, LEAD + at + 1)
                for k in range(2):
                    values = T.v_parts[:, bass.ds(tile + 2 * pr + k, 1), h // 2, :].rearrange("p a m -> p (a m)")
                    for part in (high, low):
                        last = nc.tensor.matmul(heads[h][:, c], values, part[u % 2][:, k, c],
                                                start=(first and pr == 0 and k == 0 and part is high),
                                                stop=True, skip_group_check=True)
                last.then_inc(multiplied, 1)

            def project(g, k):
                for h in range(NHEAD):
                    o = sc[k % 2][:, h // 2, (h % 2) * (P + 1):(h % 2 + 1) * (P + 1)]
                    last = nc.tensor.matmul(o, ot[:, h, k * P:(k + 1) * P], wo[:, h, :], start=True, stop=True)
                last.then_inc(projected, 1)

            def two_pairs(g, it, diag=False, first=False):
                at0 = before(g) + it * UP
                for u in range(UP):
                    if first and g >= 1 and u in (2, 4):
                        pe.wait_ge(heads_out, 2 * g)
                        for k in (u - 2, u - 1):
                            pe.wait_ge(exps_ready, LEAD + at0 + k + 1)
                            project(g - 1, k)
                    if first and g >= 1 and 2 <= u < 2 + TPG:
                        pe.wait_ge(added, TPG * (g - 1) + u - 1)
                    score(g, at0 + u, u, it * TPG, diag)
                    v = u - SKEW
                    if v >= 0:
                        multiply(g, at0 + v, v, it * TPG, diag, first)
                    elif not first:
                        multiply(g, at0 + v, v + UP, it * TPG - TPG, False)

            for g in range(NG):
                if g >= 1:
                    two_pairs(g, 0, first=True)
                if g >= 2:
                    with pe.Fori(1, g) as it:
                        two_pairs(g, it)
                two_pairs(g, g, diag=True, first=(g == 0))
                for v in range(UP - SKEW, UP):
                    multiply(g, before(g) + g * UP + v, v, g * TPG, True)
            pe.wait_ge(heads_out, 2 * NG)
            for k in range(TPG):
                if k >= 2:
                    pe.wait_ge(added, TPG * (NG - 1) + k - 1)
                project(NG - 1, k)

        @block.scalar
        def _(act):
            lead(act, exps_ready)
            act.wait_ge(shift_ready, 1)

            def exps(at0, diag):
                for u in range(UP):
                    at = at0 + u
                    c = queries(u, diag)
                    act.wait_ge(scored, LEAD + at + 1)
                    act.wait_ge(low_ready, LEAD + at - 3)
                    exp = nc.scalar.activation(exp32[u % 4][:, :, c], sc[u % 2][:, :, c], ACT.Exp,
                                               bias=shift[:, :], scale=float(1.0 / np.sqrt(np.float32(HD))))
                    if u % 2:
                        act.wait_ge(multiplied, LEAD + at - 1)
                        exp = nc.scalar.activation(high[u % 2][:, :, c], sc[u % 2][:, :, c], ACT.Exp,
                                                   bias=shift[:, :], scale=float(1.0 / np.sqrt(np.float32(HD))))
                    exp.then_inc(exps_ready, 1)

            for g in range(NG):
                if g >= 1:
                    with act.Fori(0, g) as it:
                        exps(before(g) + it * UP, False)
                exps(before(g) + g * UP, True)
                act.wait_ge(multiplied, LEAD + before(g + 1))
                if g >= 1:
                    act.wait_ge(projected, TPG * g)
                for h in range(2):
                    last = nc.scalar.copy(ot[:, h, :], heads[h][:, :])
                last.then_inc(heads_out, 1)

        @block.gpsimd
        def _(pool):
            nc.gpsimd.memset(shift[:, :], PROB_SHIFT).then_inc(shift_ready, 1)
            nc.gpsimd.memset(wo[:, :, :], 0.0).then_inc(wo_zeroed, 1)
            pool.wait_ge(wo_zeroed, 1)
            nc.gpsimd.memset(wo[VW - 1:VW, :, P:P + 1], 1.0).then_inc(wo_one, 1)

        @block.vector
        def _(dve):
            lead(dve, high_ready, low_ready)

            def add_tile(g, k):
                t = TPG * g + k
                dve.wait_ge(projected, t + 1)
                s2 = sc[k % 2][:, :, 0:2 * (P + 1)].rearrange("p a (b c) -> p a b c", b=2)
                if t >= 2:
                    dve.wait_ge(added, t - 1)
                nc.vector.reciprocal(inv[:, k % 2, :].rearrange("p (a b) -> p a b", a=2),
                                     s2[:, :, :, P]).then_inc(inv_ready, 1)
                dve.wait_ge(inv_ready, t + 1)
                for h in range(NHEAD):
                    ins = nc.vector.scalar_tensor_tensor(out=T.xn[:, t, :], in0=s2[:, h // 2, h % 2, 0:P],
                                                         scalar=inv[:, k % 2, h:h + 1], in1=T.xn[:, t, :],
                                                         op0=ALU.mult, op1=ALU.add)
                    if h < NHEAD - 1:
                        ins.then_inc(head_added, 1)
                        dve.wait_ge(head_added, (NHEAD - 1) * t + h + 1)
                ins.then_inc(added, 1)

            def split(at0, highs, diag, projection=None):
                for u in range(UP):
                    if projection is not None and u in (2, 4):
                        for k in (u - 2, u - 1):
                            add_tile(projection, k)
                    at = at0 + u
                    c = queries(u, diag)
                    dve.wait_ge(exps_ready, LEAD + at + 1)
                    dve.wait_ge(multiplied, LEAD + at - 1)
                    if u % 2 == 0:
                        nc.vector.tensor_copy(high[0][:, :, c], exp32[u % 4][:, :, c]).then_inc(high_ready, 1)
                        dve.wait_ge(high_ready, LEAD + highs + u // 2 + 1)
                    nc.vector.tensor_tensor(low[u % 2][:, :, c], exp32[u % 4][:, :, c], high[u % 2][:, :, c],
                                            ALU.subtract).then_inc(low_ready, 1)

            for g in range(NG):
                if g >= 1:
                    split(before(g), before(g) // 2, False, g - 1)
                if g >= 2:
                    with dve.Fori(1, g) as it:
                        split(before(g) + it * UP, before(g) // 2 + it * (UP // 2), False)
                split(before(g) + g * UP, (before(g) + g * UP) // 2, True)
                dve.wait_ge(multiplied, LEAD + before(g + 1))
                if g >= 1:
                    dve.wait_ge(projected, TPG * g)
                for h in range(2, NHEAD):
                    last = nc.vector.tensor_copy(ot[:, h, :], heads[h][:, :])
                last.then_inc(heads_out, 1)
            for k in range(TPG):
                add_tile(NG - 1, k)


def route(nc, T):
    with Phase(nc, "route") as ph:
        rw = ph.sb("rw", [P, NE])
        e = ph.sb("e", [P, NT, NE])
        neg = ph.sb("neg", [P, NT])
        logits = ph.sb("logits", [P, NT, NE])
        top = ph.sb("top", [P, NT, 8])
        idx = ph.sb("idx", [P, NT, 8], mybir.dt.uint32)
        best = ph.sb("best", [P, 2, NT])
        number = ph.sb("number", [P, NE])
        s1 = ph.sb("s1", [P, NT])
        hot = ph.sb("hot", [P, 2, NT, NE])
        high16 = ph.sb("high16", [P, NT, NE], F16)
        parts = ph.sb("parts", [P, NT, 2, NE])
        lp = ph.ps("lp", [P, NT, NE])
        back = [ph.ps(f"back{i}", [2 * NE, G]) for i in range(2)]
        loaded, multiplied, less_max_ready, exps_ready = (ph.sem(n) for n in ("loaded", "multiplied", "less_max_ready", "exps_ready"))
        route_zeroed, w1_loaded, w3_loaded, w2_loaded = (ph.sem(n) for n in ("route_zeroed", "w1_loaded", "w3_loaded", "w2_loaded"))
        weights_ready, transposed, copied, chain = (ph.sem(n) for n in ("weights_ready", "transposed", "copied", "chain"))
        block = ph.block()

        @block.sync
        def _(sp):
            sp.dma_start(rw[:, :], T.D["router_w"]).then_inc(loaded, 16)
            sp.dma_start(T.w1[:, :, :], T.D["w1"].rearrange("e c h -> c e h")).then_inc(w1_loaded, 16)
            sp.dma_start(T.w3[:, :, :], T.D["w3"].rearrange("e c h -> c e h")).then_inc(w3_loaded, 16)
            for c, (h0, hn) in enumerate(HCH):
                sp.dma_start(T.w2[0:hn, :, c, :],
                             T.D["w2"][:, h0:h0 + hn, :].rearrange("e h c -> h e c")).then_inc(w2_loaded, 16)
            sp.wait_ge(w2_loaded, 16 * len(HCH))

        @block.tensor
        def _(pe):
            pe.wait_ge(loaded, 16)
            for t in range(NT):
                last = nc.tensor.matmul(lp[:, t, :], T.xn_t[:, t * P:(t + 1) * P], rw[:, :], start=True, stop=True)
            last.then_inc(multiplied, 1)
            pe.wait_ge(weights_ready, 1)
            for g in range(NG):
                if g >= 2:
                    pe.wait_ge(copied, g - 1)
                for k in range(TPG):
                    last = nc.tensor.transpose(back[g % 2][:, k * P:(k + 1) * P],
                                               parts[:, TPG * g + k, :, :].rearrange("p a n -> p (a n)"),
                                               T.ident[:, :])
                last.then_inc(transposed, 1)

        @block.scalar
        def _(act):
            act.wait_ge(less_max_ready, 1)
            nc.scalar.activation(e[:, :, :], logits[:, :, :], ACT.Exp).then_inc(exps_ready, 1)
            for g in range(NG):
                act.wait_ge(transposed, g + 1)
                act.wait_ge(route_zeroed, 1)
                nc.scalar.copy(T.route_t[0:2 * NE, g * G:(g + 1) * G], back[g % 2][:, :]).then_inc(copied, 1)

        @block.vector
        def _(dve):
            s = Steps(dve, chain)
            nc.vector.memset(T.route_t[:, :], 0.0).then_inc(route_zeroed, 1)
            wide = lambda ap: ap.rearrange("p (t o) -> p t o", o=1).broadcast_to([P, NT, NE])
            for n in range(NE):
                s.mark(nc.vector.memset(number[:, n:n + 1], float(n)))
            s.mark(nc.vector.tensor_reduce(T.largest[:, 0:1], T.xn_t[:, 0:N], AX.X, ALU.max,
                                           apply_absolute_value=True))
            for j, (w, w_loaded) in enumerate(((T.w1, w1_loaded), (T.w3, w3_loaded))):
                dve.wait_ge(w_loaded, 16)
                s.mark(nc.vector.tensor_reduce(T.largest[:, 1 + j:2 + j], w[:, :, :], AX.XY, ALU.max,
                                               apply_absolute_value=True))
            dve.wait_ge(multiplied, 1)
            s.done(nc.vector.tensor_copy(logits[:, :, :], lp[:, :, :]))
            s.done(nc.vector.tensor_reduce(neg[:, :], logits[:, :, :], AX.X, ALU.max, negate=True))
            nc.vector.tensor_tensor(logits[:, :, :], logits[:, :, :], wide(neg[:, :]), ALU.add).then_inc(less_max_ready, 1)
            dve.wait_ge(exps_ready, 1)
            s.done(nc.vector.tensor_reduce(s1[:, :], e[:, :, :], AX.X, ALU.add))
            s.done(nc.vector.reciprocal(s1[:, :], s1[:, :]))
            s.done(nc.vector.tensor_tensor(e[:, :, :], e[:, :, :], wide(s1[:, :]), ALU.mult))
            for t in range(NT):
                s.mark(nc.vector.max(top[:, t, :], e[:, t, :]))
            s.sync()
            for t in range(NT):
                s.mark(nc.vector.max_index(idx[:, t, :], top[:, t, :], e[:, t, :]))
            s.mark(nc.vector.tensor_tensor(s1[:, :], top[:, :, 0], top[:, :, 1], ALU.add))
            s.sync()
            s.done(nc.vector.tensor_scalar(s1[:, :], s1[:, :], 1e-9, None, ALU.add))
            s.done(nc.vector.reciprocal(s1[:, :], s1[:, :]))
            for j in range(2):
                s.mark(nc.vector.tensor_copy(best[:, j, :], idx[:, :, j]))
            s.mark(nc.vector.tensor_tensor(top[:, :, 0:2], top[:, :, 0:2],
                                           s1[:, :].rearrange("p (t o) -> p t o", o=1).broadcast_to([P, NT, 2]),
                                           ALU.mult))
            s.sync()
            for j in range(2):
                s.done(nc.vector.tensor_tensor(hot[:, j, :, :],
                                               number[:, :].rearrange("p (o n) -> p o n", o=1).broadcast_to([P, NT, NE]),
                                               wide(best[:, j, :]), ALU.is_equal))
                s.done(nc.vector.tensor_tensor(hot[:, j, :, :], hot[:, j, :, :],
                                               top[:, :, j:j + 1].broadcast_to([P, NT, NE]), ALU.mult))
            s.done(nc.vector.tensor_tensor(hot[:, 0, :, :], hot[:, 0, :, :], hot[:, 1, :, :], ALU.add))
            s.done(nc.vector.tensor_scalar(high16[:, :, :], hot[:, 0, :, :], ROUTE_SCALE, None, ALU.mult))
            s.mark(nc.vector.tensor_copy(parts[:, :, 0, :], high16[:, :, :]))
            nc.vector.scalar_tensor_tensor(out=parts[:, :, 1, :], in0=hot[:, 0, :, :], scalar=ROUTE_SCALE,
                                           in1=high16[:, :, :], op0=ALU.mult, op1=ALU.subtract).then_inc(weights_ready, 1)


def experts(nc, T, out):
    NC = len(HCH)
    FIRST_AND_OTHERS = (slice(0, 1), slice(1, NE))
    with Phase(nc, "experts") as ph:
        w13 = ph.sb("w13", [P, 2, 2, NE, HID], F16)
        f = [ph.sb(f"f{i}", [P, 2, G], F16) for i in range(2)]
        sel = ph.sb("sel", [P, NE, P], F16)
        top = ph.sb("top", [P, 3])
        scale = ph.sb("scale", [P, 2])
        unscale = ph.sb("unscale", [P, 3])
        zero = ph.sb("zero", [P, G])
        up = [[ph.ps(f"up{i}{j}", [P, G]) for j in range(2)] for i in range(2)]
        down = [ph.ps(f"down{i}", [P, G]) for i in range(2)]
        spread = ph.ps("spread", [P, G])
        back = ph.ps("back", [P, TPG, P])
        act_out = [ph.sb(f"silu{i}", [P, G]) for i in range(2)]
        hidden = [ph.sb(f"hidden{i}", [P, G]) for i in range(2 * NC)]
        weight = [ph.sb(f"weight{i}", [P, G]) for i in range(2)]
        scaled = [ph.sb(f"scaled{i}", [P, G]) for i in range(2)]
        total = [ph.sb(f"total{i}", [P, G]) for i in range(2)]
        sel_ready, chain, top_ready, scale_ready = (ph.sem(n) for n in ("sel_ready", "chain", "top_ready", "scale_ready"))
        w_high, w_low, f_high, f_low = (ph.sem(n) for n in ("w_high", "w_low", "f_high", "f_low"))
        upped, silu_ready, hidden_ready = ph.sem("upped"), ph.sem("silu_ready"), ph.sem("hidden_ready")
        downed, spread_ready, weight_ready = ph.sem("downed"), ph.sem("spread_ready"), ph.sem("weight_ready")
        scaled_ready, total_ready, back_ready, added = (ph.sem(n) for n in ("scaled_ready", "total_ready", "back_ready", "added"))
        stored, summed, zeroed = ph.sem("stored"), ph.sem("summed"), ph.sem("zeroed")
        block = ph.block()

        @block.sync
        def _(sp):
            with sp.Fori(0, NG) as g:
                sp.wait_ge(added, LEAD + g + 1)
                sp.dma_start(out[bass.ds(g * G, G), :].rearrange("(t p) c -> p t c", p=P),
                             T.x[:, bass.ds(g * TPG, TPG), :]).then_inc(stored, 16)
            sp.wait_ge(stored, 16 * NG)

        @block.tensor
        def _(pe):
            lead(pe, upped, downed, back_ready)
            pe.wait_ge(w_low, 2)
            pe.wait_ge(sel_ready, 3)

            def ups(g, b, e):
                pe.wait_ge(weight_ready, LEAD + g * NE + e)
                nc.tensor.matmul(spread[:, :], sel[:, e, :], T.route_t[:, bass.ds(g * G, G)],
                                 start=True, stop=True).then_inc(spread_ready, 1)
                if e == 0:
                    pe.wait_ge(f_low, LEAD + g + 1)
                if e == 1:
                    pe.wait_ge(w_low, 4)
                for c, (h0, hn) in enumerate(HCH):
                    u = NC * e + c
                    pe.wait_ge(hidden_ready, LEAD + g * (NE * NC) + u - 1)
                    for j in range(2):
                        for n, (wp, fp) in enumerate(((0, 0), (0, 1), (1, 0))):
                            last = nc.tensor.matmul(up[u % 2][j][0:hn, :], w13[:, j, wp, e, h0:h0 + hn],
                                                    f[b][:, fp, :], start=(n == 0), stop=(n == 2))
                    last.then_inc(upped, 1)

            def downs(g, e):
                pe.wait_ge(scaled_ready, LEAD + g * NE + e - 1)
                for c, (h0, hn) in enumerate(HCH):
                    pe.wait_ge(hidden_ready, LEAD + g * (NE * NC) + NC * e + c + 1)
                    last = nc.tensor.matmul(down[e % 2][:, :], T.w2[0:hn, e, c, :], hidden[(e % 2) * NC + c][0:hn, :],
                                            start=(c == 0), stop=(c == NC - 1))
                last.then_inc(downed, 1)

            def turn_back(g):
                pe.wait_ge(total_ready, LEAD + (g + 1) * NE)
                pe.wait_ge(added, LEAD + g)
                for k in range(TPG):
                    last = nc.tensor.transpose(back[:, k, :], total[(NE - 1) % 2][:, k * P:(k + 1) * P],
                                               T.ident[:, :])
                last.then_inc(back_ready, 1)

            with pe.Fori(0, NG // 2) as gg:
                for b in range(2):
                    g = gg * 2 + b
                    for e in range(NE):
                        ups(g, b, e)
                        if b == 1 and e == 0:
                            turn_back(g - 1)
                        if e >= 1:
                            downs(g, e - 1)
                    downs(g, NE - 1)
                turn_back(gg * 2 + 1)

        @block.scalar
        def _(act):
            lead(act, weight_ready, silu_ready, f_high)

            def high_of_f(g, b):
                nc.scalar.activation(f[b][:, 0, :], T.xn_t[:, bass.ds(g * G, G)], ACT.Copy,
                                     scale=scale[:, 0:1]).then_inc(f_high, 1)

            act.wait_ge(scale_ready, 1)
            high_of_f(0, 0)
            for which in FIRST_AND_OTHERS:
                for j, w in enumerate((T.w1, T.w3)):
                    nc.scalar.activation(w13[:, j, 0, which, :], w[:, which, :], ACT.Copy,
                                         scale=scale[:, 1:2]).then_inc(w_high, 1)
            with act.Fori(0, NG // 2) as gg:
                for b in range(2):
                    g = gg * 2 + b
                    for e in range(NE):
                        if e == 2:
                            act.wait_ge(upped, LEAD + g * (NE * NC))
                            high_of_f(g + 1, 1 - b)
                        act.wait_ge(spread_ready, g * NE + e + 1)
                        act.wait_ge(scaled_ready, LEAD + g * NE + e - 1)
                        nc.scalar.copy(weight[e % 2][:, :], spread[:, :]).then_inc(weight_ready, 1)
                        for c, (h0, hn) in enumerate(HCH):
                            u = NC * e + c
                            act.wait_ge(upped, LEAD + g * (NE * NC) + u + 1)
                            act.wait_ge(hidden_ready, LEAD + g * (NE * NC) + u - 1)
                            nc.scalar.activation(act_out[u % 2][0:hn, :], up[u % 2][0][0:hn, :],
                                                 ACT.Silu, scale=unscale[0:hn, 2:3]).then_inc(silu_ready, 1)

        @block.vector
        def _(dve):
            lead(dve, hidden_ready, scaled_ready, added, f_low)
            s = Steps(dve, chain)
            nc.vector.memset(zero[:, :], 0.0).then_inc(zeroed, 1)
            nc.vector.memset(T.xn_t[:, N:N + G], 0.0)
            dve.wait_ge(top_ready, 1)
            s.done(nc.vector.tensor_tensor(top[:, 1:2], top[:, 1:2], top[:, 2:3], ALU.max))
            s.done(nc.vector.tensor_scalar(unscale[:, 0:2].bitcast(I32), top[:, 0:2].bitcast(I32), 0x7F800000, None,
                                           ALU.bitwise_and))
            s.done(nc.vector.tensor_scalar(unscale[:, 0:2], unscale[:, 0:2], 2.0 ** -20, 2.0 ** -13, ALU.max, ALU.mult))
            s.mark(nc.vector.tensor_tensor(unscale[:, 2:3], unscale[:, 0:1], unscale[:, 1:2], ALU.mult))
            s.mark(nc.vector.reciprocal(scale[:, :], unscale[:, 0:2]))
            s.sync()
            nc.vector.tensor_scalar(top[:, 0:1], top[:, 0:1], 1.0, None, ALU.mult).then_inc(scale_ready, 1)

            def low_of_f(g, b):
                dve.wait_ge(f_high, LEAD + g + 1)
                nc.vector.scalar_tensor_tensor(out=f[b][:, 1, :], in0=T.xn_t[:, bass.ds(g * G, G)], scalar=scale[:, 0:1],
                                               in1=f[b][:, 0, :], op0=ALU.mult, op1=ALU.subtract).then_inc(f_low, 1)

            def add_group(g):
                o = T.x[:, bass.ds(g * TPG, TPG), :].rearrange("p t c -> p (t c)")
                n = T.xn[:, bass.ds(g * TPG, TPG), :].rearrange("p t c -> p (t c)")
                nc.vector.tensor_tensor(o, o, n, ALU.add).then_inc(summed, 1)
                dve.wait_ge(summed, g + 1)
                dve.wait_ge(back_ready, LEAD + g + 1)
                nc.vector.tensor_tensor(o, o, back[:, :, :].rearrange("p t c -> p (t c)"), ALU.add).then_inc(added, 1)

            low_of_f(0, 0)
            for n, which in enumerate(FIRST_AND_OTHERS):
                for j, w in enumerate((T.w1, T.w3)):
                    dve.wait_ge(w_high, 2 * n + j + 1)
                    nc.vector.scalar_tensor_tensor(out=w13[:, j, 1, which, :], in0=w[:, which, :], scalar=scale[:, 1:2],
                                                   in1=w13[:, j, 0, which, :], op0=ALU.mult,
                                                   op1=ALU.subtract).then_inc(w_low, 1)
            with dve.Fori(0, NG // 2) as gg:
                for b in range(2):
                    g = gg * 2 + b

                    def scale_expert(e):
                        dve.wait_ge(downed, LEAD + g * NE + e + 1)
                        dve.wait_ge(weight_ready, LEAD + g * NE + e + 1)
                        dve.wait_ge(total_ready, LEAD + g * NE + e - 1)
                        nc.vector.tensor_tensor(scaled[e % 2][:, :], down[e % 2][:, :], weight[e % 2][:, :],
                                                ALU.mult).then_inc(scaled_ready, 1)

                    for e in range(NE):
                        if e == 3:
                            low_of_f(g + 1, 1 - b)
                        for c, (h0, hn) in enumerate(HCH):
                            u = NC * e + c
                            dve.wait_ge(silu_ready, LEAD + g * (NE * NC) + u + 1)
                            dve.wait_ge(downed, LEAD + g * NE + e - 1)
                            nc.vector.scalar_tensor_tensor(out=hidden[(e % 2) * NC + c][0:hn, :],
                                                           in0=up[u % 2][1][0:hn, :], scalar=unscale[0:hn, 2:3],
                                                           in1=act_out[u % 2][0:hn, :], op0=ALU.mult,
                                                           op1=ALU.mult).then_inc(hidden_ready, 1)
                        if e >= 1:
                            scale_expert(e - 1)
                        if b == 1 and e == 1:
                            add_group(g - 1)
                    scale_expert(NE - 1)
                add_group(gg * 2 + 1)

        @block.gpsimd
        def _(pool):
            lead(pool, total_ready)
            nc.gpsimd.partition_all_reduce(top[:, :], T.largest[:, :], P, RMAX).then_inc(top_ready, 1)
            pool.wait_ge(top_ready, 1)
            nc.gpsimd.memset(sel[:, :, :], 0.0).then_inc(sel_ready, 1)
            for part in range(2):
                pool.wait_ge(sel_ready, part + 1)
                nc.gpsimd.affine_select(out=sel[:, :, :], in_=sel[:, :, :], compare_op=ALU.not_equal,
                                        fill=1 / ROUTE_SCALE, base=-part * NE, pattern=[[-1, NE], [0, P]],
                                        channel_multiplier=1).then_inc(sel_ready, 1)
            pool.wait_ge(zeroed, 1)
            with pool.Fori(0, NG) as g:
                for e in range(NE):
                    pool.wait_ge(scaled_ready, LEAD + g * NE + e + 1)
                    if e == (NE - 1) % 2:
                        pool.wait_ge(back_ready, LEAD + g)
                    if e == 0:
                        nc.gpsimd.tensor_tensor(total[0][:, :], zero[:, :], scaled[0][:, :],
                                                ALU.add).then_inc(total_ready, 1)
                    else:
                        pool.wait_ge(total_ready, LEAD + g * NE + e)
                        nc.gpsimd.tensor_tensor(total[e % 2][:, :], total[(e - 1) % 2][:, :], scaled[e % 2][:, :],
                                                ALU.add).then_inc(total_ready, 1)


def make_masks(nc, T):
    with Phase(nc, "masks") as ph:
        made = ph.sem("made")
        block = ph.block()

        @block.vector
        def _(dve):
            nc.vector.memset(T.ident16[:, :], 0.0).then_inc(made, 1)
            nc.vector.memset(T.future_keys[:, :, :], 0.0).then_inc(made, 1)
            nc.vector.memset(T.past_queries[:, :, :], 0.0).then_inc(made, 1)

        @block.gpsimd
        def _(pool):
            pool.wait_ge(made, 3)
            nc.gpsimd.affine_select(out=T.ident16[:, :], in_=T.ident16[:, :], compare_op=ALU.not_equal, fill=1.0,
                                    base=0, pattern=[[-1, P]], channel_multiplier=1)
            nc.gpsimd.affine_select(out=T.future_keys[:, :, :], in_=T.future_keys[:, :, :], compare_op=ALU.is_ge,
                                    fill=-1e30, base=0, pattern=[[P, TPG], [-1, G]], channel_multiplier=1)
            nc.gpsimd.affine_select(out=T.past_queries[:, :, :], in_=T.past_queries[:, :, :], compare_op=ALU.is_ge,
                                    fill=-1e30, base=0, pattern=[[-P, TPG], [1, G]], channel_multiplier=-1)


class Tensors:
    pass


def program(nc, D, out):
    T = Tensors()
    Phase.used.clear()
    with ExitStack() as ctx:
        def sb(name, shape, dt=F32):
            return ctx.enter_context(nc.sbuf_tensor(name, shape, dt))

        T.x = sb("x", [P, NT, P])
        T.xn = sb("xn", [P, NT, P])
        T.xn_t = sb("xn_t", [P, N + G])
        T.ident = sb("ident", [P, P])
        T.ones = sb("ones", [P, P])
        T.tiny = sb("tiny", [P, 1])
        T.D = D
        with ExitStack() as first:
            ctx_first = first.enter_context
            T.gnn_w = ctx_first(nc.sbuf_tensor("gnn_w", [P, P], F32))
            T.gnn_b = ctx_first(nc.sbuf_tensor("gnn_b", [P, P], F32))
            T.wih = ctx_first(nc.sbuf_tensor("wih", [P, 4 * P], F32))
            T.whh = ctx_first(nc.sbuf_tensor("whh", [P, 4 * P], F32))
            T.bias_rows = ctx_first(nc.sbuf_tensor("bias_rows", [P, 2, 4 * P], F32))
            T.msg = ctx_first(nc.sbuf_tensor("msg", [P, NT, P], F32))
            load_constants(nc, T, D)
            normalise(nc, "norm0", T, T.x, T.xn, T.xn_t)
            project_rows(nc, "message", T.xn_t, T.gnn_w, T.msg, T.gnn_b)
            graph_product(nc, "gnn0", T, D["adj"], T.msg, T.x, True, groups=1)
            normalise(nc, "norm1", T, T.x, T.xn, T.xn_t, tiles=TPG)
            T.hid_t = ctx_first(nc.sbuf_tensor("hid_t", [P, N], F32))
            lstm(nc, T)
            add_sequence_sums(nc, T)

        with ExitStack() as second:
            def sb2(name, shape, dt=F32):
                return second.enter_context(nc.sbuf_tensor(name, shape, dt))

            T.h = sb2("h", [P, NT, P])
            T.agg_t = sb2("agg_t", [P, N])
            T.deg = sb2("deg", [P, NT])
            T.neigh_w = sb2("neigh_w", [P, P])
            load(nc, "neigh", (T.neigh_w[:, :], D["neigh_w"]))
            normalise(nc, "norm2", T, T.x, T.xn, T.xn_t)
            project_rows(nc, "neigh", T.xn_t, T.neigh_w, T.h)
            graph_product(nc, "gnn1", T, D["adj"], T.h, T.agg_t, False, T.deg)
            combine_neighbours(nc, T)

        clear_semaphores(nc)
        normalise(nc, "norm3", T, T.x, T.xn, None)
        with ExitStack() as third:
            def sb3(name, shape, dt=F32):
                return third.enter_context(nc.sbuf_tensor(name, shape, dt))

            with ExitStack() as fourth:
                T.h1 = fourth.enter_context(nc.sbuf_tensor("h1", [P, NT, P], F32))
                T.ln_w = fourth.enter_context(nc.sbuf_tensor("ln_w", [P, P], F32))
                load(nc, "ln1", (T.ln_w[:, :], D["ln1"].broadcast_to([P, P])))
                normalise(nc, "rms1", T, T.xn, T.h1, T.xn_t, rms_weight=T.ln_w, eps=1e-6)
            T.qa = [sb3(f"qa{h}", [P, N], BF16) for h in range(NHEAD)]
            T.qb = [sb3(f"qb{h}", [P, N], BF16) for h in range(NHEAD)]
            T.ka = [sb3(f"ka{h}", [P, N], BF16) for h in range(NKV)]
            T.kb = [sb3(f"kb{h}", [P, N], BF16) for h in range(NKV)]
            T.v_parts = sb3("v_parts", [P, NT, NKV, VW], BF16)
            T.ident16 = sb3("ident16", [P, P], BF16)
            T.past_queries = sb3("past_queries", [P, TPG, G], BF16)
            with ExitStack() as till_attend:
                T.v = till_attend.enter_context(nc.sbuf_tensor("v", [P, NT, NKV, HD], F32))
                split_heads(nc, T)
                T.future_keys = till_attend.enter_context(nc.sbuf_tensor("future_keys", [P, TPG, G], BF16))
                make_masks(nc, T)
                row_maxima(nc, T)
            attend(nc, T)
        with ExitStack() as fifth:
            T.route_t = fifth.enter_context(nc.sbuf_tensor("route_t", [P, N], F16))
            T.w1, T.w3 = (fifth.enter_context(nc.sbuf_tensor(n, [P, NE, HID], F32)) for n in ("w1", "w3"))
            T.w2 = fifth.enter_context(nc.sbuf_tensor("w2", [P, NE, len(HCH), P], F32))
            T.largest = fifth.enter_context(nc.sbuf_tensor("largest", [P, 3], F32))
            with ExitStack() as sixth:
                T.h2 = sixth.enter_context(nc.sbuf_tensor("h2", [P, NT, P], F32))
                T.ln_w = sixth.enter_context(nc.sbuf_tensor("ln_w2", [P, P], F32))
                load(nc, "ln2", (T.ln_w[:, :], D["ln2"].broadcast_to([P, P])))
                normalise(nc, "rms2", T, T.xn, T.h2, T.xn_t, rms_weight=T.ln_w, eps=1e-6)
            route(nc, T)
            experts(nc, T, out)


def rope_tables():
    inv = 1.0 / 10000.0 ** (np.arange(0, HD, 2, dtype=np.float32) / HD)
    freqs = np.outer(np.arange(N, dtype=np.float32), inv)
    emb = np.concatenate([freqs, freqs], axis=-1)
    cos, sin = np.cos(emb).T, np.sin(emb).T
    sign = np.where(np.arange(HD) < HD // 2, -1.0, 1.0).astype(np.float32)[:, None]
    return np.ascontiguousarray(cos), np.ascontiguousarray(sin * sign)


def layouts(inputs):
    a = {k: np.asarray(v) for k, v in inputs.items()}
    t = lambda w: np.ascontiguousarray(np.swapaxes(w, -1, -2))
    row = lambda w: np.ascontiguousarray(w.reshape(1, -1))
    cos, sin = rope_tables()
    heads = np.concatenate([a["L1_ffn_wq"], a["L1_ffn_wk"]]).reshape(NHEAD + NKV, HD, P)
    swapped = np.concatenate([heads[:, HD // 2:], heads[:, :HD // 2]], axis=1)
    wqk = np.stack([np.tile(heads, (1, 4, 1)), np.tile(swapped, (1, 4, 1))], axis=1)
    return {
        "x": a["x"], "adj": a["adj"], "gnn_w": a["L0_gnn_W"], "gnn_b": row(a["L0_gnn_B"]),
        "wih": t(a["L0_ffn_W_ih"]), "whh": t(a["L0_ffn_W_hh"]),
        "b_ih": row(a["L0_ffn_b_ih"]), "b_hh": row(a["L0_ffn_b_hh"]),
        "neigh_w": t(a["L1_gnn_neigh_W"]), "lin_w": t(a["L1_gnn_lin_W"]),
        "w_lin": t(a["L0_ffn_W_lin"]), "b_lin": row(a["L0_ffn_b_lin"]),
        "fw_att": t(a["L0_ffn_fw_att"]), "bw_att": t(a["L0_ffn_bw_att"]),
        "ln1": row(a["L1_ffn_ln1_w"]), "ln2": row(a["L1_ffn_ln2_w"]),
        "wqk": t(wqk.reshape(-1, P)), "wv": t(a["L1_ffn_wv"]), "wo": t(a["L1_ffn_wo"]),
        "cos": cos, "sin": sin, "router_w": t(a["L1_ffn_router_w"]),
        "w1": t(a["L1_ffn_w1"]), "w2": t(a["L1_ffn_w2"]), "w3": t(a["L1_ffn_w3"]),
    }


def kernel(**inputs):
    import concourse.bacc as bacc
    from concourse.bass_utils import run_bass_kernel_spmd as run

    nc = bacc.Bacc("TRN2", target_bir_lowering=False, num_devices=1)
    arrays = layouts(inputs)
    D = {k: nc.dram_tensor(f"in_{k}", v.shape, mybir.dt.from_np(v.dtype), kind="ExternalInput").ap()
         for k, v in arrays.items()}
    out = nc.dram_tensor("out", [N, P], F32, kind="ExternalOutput").ap()
    program(nc, D, out)
    r = run(nc, [{f"in_{k}": v for k, v in arrays.items()}], core_ids=[0])
    return r.results[0]["out"]
```
